# Optimizing a Trainium2 kernel written in Bass

```python
import numpy as np
import jax
import jax.numpy as jnp

def _softmax(x, axis=-1):
    return jax.nn.softmax(x, axis=axis)

def _gelu(x):
    return jax.nn.gelu(x, approximate=True)

def _silu(x):
    return jax.nn.silu(x)

def _sigmoid(x):
    return jax.nn.sigmoid(x)

def _layernorm(x, axis=-1, eps=1e-05):
    m = jnp.mean(x, axis=axis, keepdims=True)
    v = jnp.var(x, axis=axis, keepdims=True)
    return (x - m) / jnp.sqrt(v + eps)

def _scatter_add(tgt, idx, src, axis=0):
    return tgt.at[idx].add(src)

def _segment_sum(src, seg, n):
    return jax.ops.segment_sum(src, seg, n)
kernel_name = 'mk_decoder_preln_d1_seqx_r2_96012c'

def setup_inputs(seed: int=0):
    np.random.seed(seed)
    _w = jnp.asarray

    def _rec_inputs():
        import jax
        import jax.numpy as jnp
        _rk = jax.random.key(seed)
        x = -0.0003929 + 0.9999 * jax.random.normal(jax.random.fold_in(_rk, 1), (8, 512, 512), jnp.float32)
        _lenS = 512 - jax.random.randint(jax.random.fold_in(_rk, 7), (8,), 0, max(1, 512 // 4) + 1, jnp.int32)
        _lenS2 = 512 - jax.random.randint(jax.random.fold_in(_rk, 8), (8,), 0, max(1, 512 // 4) + 1, jnp.int32)
        _ctx_768P = jax.random.normal(jax.random.fold_in(_rk, 11), (8, 16, 384), jnp.float32)
        _ctx_768c = jax.random.dirichlet(jax.random.fold_in(_rk, 511), 0.3 * jnp.ones((16,), jnp.float32), (8, 512))
        _ctx_768t = jnp.einsum('bsk,bkd->bsd', _ctx_768c, _ctx_768P)
        _ctx_768t = _ctx_768t * jax.lax.rsqrt(jnp.mean(jnp.square(_ctx_768t)) + 1e-12) * 0.953939
        ctx_768 = 0.00095986 + 0.999812 * (_ctx_768t + 0.3 * jax.random.normal(jax.random.fold_in(_rk, 611), (8, 512, 384), jnp.float32))
        _validS = jnp.arange(512)[None, :] < _lenS[:, None]
        _validS2 = jnp.arange(512)[None, :] < _lenS2[:, None]
        _causal = jnp.tril(jnp.ones((512, 512), dtype=bool))
        mask_BxS2_bf1 = jnp.ones((8, 512), dtype=bool)
        return (x, ctx_768, mask_BxS2_bf1)
    x, ctx_768, mask_BxS2_bf1 = _rec_inputs()

    def _L0_attn_setup():
        import jax, jax.numpy as jnp
        import numpy as np
        NUM_HEADS = 16
        HIDDEN = 512
        ATTN_DIM = 64
        HEAD_OUT = 64
        OUT_DIM = 512
        BATCH, SEQ = (2, 1024)

        def _split_heads(y, h):
            b, s, _ = y.shape
            return y.reshape(b, s, h, -1).transpose(0, 2, 1, 3)
        key = jax.random.key(seed)
        ks = jax.random.split(key, 9)
        s_in = 1.0 / np.sqrt(HIDDEN)
        s_o = 1.0 / np.sqrt(NUM_HEADS * HEAD_OUT)
        return {'x': jax.random.normal(ks[0], (BATCH, SEQ, HIDDEN), dtype=jnp.float32), 'Wq': jax.random.uniform(ks[1], (HIDDEN, NUM_HEADS * ATTN_DIM), jnp.float32, -s_in, s_in), 'bq': jax.random.uniform(ks[2], (NUM_HEADS * ATTN_DIM,), jnp.float32, -s_in, s_in), 'Wk': jax.random.uniform(ks[3], (HIDDEN, NUM_HEADS * ATTN_DIM), jnp.float32, -s_in, s_in), 'bk': jax.random.uniform(ks[4], (NUM_HEADS * ATTN_DIM,), jnp.float32, -s_in, s_in), 'Wv': jax.random.uniform(ks[5], (HIDDEN, NUM_HEADS * HEAD_OUT), jnp.float32, -s_in, s_in), 'bv': jax.random.uniform(ks[6], (HIDDEN, NUM_HEADS * HEAD_OUT)[1:], jnp.float32, -s_in, s_in), 'Wo': jax.random.uniform(ks[7], (NUM_HEADS * HEAD_OUT, OUT_DIM), jnp.float32, -s_o, s_o), 'bo': jax.random.uniform(ks[8], (OUT_DIM,), jnp.float32, -s_o, s_o)}
    _L0_attn_all = _L0_attn_setup()
    _L0_attn_in = {k: v for k, v in _L0_attn_all.items() if k in ('Wq', 'bq', 'Wk', 'bk', 'Wv', 'bv', 'Wo', 'bo')}
    del _L0_attn_all

    def _L0_xattn_setup():
        import jax, jax.numpy as jnp
        import numpy as np
        DIM = 512
        CTX_DIM = 384
        HEADS = 16
        key = jax.random.key(seed)
        ks = jax.random.split(key, 7)
        B, N, M = (4, 2048, 128)
        x = jax.random.normal(ks[0], (B, N, DIM), dtype=jnp.float32)
        context = jax.random.normal(ks[1], (B, M, CTX_DIM), dtype=jnp.float32)
        context_mask = jnp.ones((B, M), dtype=bool)
        s_d = 1.0 / np.sqrt(DIM)
        s_c = 1.0 / np.sqrt(CTX_DIM)
        Wq = jax.random.normal(ks[2], (DIM, DIM), dtype=jnp.float32) * s_d
        Wk = jax.random.normal(ks[3], (CTX_DIM, DIM), dtype=jnp.float32) * s_c
        Wv = jax.random.normal(ks[4], (CTX_DIM, DIM), dtype=jnp.float32) * s_c
        Wo = jax.random.normal(ks[5], (DIM, DIM), dtype=jnp.float32) * s_d
        return {'x': x, 'context': context, 'context_mask': context_mask, 'Wq': Wq, 'Wk': Wk, 'Wv': Wv, 'Wo': Wo}
    _L0_xattn_all = _L0_xattn_setup()
    _L0_xattn_in = {k: v for k, v in _L0_xattn_all.items() if k in ('Wq', 'Wk', 'Wv', 'Wo')}
    del _L0_xattn_all

    def _L0_ffn_setup():
        import jax, jax.numpy as jnp
        import numpy as np
        BLOCK = 32
        W_BITS = 4
        ACT_BITS = 16

        def act_qdq(x):
            qmax = 2.0 ** (ACT_BITS - 1) - 1.0
            scale = jnp.maximum(jnp.max(jnp.abs(x)) / qmax, 1e-12)
            return jnp.clip(jnp.round(x / scale), -qmax - 1.0, qmax) * scale

        def fixed_qdq_u16(x):
            scale = 1.0 / 65536.0
            return jnp.clip(jnp.round(x / scale), 0.0, 65535.0) * scale

        def lpbq_dequant(w):
            O, I = w.shape
            qmax = 2.0 ** (W_BITS - 1) - 1.0
            wb = w.reshape(O, I // BLOCK, BLOCK)
            s = jnp.maximum(jnp.max(jnp.abs(wb), axis=-1, keepdims=True) / qmax, 1e-12)
            wq = jnp.clip(jnp.round(wb / s), -qmax - 1.0, qmax) * s
            return wq.reshape(O, I)
        key = jax.random.key(seed)
        k1, k2, k3, k4 = jax.random.split(key, 4)
        B, S, H, I = (2, 2048, 512, 1536)
        x = jax.random.normal(k1, (B, S, H), jnp.float32)
        w_gate = jax.random.normal(k2, (I, H), jnp.float32) * 0.02
        w_up = jax.random.normal(k3, (I, H), jnp.float32) * 0.02
        w_down = jax.random.normal(k4, (H, I), jnp.float32) * 0.02
        return {'x': x, 'w_gate': w_gate, 'w_up': w_up, 'w_down': w_down}
    _L0_ffn_all = _L0_ffn_setup()
    _L0_ffn_in = {k: v for k, v in _L0_ffn_all.items() if k in ('w_gate', 'w_up', 'w_down')}
    del _L0_ffn_all
    return {'x': x, 'ctx_768': ctx_768, 'mask_BxS2_bf1': mask_BxS2_bf1, 'L0_attn_Wq': _L0_attn_in['Wq'], 'L0_attn_bq': _L0_attn_in['bq'], 'L0_attn_Wk': _L0_attn_in['Wk'], 'L0_attn_bk': _L0_attn_in['bk'], 'L0_attn_Wv': _L0_attn_in['Wv'], 'L0_attn_bv': _L0_attn_in['bv'], 'L0_attn_Wo': _L0_attn_in['Wo'], 'L0_attn_bo': _L0_attn_in['bo'], 'L0_xattn_Wq': _L0_xattn_in['Wq'], 'L0_xattn_Wk': _L0_xattn_in['Wk'], 'L0_xattn_Wv': _L0_xattn_in['Wv'], 'L0_xattn_Wo': _L0_xattn_in['Wo'], 'L0_ffn_w_gate': _L0_ffn_in['w_gate'], 'L0_ffn_w_up': _L0_ffn_in['w_up'], 'L0_ffn_w_down': _L0_ffn_in['w_down']}

def reference(x, ctx_768, mask_BxS2_bf1, L0_attn_Wq, L0_attn_bq, L0_attn_Wk, L0_attn_bk, L0_attn_Wv, L0_attn_bv, L0_attn_Wo, L0_attn_bo, L0_xattn_Wq, L0_xattn_Wk, L0_xattn_Wv, L0_xattn_Wo, L0_ffn_w_gate, L0_ffn_w_up, L0_ffn_w_down):
    import jax
    import jax.numpy as jnp

    def _L0_attn_ref(x, Wq, bq, Wk, bk, Wv, bv, Wo, bo):
        import jax, jax.numpy as jnp
        import numpy as np
        NUM_HEADS = 16
        HIDDEN = 512
        ATTN_DIM = 64
        HEAD_OUT = 64
        OUT_DIM = 512
        BATCH, SEQ = (2, 1024)

        def _split_heads(y, h):
            b, s, _ = y.shape
            return y.reshape(b, s, h, -1).transpose(0, 2, 1, 3)
        h = NUM_HEADS
        q = _split_heads(x @ Wq + bq, h)
        k = _split_heads(x @ Wk + bk, h)
        v = _split_heads(x @ Wv + bv, h)
        scale = 1.0 / jnp.sqrt(jnp.float32(ATTN_DIM))
        pattern = jnp.einsum('bhid,bhjd->bhij', k, q) * scale
        prob = jax.nn.softmax(pattern, axis=-2)
        out = jnp.einsum('bhis,bhid->bhsd', prob, v)
        b, _, s, dv = out.shape
        concat = out.transpose(0, 2, 1, 3).reshape(b, s, h * dv)
        return concat @ Wo + bo

    def _L0_xattn_ref(x, context, context_mask, Wq, Wk, Wv, Wo):
        import jax, jax.numpy as jnp
        import numpy as np
        DIM = 512
        CTX_DIM = 384
        HEADS = 16
        B, N, _ = x.shape
        M = context.shape[1]
        hd = DIM // HEADS
        scale = hd ** (-0.5)
        q = (x @ Wq).reshape(B, N, HEADS, hd).transpose(0, 2, 1, 3)
        k = (context @ Wk).reshape(B, M, HEADS, hd).transpose(0, 2, 1, 3)
        v = (context @ Wv).reshape(B, M, HEADS, hd).transpose(0, 2, 1, 3)
        scores = jnp.einsum('bhid,bhjd->bhij', q, k) * scale
        max_neg = -jnp.finfo(scores.dtype).max
        scores = jnp.where(context_mask[:, None, None, :], scores, max_neg)
        attn = jax.nn.softmax(scores, axis=-1)
        out = jnp.einsum('bhij,bhjd->bhid', attn, v)
        out = out.transpose(0, 2, 1, 3).reshape(B, N, DIM)
        return out @ Wo

    def _L0_ffn_ref(x, w_gate, w_up, w_down):
        import jax, jax.numpy as jnp
        import numpy as np
        BLOCK = 32
        W_BITS = 4
        ACT_BITS = 16

        def act_qdq(x):
            qmax = 2.0 ** (ACT_BITS - 1) - 1.0
            scale = jnp.maximum(jnp.max(jnp.abs(x)) / qmax, 1e-12)
            return jnp.clip(jnp.round(x / scale), -qmax - 1.0, qmax) * scale

        def fixed_qdq_u16(x):
            scale = 1.0 / 65536.0
            return jnp.clip(jnp.round(x / scale), 0.0, 65535.0) * scale

        def lpbq_dequant(w):
            O, I = w.shape
            qmax = 2.0 ** (W_BITS - 1) - 1.0
            wb = w.reshape(O, I // BLOCK, BLOCK)
            s = jnp.maximum(jnp.max(jnp.abs(wb), axis=-1, keepdims=True) / qmax, 1e-12)
            wq = jnp.clip(jnp.round(wb / s), -qmax - 1.0, qmax) * s
            return wq.reshape(O, I)
        x = act_qdq(x)
        up = act_qdq(x @ lpbq_dequant(w_up).T)
        gate = act_qdq(x @ lpbq_dequant(w_gate).T)
        sig = fixed_qdq_u16(jax.nn.sigmoid(gate))
        gate = act_qdq(gate * sig)
        o = act_qdq(gate * up)
        return o @ lpbq_dequant(w_down).T
    x = x + _L0_attn_ref(_layernorm(x, axis=-1), L0_attn_Wq, L0_attn_bq, L0_attn_Wk, L0_attn_bk, L0_attn_Wv, L0_attn_bv, L0_attn_Wo, L0_attn_bo)
    x = x + _L0_xattn_ref(_layernorm(x, axis=-1), ctx_768, mask_BxS2_bf1, L0_xattn_Wq, L0_xattn_Wk, L0_xattn_Wv, L0_xattn_Wo)
    x = x + _L0_ffn_ref(_layernorm(x, axis=-1), L0_ffn_w_gate, L0_ffn_w_up, L0_ffn_w_down)
    return x

_drawn_inputs = setup_inputs


def setup_inputs(seed=0):
    import zlib

    import numpy as np

    out = dict(_drawn_inputs(seed))
    spreads = {}
    factors = {'L0_attn_Wq': 8.0,
     'L0_attn_bq': 8.0,
     'L0_attn_Wk': 8.0,
     'L0_attn_bk': 64.0,
     'L0_attn_Wv': 3.863,
     'L0_attn_bv': 3.966,
     'L0_attn_Wo': 2.849,
     'L0_attn_bo': 11.436}
    for name, (base, spread) in spreads.items():
        noise = np.random.default_rng([zlib.crc32(name.encode()), seed]).standard_normal(out[name].shape)
        drawn = base * np.exp(spread * noise) if base else spread * noise
        out[name] = jnp.asarray(drawn.astype(out[name].dtype))
    for name, factor in factors.items():
        out[name] = (out[name] * factor).astype(out[name].dtype)
    return out
```

```python
from contextlib import ExitStack

import concourse.bass as bass
from concourse import mybir

F32 = mybir.dt.float32
F32R = mybir.dt.float32r
I16 = mybir.dt.int16
U16 = mybir.dt.uint16
U8 = mybir.dt.uint8
ALU = mybir.AluOpType
ACT = mybir.ActivationFunctionType
AX_X = mybir.AxisListType.X
AX_XY = mybir.AxisListType.XY
RMAX = bass.bass_isa.ReduceOp.max

P = 128
B, S, D, CD = 8, 512, 512, 384
T = B * S
DK = D // P
CK = CD // P
NT = S // P
NH = 16
HB = B // 2
HTOK = HB * S
HD = 64
HP = NH // 2
XD = D // NH
XG = D // P
FF = 1536
FT = FF // P
CTX_TILES = D // P
BLK = 32
EPS = 1e-5
QMAX = 32767.0
WQMAX = 7.0
ZEROED = 7
BIG = float(2.0 ** 100)


class Space:

    def __init__(self, nc, ctx, tag):
        self.nc, self.ctx, self.tag, self.sems = nc, ctx, tag, []
        ctx.callback(self.clear)

    def sb(self, name, shape, dt=F32):
        return self.ctx.enter_context(self.nc.sbuf_tensor(f"{self.tag}_{name}", shape, dt))

    def ps(self, name, shape, dt=F32):
        return self.ctx.enter_context(self.nc.psum_tensor(f"{self.tag}_{name}", shape, dt))

    def sem(self, name):
        self.sems.append(self.nc.alloc_semaphore(f"{self.tag}_{name}"))
        return self.sems[-1]

    def clear(self):
        self.nc.clear_and_free_semaphores(self.sems)
        self.nc.all_engine_barrier()


def f32(ap):
    return ap.bitcast(F32)


def layernorm_stage(nc, env, half):
    xh, xl, ident, mhalf = env["xt_hi"], env["xt_lo"], env["ident"], env["minus_half"]
    x = env["x"]
    with ExitStack() as ctx:
        sp = Space(nc, ctx, f"ln{half}")
        xt = sp.sb("x", [P, 2, NT, D])
        xn = sp.sb("xn", [P, NT, D])
        stats = sp.sb("stats", [P, NT, 6])
        mv = sp.sb("mv", [P, NT, 2])
        ve = sp.sb("ve", [P, NT])
        rstd = sp.sb("rstd", [P, NT])
        pt = sp.ps("pt", [P, NT, DK, P])
        x_in = [sp.sem(f"x_in{i}") for i in range(2)]
        passed = sp.sem("passed")
        dve_st = sp.sem("dve_st")
        pool_rs = sp.sem("pool_rs")
        dve_xn = sp.sem("dve_xn")
        pe_tr = sp.sem("pe_tr")
        act_hi = sp.sem("act_hi")
        dve_lo = sp.sem("dve_lo")
        xs = x.rearrange("(g n p) d -> g p n d", n=NT, p=P)
        block = ctx.enter_context(nc.Block())

        @block.sync
        def _(e):
            with e.Fori(0, HB // 2) as g2:
                for u in range(2):
                    e.wait_ge(dve_xn, 8 * g2 + 4 * u + 4)
                    e.dma_start(xt[:, u], xs[half * HB + 2 * g2 + u]).then_inc(x_in[u], 16)

        @block.vector
        def _(e):
            e.sem_inc(dve_xn, 8)
            e.sem_inc(dve_lo, 4)
            with e.Fori(0, HB // 2) as g2:
                for u in range(2):
                    g = 2 * g2 + u
                    e.wait_ge(x_in[u], 16 * g2 + 16)
                    for t in range(NT):
                        nc.vector.bn_stats(stats[:, t], xt[:, u, t]).then_inc(dve_st, 1)
                    for t in range(NT):
                        e.wait_ge(dve_st, 9 * g + t + 1)
                        e.sem_inc(passed, 1)
                        nc.vector.bn_aggr(mv[:, t], stats[:, t]).then_inc(dve_st, 1)
                    e.wait_ge(dve_st, 9 * g + 8)
                    nc.vector.tensor_scalar(ve[:, :], mv[:, :, 1], EPS, None, ALU.add).then_inc(dve_st, 1)
                    e.wait_ge(pool_rs, g + 1)
                    for t in range(NT):
                        e.wait_ge(pe_tr, 4 * g + t + 1)
                        nc.vector.tensor_scalar(xn[:, t], xt[:, u, t], mv[:, t, 0:1], rstd[:, t:t + 1],
                                                ALU.subtract, ALU.mult).then_inc(dve_xn, 1)
                    for t in range(NT):
                        e.wait_ge(act_hi, 4 * g + t + 5)
                        at = bass.ds(g * S + t * P, P)
                        nc.vector.tensor_tensor(xl[:, :, at], pt[:, t], f32(xh[:, :, at]),
                                                ALU.subtract).then_inc(dve_lo, 1)

        @block.gpsimd
        def _(e):
            with e.Fori(0, HB) as g:
                e.wait_ge(dve_st, 9 * g + 9)
                nc.gpsimd.tensor_tensor(rstd[:, :], ve[:, :], mhalf[:, 0:NT], ALU.pow).then_inc(pool_rs, 1)

        @block.tensor
        def _(e):
            e.sem_inc(pe_tr, 4)
            with e.Fori(0, HB) as g:
                for t in range(NT):
                    e.wait_ge(dve_xn, 4 * g + t + 9)
                    e.wait_ge(dve_lo, 4 * g + t + 1)
                    for k in range(DK):
                        last = nc.tensor.transpose(pt[:, t, k], xn[:, t, k * P:(k + 1) * P], ident[:, :])
                    last.then_inc(pe_tr, 1)

        @block.scalar
        def _(e):
            e.sem_inc(act_hi, 4)
            with e.Fori(0, HB) as g:
                for t in range(NT):
                    e.wait_ge(pe_tr, 4 * g + t + 5)
                    at = bass.ds(g * S + t * P, P)
                    nc.scalar.activation(xh[:, :, at], pt[:, t], ACT.Copy).then_inc(act_hi, 1)


def self_attention_stage(nc, env, half):
    xh, xl, ident, ident_r = env["xt_hi"], env["xt_lo"], env["ident"], env["ident_r"]
    o_raw, o_sum = env["o_raw"], env["o_sum"]
    weights = [env[n].rearrange("(k p) (m n) -> m p k n", p=P, n=P) for n in ("Wq", "Wk", "Wv")]
    biases = [env[n].rearrange("(m p o) -> m p o", p=P, o=1) for n in ("bq", "bk", "bv")]
    SCALE = HD ** -0.5
    LAG = 2
    own = (slice(0, HD), slice(HD, P))
    other = (slice(HD, P), slice(0, HD))
    mrow = (HD, 0)

    with ExitStack() as ctx:
        sp = Space(nc, ctx, f"sa{half}")
        w_raw = sp.sb("w_raw", [P, 3, DK, P])
        b_raw = sp.sb("b_raw", [P, 4])
        w_hi = sp.sb("w_hi", [P, 3, DK, P], F32R)
        w_lo = sp.sb("w_lo", [P, 3, DK, P], F32R)
        bias = sp.sb("bias", [P, 4])
        qa = sp.sb("qa", [P, 2, 2, S], F32R)
        qb = sp.sb("qb", [P, 2, 2, S], F32R)
        ka = sp.sb("ka", [P, 2, 2, S], F32R)
        kb = sp.sb("kb", [P, 2, 2, S], F32R)
        vt = sp.sb("vt", [P, S])
        va = sp.sb("va", [P, 2, NT, 3, HD], F32R)
        vb = sp.sb("vb", [P, 2, NT, 3, HD], F32R)
        ex = sp.sb("ex", [P, 2, S])
        eh = sp.sb("eh", [P, 4, S], F32R)
        el = sp.sb("el", [P, 4, S], F32R)
        negm = sp.sb("negm", [P, 2, NT, P], F32R)
        osb = sp.sb("osb", [P, 2, S])
        pj = sp.ps("pj", [P, 2, S])
        st = sp.ps("st", [P, 2, S])
        mx = sp.ps("mx", [P, 2, S])
        ov = sp.ps("ov", [P, S])
        mr = sp.ps("mr", [P, S])

        w_in = sp.sem("w_in")
        w_split = sp.sem("w_split")
        act_w = sp.sem("act_w")
        pe_pj = sp.sem("pe_pj")
        act_ev = sp.sem("act_ev")
        dve_ev = sp.sem("dve_ev")
        pool_ev = sp.sem("pool_ev")
        passed = sp.sem("passed")
        zeroed = sp.sem("zeroed")
        pe_mx = sp.sem("pe_mx")
        dve_mx = sp.sem("dve_mx")
        pe_mr = sp.sem("pe_mr")
        act_mr = sp.sem("act_mr")
        pe_st = sp.sem("pe_st")
        act_ex = sp.sem("act_ex")
        act_eh = sp.sem("act_eh")
        dve_el = sp.sem("dve_el")
        pe_av = sp.sem("pe_av")
        act_ov = sp.sem("act_ov")
        o_out = [sp.sem(f"o_out{i}") for i in range(2)]

        block = ctx.enter_context(nc.Block())

        def each_pair(e, step, extra):
            with e.Fori(0, HP) as hp:
                for b in range(HB):
                    step(hp, b, True)
            step(HP, 0, False)
            extra()

        @block.sync
        def _(e):
            def load_weights(hp):
                for m in range(3):
                    e.dma_start(w_raw[:, m], weights[m][hp]).then_inc(w_in, 16)
                    e.dma_start(b_raw[:, m:m + 1], biases[m][hp]).then_inc(w_in, 16)

            def step(hp, b, proj):
                s = HB * hp + b
                bp = (b - 1) % HB
                slot = hp + (1 if b else 0)
                if proj and b == 1:
                    e.wait_ge(act_w, 4 * hp + 4)
                    e.wait_ge(w_split, 3 * hp + 3)
                    load_weights((hp + 1) % HP)
                for h in range(2):
                    e.wait_ge(act_ov, 2 * s + h + 2)
                    rows = own[h]
                    sums = HD if h == 0 else 0
                    e.dma_start(o_raw[slot, rows, half * HTOK + bp * S:half * HTOK + (bp + 1) * S],
                                osb[rows, h]).then_inc(o_out[h], 16)
                    e.dma_start(o_sum[slot, h:h + 1, half * HTOK + bp * S:half * HTOK + (bp + 1) * S],
                                osb[sums:sums + 1, h]).then_inc(o_out[h], 16)

            def end():
                for h in range(2):
                    e.wait_ge(o_out[h], 32 * (HB * HP + 2))
                e.wait_ge(w_in, 96 * (HP + 1))

            load_weights(0)
            each_pair(e, step, end)

        @block.scalar
        def _(e):
            def split_weights(n):
                e.wait_ge(w_in, 96 * n + 96)
                for m in range(3):
                    nc.scalar.activation(w_hi[:, m], w_raw[:, m], ACT.Copy).then_inc(act_w, 1)
                nc.scalar.activation(bias[:, 0:3], b_raw[:, 0:3], ACT.Copy).then_inc(act_w, 1)

            def exp_tile(s, t):
                u = 8 * s + t
                e.wait_ge(pe_st, u + 1)
                e.wait_ge(dve_el, u + 1)
                nc.scalar.activation(ex[:, t % 2], st[:, t % 2], ACT.Exp, scale=SCALE).then_inc(act_ex, 1)

            def high_tile(s, t):
                u = 8 * s + t
                e.wait_ge(act_ex, u + 3)
                e.wait_ge(pe_av, u + 1)
                nc.scalar.activation(eh[:, t % 4], ex[:, t % 2], ACT.Copy).then_inc(act_eh, 1)

            def high_part(dst, s, b, m, h, count):
                e.wait_ge(pe_pj, 4 * s + m + 1)
                nc.scalar.activation(dst[own[h], b % 2, h], pj[own[h], m], ACT.Identity,
                                     bias=bias[own[h], m:m + 1]).then_inc(act_ev, 1)

            def max_row(s, par, h, n):
                e.wait_ge(pe_mr, n)
                r = mrow[h]
                nc.scalar.activation(qb[r:r + 1, par, h], mr[r:r + 1, :], ACT.Copy).then_inc(act_mr, 1)

            def out_tile(s, h):
                e.wait_ge(pe_av, 8 * s + 4 * h + 8)
                e.wait_ge(o_out[h], 32 * s + 32)
                nc.scalar.activation(osb[:, h], ov[:, :], ACT.Copy).then_inc(act_ov, 1)

            def step(hp, b, proj):
                s = HB * hp + b
                for t in range(8 + LAG):
                    if t < 8:
                        exp_tile(s, t)
                    if proj and t in (1, 2):
                        high_part(qa, s, b, 0, t - 1, 0)
                    if proj and t in (3, 4):
                        high_part(ka, s, b, 1, t - 3, 0)
                    if t == 2:
                        max_row(s, (b - 1) % 2, 1, 2 * s + 1)
                    if 1 <= t < 9:
                        high_tile(s, t - 1)
                    if proj and t == 6:
                        e.wait_ge(pe_pj, 4 * s + 3)
                        nc.scalar.activation(vt[:, :], pj[:, 0], ACT.Identity,
                                             bias=bias[:, 2:3]).then_inc(act_ev, 1)
                    if t == 6:
                        out_tile(s, 0)
                    if proj and t == 8:
                        e.wait_ge(pe_pj, 4 * s + 4)
                        nc.scalar.activation(va[:, b % 2, :, 0:3:2, :],
                                             pj[:, 1].rearrange("p (k h d) -> p k h d", h=2, d=HD),
                                             ACT.Copy).then_inc(act_ev, 1)
                        if b == HB - 1:
                            e.wait_ge(dve_ev, 5 * s + 9)
                            split_weights(hp + 1)
                if proj:
                    max_row(s, b % 2, 0, 2 * s + 2)
                out_tile(s, 1)

            e.sem_inc(act_ev, 6)
            e.sem_inc(act_mr, 1)
            e.sem_inc(act_ex, 2)
            e.sem_inc(act_ov, 1)
            e.sem_inc(o_out[0], 32)
            e.sem_inc(o_out[1], 32)
            split_weights(0)
            e.wait_ge(act_w, 4)
            e.wait_ge(zeroed, 12)
            each_pair(e, step, lambda: None)

        @block.vector
        def _(e):
            def split_weights(n):
                for m in range(3):
                    e.wait_ge(act_w, 4 * n + m + 1)
                    nc.vector.tensor_tensor(w_lo[:, m], w_raw[:, m], f32(w_hi[:, m]),
                                            ALU.subtract).then_inc(w_split, 1)

            def low_tile(s, t):
                u = 8 * s + t
                e.wait_ge(act_eh, u + 1)
                nc.vector.tensor_tensor(el[:, t % 4], ex[:, t % 2], f32(eh[:, t % 4]),
                                        ALU.subtract).then_inc(dve_el, 1)

            def low_part(dst, rows, hi, s, b, m, h):
                e.wait_ge(act_ev, 6 * s + 2 * m + h + 7)
                nc.vector.scalar_tensor_tensor(dst[rows, b % 2, h], pj[own[h], m],
                                               bias[own[h], m:m + 1], f32(hi[own[h], b % 2, h]),
                                               ALU.add, ALU.subtract).then_inc(dve_ev, 1)

            def max_tile(s, v):
                e.wait_ge(pe_mx, 8 * s + v + 1)
                h, t = v // NT, v % NT
                nc.vector.tensor_reduce(negm[:, h, t, mrow[h]:mrow[h] + 1], mx[:, v % 2], AX_X,
                                        ALU.max, negate=True).then_inc(dve_mx, 1)

            def step(hp, b, proj):
                s = HB * hp + b
                for t in range(8 + LAG):
                    if 1 <= t < 9:
                        low_tile(s, t - 1)
                    if not proj:
                        continue
                    if t in (2, 3):
                        low_part(qa, other[t - 2], qa, s, b, 0, t - 2)
                    if t in (4, 5):
                        low_part(kb, own[t - 4], ka, s, b, 1, t - 4)
                    if t == 9:
                        e.wait_ge(act_ev, 6 * s + 12)
                        nc.vector.tensor_tensor(vb[:, b % 2, :, 0:3:2, :],
                                                pj[:, 1].rearrange("p (k h d) -> p k h d", h=2, d=HD),
                                                f32(va[:, b % 2, :, 0:3:2, :]),
                                                ALU.subtract).then_inc(dve_ev, 1)
                        if b == HB - 1:
                            split_weights(hp + 1)
                    for v in MAX_AT.get(t, ()):
                        max_tile(s, v)

            for tile, value in ((qa, 0.0), (qb, 0.0), (ka, 0.0), (kb, 0.0), (va, 0.0), (vb, 0.0),
                                (negm, 0.0)):
                nc.vector.memset(f32(tile[:]), value).then_inc(zeroed, 1)
            e.wait_ge(zeroed, 7)
            nc.vector.memset(f32(va[:, :, :, 1, :]), 1.0).then_inc(zeroed, 1)
            for h in range(2):
                for par in range(2):
                    nc.vector.memset(f32(kb[mrow[h]:mrow[h] + 1, par, h]), 1.0).then_inc(zeroed, 1)
            e.wait_ge(zeroed, 12)
            e.sem_inc(dve_ev, 5)
            e.sem_inc(dve_mx, 2)
            e.sem_inc(dve_el, 2)
            split_weights(0)
            each_pair(e, step, lambda: None)

        @block.gpsimd
        def _(e):
            e.wait_ge(zeroed, 12)

            def step(hp, b, proj):
                if not proj:
                    return
                s = HB * hp + b
                for h in range(2):
                    e.wait_ge(act_ev, 6 * s + h + 7)
                    e.sem_inc(passed, 1)
                    nc.gpsimd.tensor_scalar(qb[own[h], b % 2, h], f32(qa[own[h], b % 2, h]), 1.0, 1.0,
                                            ALU.mult, ALU.mult).then_inc(pool_ev, 1)
                    e.wait_ge(pool_ev, 4 * s + h + 1)
                for h in range(2):
                    e.wait_ge(act_ev, 6 * s + h + 9)
                    e.sem_inc(passed, 1)
                    nc.gpsimd.tensor_scalar(ka[other[h], b % 2, h], f32(ka[own[h], b % 2, h]), 1.0, 1.0,
                                            ALU.mult, ALU.mult).then_inc(pool_ev, 1)
                    e.wait_ge(pool_ev, 4 * s + h + 3)

            each_pair(e, step, lambda: None)

        @block.tensor
        def _(e):
            def projection(b, m):
                passes = [(w_hi, xh), (w_lo, xh), (w_hi, xl)]
                for n, (w, xx) in enumerate(passes):
                    for k in range(DK):
                        yield nc.tensor.matmul(pj[:, m % 2], w[:, m, k], xx[:, k, b * S:(b + 1) * S],
                                               start=(n == 0 and k == 0), stop=(n == 2 and k == DK - 1))

            def scores(s, par, t):
                u = 8 * s + t
                h, kt = t // NT, t % NT
                cols = slice(kt * P, (kt + 1) * P)
                if kt == 0:
                    e.wait_ge(act_mr, 2 * s + h + 1)
                    e.wait_ge(dve_ev, 5 * s + 5)
                e.wait_ge(act_ex, u + 1)
                nc.tensor.matmul(st[:, t % 2], ka[:, par, h, cols], qa[:, par, h], start=True, stop=False)
                nc.tensor.matmul(st[:, t % 2], kb[:, par, h, cols], qb[:, par, h], start=False,
                                 stop=True).then_inc(pe_st, 1)

            def product(s, par, t):
                u = 8 * s + t
                h, kt = t // NT, t % NT
                e.wait_ge(dve_el, u + 3)
                if kt == 0:
                    e.wait_ge(act_ov, 2 * s + h + 1)
                a = va[:, par, kt].rearrange("p c d -> p (c d)")[:, HD * h:HD * h + P]
                c = vb[:, par, kt].rearrange("p c d -> p (c d)")[:, HD * h:HD * h + P]
                nc.tensor.matmul(ov[:, :], a, eh[:, t % 4], start=(kt == 0), stop=False)
                nc.tensor.matmul(ov[:, :], c, eh[:, t % 4], start=False, stop=False)
                nc.tensor.matmul(ov[:, :], a, el[:, t % 4], start=False, stop=(kt == NT - 1)).then_inc(pe_av, 1)

            def max_scores(s, par, v):
                h, qt = v // NT, v % NT
                if v == 0:
                    e.wait_ge(act_ev, 6 * s + 10)
                    e.wait_ge(dve_ev, 5 * s + 7)
                    e.wait_ge(pool_ev, 4 * s + 4)
                e.wait_ge(dve_mx, 8 * s + v + 1)
                nc.tensor.matmul(mx[:, v % 2], qa[:, par, h, qt * P:(qt + 1) * P], ka[:, par, h],
                                 start=True, stop=True).then_inc(pe_mx, 1)

            def max_row(s, h, maxima, rows):
                e.wait_ge(dve_mx, maxima)
                e.wait_ge(act_mr, rows)
                for t in range(NT):
                    last = nc.tensor.matmul(mr[:, t * P:(t + 1) * P], negm[:, h, t], ident_r[:, :],
                                            start=True, stop=True)
                last.then_inc(pe_mr, 1)

            def step(hp, b, proj):
                s = HB * hp + b
                par = (b - 1) % 2
                work = None
                for t in range(8 + LAG):
                    if proj and t in (0, 2, 4):
                        m = t // 2
                        if b == 0 and m == 0:
                            e.wait_ge(act_w, 4 * hp + 4)
                            e.wait_ge(w_split, 3 * hp + 3)
                        if m == 0:
                            e.wait_ge(act_ev, 6 * s + 5)
                        elif m == 1:
                            e.wait_ge(act_ev, 6 * s + 6)
                            e.wait_ge(dve_ev, 5 * s + 5)
                        else:
                            e.wait_ge(act_ev, 6 * s + 8)
                            e.wait_ge(dve_ev, 5 * s + 7)
                        work = projection(b, m)
                    if work is not None:
                        for _ in range(6):
                            last = next(work)
                        if t % 2:
                            last.then_inc(pe_pj, 1)
                            work = None
                    if t == 2:
                        max_row(s, 1, 8 * s + 2, 2 * s + 1)
                    if t < 8:
                        scores(s, par, t)
                    if t >= LAG:
                        product(s, par, t - LAG)
                    if proj and t == 7:
                        e.wait_ge(act_ev, 6 * s + 11)
                        e.wait_ge(dve_ev, 5 * s + 9)
                        for kt in range(NT):
                            last = nc.tensor.transpose(pj[:, 1, kt * P:(kt + 1) * P],
                                                       vt[:, kt * P:(kt + 1) * P], ident[:, :])
                        last.then_inc(pe_pj, 1)
                    if proj:
                        for v in MAX_AT.get(t, ()):
                            max_scores(s, b % 2, v)
                if proj:
                    max_row(s, 0, 8 * s + 6, 2 * s + 2)

            e.sem_inc(pe_av, 4)
            e.wait_ge(zeroed, 12)
            each_pair(e, step, lambda: None)


MAX_AT = {5: (0,), 6: (1, 2), 7: (3, 4), 8: (5, 6), 9: (7,)}


def reciprocal_stage(nc, env, name):
    dst = env[f"{name}_rcp"]
    src = env["o_sum"][1:] if name == "o" else env["c_raw"][:, :, 2 * XD, S:]
    slots, heads = dst.shape[0], dst.shape[1]
    cut = P // (slots * heads)
    width = T // cut
    with ExitStack() as ctx:
        sp = Space(nc, ctx, f"{name}rc")
        sums = sp.sb("sums", [P, width])
        rcp = sp.sb("rcp", [P, width])
        landed = sp.sem("landed")
        done = sp.sem("done")
        stored = sp.sem("stored")
        block = ctx.enter_context(nc.Block())

        @block.sync
        def _(e):
            for n in range(slots):
                for h in range(heads):
                    row = (n * heads + h) * cut
                    e.dma_start(sums[row:row + cut, :], src[n, h].rearrange("(c w) -> c w", w=width)).then_inc(landed, 16)
            e.wait_ge(done, 1)
            for n in range(slots):
                for h in range(heads):
                    row = (n * heads + h) * cut
                    e.dma_start(dst[n, h].rearrange("(c w) -> c w", w=width), rcp[row:row + cut, :]).then_inc(stored, 16)
            e.wait_ge(stored, 16 * slots * heads)

        @block.vector
        def _(e):
            e.wait_ge(landed, 16 * slots * heads)
            nc.vector.reciprocal(rcp[:, :], sums[:, :]).then_inc(done, 1)


def output_stage(nc, env, name):
    ident, mhalf = env["ident"], env["minus_half"]
    final = name == "c"
    KT = CTX_TILES if final else HP
    heads = 4 if final else 2
    width = P // heads
    rcp = env[f"{name}_rcp"]
    x_in = env["x1"] if final else env["x"]
    x_out = env["x2"] if final else env["x1"]
    wo = env["Wo2" if final else "Wo"].rearrange("(k p) n -> p k n", p=P)
    RING = 4
    LW = 2
    parts = 2 if final else 1
    per_chunk = 16 * (8 + heads if final else 1 + heads)
    xt_out = [env["xn3"]] if final else [env["xn2_hi"], env["xn2_lo"]]
    OUTS = 16 * len(xt_out)

    with ExitStack() as ctx:
        sp = Space(nc, ctx, f"{name}p")
        w_raw = sp.sb("w_raw", [P, 2, LW, D])
        w_hi = sp.sb("w_hi", [P, KT, D], F32R)
        w_lo = sp.sb("w_lo", [P, KT, D], F32R)
        o = sp.sb("o", [P, RING, parts, S])
        r = sp.sb("r", [P, RING, S])
        oh = sp.sb("oh", [P, RING, S], F32R)
        ol = sp.sb("ol", [P, RING, S], F32R)
        xin = sp.sb("xin", [P, 2, NT, D])
        x1 = sp.sb("x1", [P, 2, NT, D])
        xn = sp.sb("xn", [P, NT, D])
        stats = sp.sb("stats", [P, NT, 6])
        mv = sp.sb("mv", [P, NT, 2])
        ve = sp.sb("ve", [P, NT])
        rstd = sp.sb("rstd", [P, NT])
        xo = sp.sb("xo", [P, 2, DK, S], F32 if final else F32R)
        if not final:
            xol = sp.sb("xol", [P, 2, DK, S], F32R)
            bo = sp.sb("bo", [1, D])
            bo_hi = sp.sb("bo_hi", [1, D], F32R)
            bo_lo = sp.sb("bo_lo", [1, D], F32R)
            ones = sp.sb("ones", [1, P], F32R)
        acc = sp.ps("acc", [P, NT, D])
        pt = sp.ps("pt", [P, NT, DK, P])
        w_in = [sp.sem(f"w_in{i}") for i in range(2)]
        act_w = sp.sem("act_w")
        dve_w = sp.sem("dve_w")
        chunk_in = [sp.sem(f"chunk_in{i}") for i in range(RING)]
        dve_o = sp.sem("dve_o")
        act_oh = sp.sem("act_oh")
        dve_ol = sp.sem("dve_ol")
        pe_ck = sp.sem("pe_ck")
        pe_acc = sp.sem("pe_acc")
        xin_in = [sp.sem(f"xin_in{i}") for i in range(2)]
        dve_x1 = sp.sem("dve_x1")
        x1_out = [sp.sem(f"x1_out{i}") for i in range(2)]
        passed = sp.sem("passed")
        dve_st = sp.sem("dve_st")
        pool_rs = sp.sem("pool_rs")
        dve_xn = sp.sem("dve_xn")
        pe_tr = sp.sem("pe_tr")
        act_hi = sp.sem("act_hi")
        dve_lo = sp.sem("dve_lo")
        xo_out = [sp.sem(f"xo_out{i}") for i in range(2)]
        bo_in = sp.sem("bo_in")
        ones_in = sp.sem("ones_in")

        xs_in = x_in.rearrange("(g n p) d -> g p n d", n=NT, p=P)
        xs_out = x_out.rearrange("(g n p) d -> g p n d", n=NT, p=P)
        block = ctx.enter_context(nc.Block())

        @block.sync
        def _(e):
            for n in range(KT // LW):
                if n >= 2:
                    e.wait_ge(act_w, n - 1)
                    e.wait_ge(dve_w, n - 1)
                e.dma_start(w_raw[:, n % 2], wo[:, n * LW:(n + 1) * LW]).then_inc(w_in[n % 2], 16)
            if not final:
                e.dma_start(bo[:, :], env["bo"].rearrange("(a n) -> a n", a=1)).then_inc(bo_in, 16)
            with e.Fori(0, B // 2) as g2:
                for u in range(2):
                    g = 2 * g2 + u
                    at = bass.ds(g * S, S)
                    e.wait_ge(dve_x1, 8 * g2 + 4 * u + 4)
                    e.dma_start(xin[:, u], xs_in[g]).then_inc(xin_in[u], 16)
                    for k in range(KT):
                        c = k % RING
                        e.wait_ge(dve_ol, KT * g + k + 1)
                        e.wait_ge(act_oh, KT * g + k + 1)
                        if final:
                            for n in range(parts):
                                for h in range(heads):
                                    e.dma_start(o[h * width:(h + 1) * width, c, n],
                                                env["c_raw"][k, h, n * width:(n + 1) * width,
                                                             bass.ds(g * S + S, S)]).then_inc(chunk_in[c], 16)
                        else:
                            e.dma_start(o[:, c, 0], env["o_raw"][k + 1, :, at]).then_inc(chunk_in[c], 16)
                        for h in range(heads):
                            e.dma_start(r[h * width:(h + 1) * width, c],
                                        rcp[k, h:h + 1, at].partition_broadcast(width)
                                        ).then_inc(chunk_in[c], 16)

        @block.gpsimd
        def _(e):
            with e.Fori(0, B // 2) as g2:
                for u in range(2):
                    g = 2 * g2 + u
                    e.wait_ge(dve_st, 9 * g + 9)
                    nc.gpsimd.tensor_tensor(rstd[:, :], ve[:, :], mhalf[:, 0:NT], ALU.pow).then_inc(pool_rs, 1)

        @block.scalar
        def _(e):
            for n in range(KT // LW):
                e.wait_ge(w_in[n % 2], 16 * (n // 2) + 16)
                nc.scalar.activation(w_hi[:, n * LW:(n + 1) * LW], w_raw[:, n % 2], ACT.Copy).then_inc(act_w, 1)
            if not final:
                e.wait_ge(bo_in, 16)
                nc.scalar.activation(bo_hi[:, :], bo[:, :], ACT.Copy).then_inc(ones_in, 1)
            e.sem_inc(act_oh, RING)
            e.sem_inc(act_hi, 4)
            for u in range(2):
                e.sem_inc(x1_out[u], 16)
                e.sem_inc(xo_out[u], OUTS)
            with e.Fori(0, B // 2) as g2:
                for u in range(2):
                    g = 2 * g2 + u
                    for k in range(KT):
                        c = k % RING
                        e.wait_ge(dve_o, parts * (KT * g + k + 1))
                        e.wait_ge(pe_ck, KT * g + k + 1)
                        nc.scalar.activation(oh[:, c], o[:, c, 0], ACT.Copy).then_inc(act_oh, 1)
                    e.wait_ge(xo_out[u], OUTS * g2 + OUTS)
                    for t in range(NT):
                        e.wait_ge(pe_tr, 4 * g + t + 5)
                        nc.scalar.activation(xo[:, u, :, t * P:(t + 1) * P], pt[:, t], ACT.Copy).then_inc(act_hi, 1)
                    e.wait_ge(dve_x1, 4 * g + 12)
                    e.dma_start(xs_out[g], x1[:, u]).then_inc(x1_out[u], 16)
                    e.wait_ge(act_hi, 4 * g + 8)
                    e.wait_ge(dve_lo, 4 * g + 8)
                    e.dma_start(xt_out[0][:, :, bass.ds(g * S, S)], xo[:, u].bitcast(F32)).then_inc(xo_out[u], 16)
                    if not final:
                        e.dma_start(xt_out[1][:, :, bass.ds(g * S, S)], f32(xol[:, u])).then_inc(xo_out[u], 16)
            for u in range(2):
                e.wait_ge(x1_out[u], 16 * (B // 2) + 16)
                e.wait_ge(xo_out[u], OUTS * (B // 2) + OUTS)

        @block.vector
        def _(e):
            if not final:
                nc.vector.memset(f32(ones[:, :]), 1.0).then_inc(ones_in, 1)
            for n in range(KT // LW):
                e.wait_ge(act_w, n + 1)
                nc.vector.tensor_tensor(w_lo[:, n * LW:(n + 1) * LW], w_raw[:, n % 2],
                                        f32(w_hi[:, n * LW:(n + 1) * LW]), ALU.subtract).then_inc(dve_w, 1)
            if not final:
                e.wait_ge(ones_in, 2)
                nc.vector.tensor_tensor(bo_lo[:, :], bo[:, :], f32(bo_hi[:, :]), ALU.subtract).then_inc(ones_in, 1)
            e.sem_inc(dve_ol, RING)
            e.sem_inc(dve_x1, 8)
            e.sem_inc(dve_lo, 4)
            with e.Fori(0, B // 2) as g2:
                for u in range(2):
                    g = 2 * g2 + u

                    def normalise(k):
                        c = k % RING
                        need = per_chunk * ((KT // RING) * g + k // RING + 1)
                        e.wait_ge(chunk_in[c], need)
                        if final:
                            nc.vector.tensor_tensor(o[:, c, 0], o[:, c, 0], o[:, c, 1], ALU.add).then_inc(dve_o, 1)
                            e.wait_ge(dve_o, 2 * (KT * g + k) + 1)
                        nc.vector.tensor_tensor(o[:, c, 0], o[:, c, 0], r[:, c], ALU.mult).then_inc(dve_o, 1)

                    def low(k):
                        c = k % RING
                        e.wait_ge(act_oh, KT * g + k + 1 + RING)
                        nc.vector.tensor_tensor(ol[:, c], o[:, c, 0], f32(oh[:, c]), ALU.subtract).then_inc(dve_ol, 1)

                    for k in range(KT):
                        normalise(k)
                        if k:
                            low(k - 1)
                    low(KT - 1)
                    if final:
                        e.wait_ge(pe_ck, KT * g + KT + RING)
                    else:
                        e.wait_ge(pe_acc, g + 1)
                    e.wait_ge(xin_in[u], 16 * g2 + 16)
                    e.wait_ge(x1_out[u], 16 * g2 + 16)
                    for t in range(NT):
                        nc.vector.tensor_tensor(x1[:, u, t], acc[:, t], xin[:, u, t], ALU.add).then_inc(dve_x1, 1)
                    for t in range(NT):
                        e.wait_ge(dve_x1, 4 * g + t + 9)
                        nc.vector.bn_stats(stats[:, t], x1[:, u, t]).then_inc(dve_st, 1)
                    for t in range(NT):
                        e.wait_ge(dve_st, 9 * g + t + 1)
                        e.sem_inc(passed, 1)
                        nc.vector.bn_aggr(mv[:, t], stats[:, t]).then_inc(dve_st, 1)
                    e.wait_ge(dve_st, 9 * g + 8)
                    nc.vector.tensor_scalar(ve[:, :], mv[:, :, 1], EPS, None, ALU.add).then_inc(dve_st, 1)
                    e.wait_ge(pool_rs, g + 1)
                    for t in range(NT):
                        e.wait_ge(pe_tr, 4 * g + t + 1)
                        nc.vector.tensor_scalar(xn[:, t], x1[:, u, t], mv[:, t, 0:1], rstd[:, t:t + 1],
                                                ALU.subtract, ALU.mult).then_inc(dve_xn, 1)
                    for t in range(NT):
                        e.wait_ge(act_hi, 4 * g + t + 5)
                        if final:
                            nc.vector.tensor_reduce(env["xn3_max"][:, bass.ds(4 * g + t, 1)],
                                                    xo[:, u, :, t * P:(t + 1) * P], AX_XY, ALU.max,
                                                    apply_absolute_value=True).then_inc(dve_lo, 1)
                        else:
                            cols = slice(t * P, (t + 1) * P)
                            nc.vector.tensor_tensor(xol[:, u, :, cols], pt[:, t], f32(xo[:, u, :, cols]),
                                                    ALU.subtract).then_inc(dve_lo, 1)

        @block.tensor
        def _(e):
            e.wait_ge(act_w, KT // LW)
            e.wait_ge(dve_w, KT // LW)
            if not final:
                e.wait_ge(ones_in, 3)
            e.sem_inc(pe_ck, RING)
            e.sem_inc(pe_tr, 4)
            with e.Fori(0, B) as g:
                e.wait_ge(dve_x1, 4 * g + 8)
                for k in range(KT):
                    c = k % RING
                    e.wait_ge(dve_ol, KT * g + k + 1 + RING)
                    for t in range(NT):
                        cols = slice(t * P, (t + 1) * P)
                        start = k == 0
                        stop = final and k == KT - 1
                        nc.tensor.matmul(acc[:, t], oh[:, c, cols], w_hi[:, k], start=start, stop=False)
                        nc.tensor.matmul(acc[:, t], oh[:, c, cols], w_lo[:, k], start=False, stop=False)
                        last = nc.tensor.matmul(acc[:, t], ol[:, c, cols], w_hi[:, k], start=False, stop=stop)
                    last.then_inc(pe_ck, 1)
                if not final:
                    for t in range(NT):
                        nc.tensor.matmul(acc[:, t], ones[:, :], bo_hi[:, :], start=False, stop=False)
                        last = nc.tensor.matmul(acc[:, t], ones[:, :], bo_lo[:, :], start=False, stop=True)
                    last.then_inc(pe_acc, 1)
                for t in range(NT):
                    e.wait_ge(dve_xn, 4 * g + t + 1)
                    e.wait_ge(dve_lo, 4 * g + t + 1)
                    e.wait_ge(act_hi, 4 * g + t + 1)
                    for k in range(DK):
                        last = nc.tensor.transpose(pt[:, t, k], xn[:, t, k * P:(k + 1) * P], ident[:, :])
                    last.then_inc(pe_tr, 1)


def context_stage(nc, env):
    ident = env["ident"]
    with ExitStack() as ctx:
        sp = Space(nc, ctx, "cx")
        xt = sp.sb("x", [P, 2, NT, CD])
        ch = sp.sb("ch", [P, 2, CK, S], F32R)
        cl = sp.sb("cl", [P, 2, CK, S], F32R)
        mask_u8 = sp.sb("mask_u8", [B, S], U8)
        mask_f = sp.sb("mask_f", [B, S])
        mask_n = sp.sb("mask_n", [B, S])
        pt = sp.ps("pt", [P, NT, 4, P])
        x_in = [sp.sem(f"x_in{i}") for i in range(2)]
        pe_tr = sp.sem("pe_tr")
        act_hi = sp.sem("act_hi")
        dve_lo = sp.sem("dve_lo")
        c_out = [sp.sem(f"c_out{i}") for i in range(2)]
        mask_in = sp.sem("mask_in")
        mask_done = sp.sem("mask_done")
        mask_out = sp.sem("mask_out")
        xs = env["ctx"].rearrange("(g n p) d -> g p n d", n=NT, p=P)
        block = ctx.enter_context(nc.Block())

        @block.sync
        def _(e):
            e.dma_start(mask_u8[:, :], env["mask"]).then_inc(mask_in, 16)
            with e.Fori(0, B // 2) as g2:
                for u in range(2):
                    e.wait_ge(pe_tr, 8 * g2 + 4 * u + 4)
                    e.dma_start(xt[:, u], xs[2 * g2 + u]).then_inc(x_in[u], 16)
            e.wait_ge(mask_done, 2)
            e.dma_start(env["mask_f"], mask_f[:, :]).then_inc(mask_out, 16)
            e.dma_start(env["mask_n"], mask_n[:, :]).then_inc(mask_out, 16)
            e.wait_ge(mask_out, 32)

        @block.tensor
        def _(e):
            e.sem_inc(pe_tr, 8)
            with e.Fori(0, B // 2) as g2:
                for u in range(2):
                    g = 2 * g2 + u
                    e.wait_ge(x_in[u], 16 * g2 + 16)
                    for t in range(NT):
                        e.wait_ge(dve_lo, 4 * g + t + 1)
                        for k in range(CK):
                            last = nc.tensor.transpose(pt[:, t, k], xt[:, u, t, k * P:(k + 1) * P], ident[:, :])
                        last.then_inc(pe_tr, 1)

        @block.scalar
        def _(e):
            e.sem_inc(act_hi, 4)
            e.sem_inc(c_out[0], 32)
            e.sem_inc(c_out[1], 32)
            with e.Fori(0, B // 2) as g2:
                for u in range(2):
                    g = 2 * g2 + u
                    e.wait_ge(c_out[u], 32 * g2 + 32)
                    for t in range(NT):
                        e.wait_ge(pe_tr, 4 * g + t + 9)
                        nc.scalar.activation(ch[:, u, :, t * P:(t + 1) * P], pt[:, t, 0:CK], ACT.Copy).then_inc(act_hi, 1)
                    e.wait_ge(act_hi, 4 * g + 8)
                    e.dma_start(env["ct_hi"][:, :, bass.ds(g * S, S)], f32(ch[:, u])).then_inc(c_out[u], 16)
                    e.wait_ge(dve_lo, 4 * g + 8)
                    e.dma_start(env["ct_lo"][:, :, bass.ds(g * S, S)], f32(cl[:, u])).then_inc(c_out[u], 16)
            for u in range(2):
                e.wait_ge(c_out[u], 32 * (B // 2) + 32)

        @block.vector
        def _(e):
            e.sem_inc(dve_lo, 4)
            e.wait_ge(mask_in, 16)
            nc.vector.tensor_copy(mask_f[:, :], mask_u8[:, :]).then_inc(mask_done, 1)
            e.wait_ge(mask_done, 1)
            nc.vector.tensor_scalar(mask_n[:, :], mask_f[:, :], 1.0, BIG, ALU.subtract, ALU.mult).then_inc(mask_done, 1)
            with e.Fori(0, B // 2) as g2:
                for u in range(2):
                    g = 2 * g2 + u
                    for t in range(NT):
                        cols = slice(t * P, (t + 1) * P)
                        e.wait_ge(act_hi, 4 * g + t + 5)
                        nc.vector.tensor_tensor(cl[:, u, :, cols], pt[:, t, 0:CK], f32(ch[:, u, :, cols]),
                                                ALU.subtract).then_inc(dve_lo, 1)


def cross_attention_stage(nc, env):
    ident, ident_r = env["ident"], env["ident_r"]
    SCALE = XD ** -0.5
    HS = 4
    SL = HS * NT
    LAG = 2
    VW = 3 * XD
    MR = 3 * XD
    ROWS = 2 * XD + 1

    with ExitStack() as ctx:
        sp = Space(nc, ctx, "ca")
        w_raw = sp.sb("w_raw", [P, 2, D])
        w_hi = sp.sb("w_hi", [P, 10, D], F32R)
        w_lo = sp.sb("w_lo", [P, 10, D], F32R)
        xq = sp.sb("xq", [P, 2, DK, S], F32R)
        xc = sp.sb("xc", [P, 2, CK, S], F32R)
        maskb = sp.sb("maskb", [P, S])
        qh = sp.sb("qh", [P, S], F32R)
        ql = sp.sb("ql", [P, S], F32R)
        km = sp.sb("km", [P, S])
        kh = sp.sb("kh", [P, S], F32R)
        kl = sp.sb("kl", [P, S], F32R)
        q4 = sp.sb("q4", [P, 2, HS, S], F32R)
        k4 = sp.sb("k4", [P, 2, HS, S], F32R)
        vt = sp.sb("vt", [P, S])
        vc = sp.sb("vc", [P, 2, NT, HS, VW], F32R)
        ex = sp.sb("ex", [P, 2, S])
        eh = sp.sb("eh", [P, 4, S], F32R)
        el = sp.sb("el", [P, 4, S], F32R)
        negm = sp.sb("negm", [P, 2, NT, P], F32R)
        osb = sp.sb("osb", [VW, 2, S])
        pj = sp.ps("pj", [P, 2, S])
        st = sp.ps("st", [P, 2, S])
        mx = sp.ps("mx", [P, 2, S])
        ov = sp.ps("ov", [P, S])
        mr = sp.ps("mr", [P, S])

        w_in = [sp.sem(f"w_in{i}") for i in range(2)]
        act_w = sp.sem("act_w")
        dve_w = sp.sem("dve_w")
        zeroed = sp.sem("zeroed")
        xc_in = sp.sem("xc_in")
        xq_in = sp.sem("xq_in")
        mk_in = [sp.sem(f"mk_in{i}") for i in range(2)]
        pe_pj = sp.sem("pe_pj")
        act_ev = sp.sem("act_ev")
        dve_ev = sp.sem("dve_ev")
        k4_in = [sp.sem(f"k4_in{i}") for i in range(2)]
        q4_in = [sp.sem(f"q4_in{i}") for i in range(2)]
        pe_mx = sp.sem("pe_mx")
        dve_mx = sp.sem("dve_mx")
        pe_mr = sp.sem("pe_mr")
        act_mr = sp.sem("act_mr")
        pe_st = sp.sem("pe_st")
        act_ex = sp.sem("act_ex")
        act_eh = sp.sem("act_eh")
        dve_el = sp.sem("dve_el")
        pe_av = sp.sem("pe_av")
        act_ov = sp.sem("act_ov")
        o_out = [sp.sem(f"o_out{i}") for i in range(2)]
        STEP_IN = 16 * 3 * HS

        block = ctx.enter_context(nc.Block())

        def each_step(e, step):
            with e.Fori(0, B) as b:
                for g in range(XG):
                    step(b, g, True)
            step(B, 0, False)

        @block.sync
        def _(e):
            def stack(dst, par, block_rows, src, landed):
                for j in range(HS):
                    e.dma_start(f32(dst[block_rows * XD:(block_rows + 1) * XD, par, j]),
                                f32(src[j * XD:(j + 1) * XD, :])).then_inc(landed, 16)

            def outputs(b, g, j):
                s = XG * b + g
                e.wait_ge(act_ov, 4 * s + j + 2)
                gp = (g - 1) % XG
                at = bass.ds((b + (1 if g else 0)) * S, S)
                e.dma_start(env["c_raw"][gp, j, 0:ROWS, at], osb[0:ROWS, j % 2]).then_inc(o_out[j % 2], 16)

            def step(b, g, proj):
                s = XG * b + g
                par = g % 2
                if proj:
                    e.wait_ge(dve_ev, 4 * s + 5)
                    stack(q4, par, 0, qh, q4_in[par])
                    stack(q4, par, 1, ql, q4_in[par])
                    stack(q4, par, 2, qh, q4_in[par])
                    if g == XG - 1:
                        load_batch_q((b + 1) % B, s)
                    e.wait_ge(dve_ev, 4 * s + 7)
                    if g < 2:
                        for j in range(HS):
                            e.dma_start(f32(k4[MR:MR + 1, par, j]), env["mask_n"][bass.ds(b, 1), :]
                                        ).then_inc(mk_in[par], 16)
                    stack(k4, par, 0, kh, k4_in[par])
                    stack(k4, par, 1, kh, k4_in[par])
                    stack(k4, par, 2, kl, k4_in[par])
                outputs(b, g, 0)
                if proj and g == XG - 1:
                    load_batch_c((b + 1) % B, s)
                for j in range(1, HS):
                    outputs(b, g, j)

            def load_batch_c(nb, s):
                if s is not None:
                    e.wait_ge(pe_pj, 4 * s + 7)
                e.dma_start(f32(xc[:, 0]), env["ct_hi"][:, :, bass.ds(nb * S, S)]).then_inc(xc_in, 16)
                e.dma_start(f32(xc[:, 1]), env["ct_lo"][:, :, bass.ds(nb * S, S)]).then_inc(xc_in, 16)
                e.dma_start(maskb[:, :], env["mask_f"][bass.ds(nb, 1), :].partition_broadcast(P)
                            ).then_inc(xc_in, 16)

            def load_batch_q(nb, s):
                if s is not None:
                    e.wait_ge(pe_pj, 4 * s + 5)
                e.dma_start(f32(xq[:, 0]), env["xn2_hi"][:, :, bass.ds(nb * S, S)]).then_inc(xq_in, 16)
                e.dma_start(f32(xq[:, 1]), env["xn2_lo"][:, :, bass.ds(nb * S, S)]).then_inc(xq_in, 16)

            tiles = [(env[n].rearrange("(k p) n -> k p n", p=P), k)
                     for n, kk in (("Wk2", CK), ("Wv2", CK), ("Wq2", DK)) for k in range(kk)]
            for n, (w, k) in enumerate(tiles):
                if n >= 2:
                    e.wait_ge(dve_w, n - 1)
                e.dma_start(w_raw[:, n % 2], w[k]).then_inc(w_in[n % 2], 16)
            load_batch_q(0, None)
            load_batch_c(0, None)
            e.wait_ge(zeroed, ZEROED)
            each_step(e, step)
            for i in range(2):
                e.wait_ge(o_out[i], 16 * (2 * XG * B + 2) + 16)
            e.wait_ge(xc_in, 48 * (B + 1))
            e.wait_ge(xq_in, 32 * (B + 1))

        @block.scalar
        def _(e):
            def exp_tile(s, t):
                u = SL * s + t
                e.wait_ge(pe_st, u + 1)
                e.wait_ge(dve_el, u + 1)
                nc.scalar.activation(ex[:, t % 2], st[:, t % 2], ACT.Exp, scale=SCALE).then_inc(act_ex, 1)

            def high_tile(s, t):
                u = SL * s + t
                e.wait_ge(act_ex, u + 3)
                e.wait_ge(pe_av, u + 1)
                nc.scalar.activation(eh[:, t % 4], ex[:, t % 2], ACT.Copy).then_inc(act_eh, 1)

            def max_row(par, h, n):
                e.wait_ge(pe_mr, n)
                nc.scalar.activation(q4[MR:MR + 2, par, h], mr[MR:MR + 2, :], ACT.Copy).then_inc(act_mr, 1)

            def out_tile(s, h):
                e.wait_ge(pe_av, SL * s + NT * h + 8)
                e.wait_ge(o_out[h % 2], 16 * (2 * s + h // 2) + 16)
                nc.scalar.activation(osb[:, h % 2], ov[0:VW, :], ACT.Copy).then_inc(act_ov, 1)

            def step(b, g, proj):
                s = XG * b + g
                par = g % 2
                for t in range(SL + LAG):
                    if t < SL:
                        exp_tile(s, t)
                    if 1 <= t <= SL:
                        high_tile(s, t - 1)
                    if proj and t == 3:
                        e.wait_ge(pe_pj, 4 * s + 5)
                        e.wait_ge(q4_in[1 - par], stacked(b, g - 1))
                        nc.scalar.activation(qh[:, :], pj[:, 1], ACT.Copy).then_inc(act_ev, 1)
                    if proj and t == 7:
                        e.wait_ge(dve_ev, 4 * s + 6)
                        e.wait_ge(k4_in[1 - par], stacked(b, g - 1))
                        nc.scalar.activation(kh[:, :], km[:, :], ACT.Copy).then_inc(act_ev, 1)
                    if proj and t == 9:
                        e.wait_ge(pe_pj, 4 * s + 7)
                        nc.scalar.activation(vt[:, :], pj[:, 1], ACT.Copy).then_inc(act_ev, 1)
                    if proj and t == 11:
                        e.wait_ge(pe_pj, 4 * s + 8)
                        nc.scalar.activation(vc[:, par, :, :, 0:XD],
                                             pj[:, 0].rearrange("p (k h d) -> p k h d", h=HS, d=XD),
                                             ACT.Copy).then_inc(act_ev, 1)
                    if t == 6:
                        max_row(1 - par, 2, 4 * s + 1)
                        out_tile(s, 0)
                    if t == 10:
                        max_row(1 - par, 3, 4 * s + 2)
                        out_tile(s, 1)
                    if t == 14:
                        out_tile(s, 2)
                    if proj and t == 17:
                        max_row(par, 0, 4 * s + 3)
                if proj:
                    max_row(par, 1, 4 * s + 4)
                out_tile(s, 3)

            def stacked(b, g):
                if g < 0:
                    return STEP_IN * 2 * b + STEP_IN
                return STEP_IN * (2 * b + g // 2 + 1) + STEP_IN

            for n in range(10):
                e.wait_ge(w_in[n % 2], 16 * (n // 2) + 16)
                nc.scalar.activation(w_hi[:, n], w_raw[:, n % 2], ACT.Copy).then_inc(act_w, 1)
            e.sem_inc(act_ev, 4)
            e.sem_inc(act_mr, 1)
            e.sem_inc(act_ex, 2)
            e.sem_inc(act_ov, 1)
            for i in range(2):
                e.sem_inc(o_out[i], 16)
                e.sem_inc(k4_in[i], STEP_IN)
                e.sem_inc(q4_in[i], STEP_IN)
            e.wait_ge(zeroed, ZEROED)
            each_step(e, step)

        @block.vector
        def _(e):
            def low_tile(s, t):
                u = SL * s + t
                e.wait_ge(act_eh, u + 1)
                nc.vector.tensor_tensor(el[:, t % 4], ex[:, t % 2], f32(eh[:, t % 4]),
                                        ALU.subtract).then_inc(dve_el, 1)

            def max_tile(n, h, qt, bank):
                e.wait_ge(pe_mx, n + 1)
                nc.vector.tensor_reduce(negm[:, h % 2, qt, MR + 1:MR + 2], mx[:, bank], AX_X,
                                        ALU.max, negate=True).then_inc(dve_mx, 1)

            def stacked(b, g):
                if g < 0:
                    return STEP_IN * 2 * b + STEP_IN
                return STEP_IN * (2 * b + g // 2 + 1) + STEP_IN

            def step(b, g, proj):
                s = XG * b + g
                par = g % 2
                for t in range(SL + LAG):
                    if proj and t == 6:
                        e.wait_ge(pe_pj, 4 * s + 6)
                        if g == 0:
                            e.wait_ge(xc_in, 48 * b + 48)
                        e.wait_ge(act_ev, 4 * s + 2)
                        nc.vector.tensor_tensor(km[:, :], pj[:, 0], maskb[:, :], ALU.mult).then_inc(dve_ev, 1)
                    if 1 <= t <= SL:
                        low_tile(s, t - 1)
                    if proj and t == 4:
                        e.wait_ge(act_ev, 4 * s + 5)
                        e.wait_ge(q4_in[1 - par], stacked(b, g - 1))
                        nc.vector.tensor_tensor(ql[:, :], pj[:, 1], f32(qh[:, :]), ALU.subtract).then_inc(dve_ev, 1)
                    if proj and t == 8:
                        e.wait_ge(act_ev, 4 * s + 6)
                        e.wait_ge(k4_in[1 - par], stacked(b, g - 1))
                        nc.vector.tensor_tensor(kl[:, :], km[:, :], f32(kh[:, :]), ALU.subtract).then_inc(dve_ev, 1)
                    if proj and t == 12:
                        e.wait_ge(act_ev, 4 * s + 8)
                        nc.vector.tensor_tensor(vc[:, par, :, :, XD:2 * XD],
                                                pj[:, 0].rearrange("p (k h d) -> p k h d", h=HS, d=XD),
                                                f32(vc[:, par, :, :, 0:XD]), ALU.subtract).then_inc(dve_ev, 1)
                    if t < 8:
                        max_tile(16 * s + t, 2 + t // NT, t % NT, t % 2)
                    for v in CROSS_MAX_AT.get(t, ()) if proj else ():
                        max_tile(16 * s + 8 + v, v // NT, v % NT, v % 2)

            nc.vector.memset(f32(q4[:]), 0.0).then_inc(zeroed, 1)
            nc.vector.memset(f32(k4[:]), 0.0).then_inc(zeroed, 1)
            nc.vector.memset(f32(negm[:]), 0.0).then_inc(zeroed, 1)
            nc.vector.memset(f32(vc[:]), 1.0).then_inc(zeroed, 1)
            e.wait_ge(zeroed, 4)
            nc.vector.memset(f32(negm[:, :, :, MR:MR + 1]), 1.0).then_inc(zeroed, 1)
            nc.vector.memset(f32(q4[MR:MR + 1]), 1.0).then_inc(zeroed, 1)
            nc.vector.memset(f32(k4[MR:MR + 2]), 1.0).then_inc(zeroed, 1)
            for n in range(10):
                e.wait_ge(act_w, n + 1)
                nc.vector.tensor_tensor(w_lo[:, n], w_raw[:, n % 2], f32(w_hi[:, n]), ALU.subtract).then_inc(dve_w, 1)
            e.sem_inc(dve_ev, 4)
            e.sem_inc(dve_mx, 2)
            e.sem_inc(dve_el, 2)
            e.wait_ge(zeroed, ZEROED)
            each_step(e, step)

        @block.tensor
        def _(e):
            def projection(first, tiles, xx, g, bank):
                cols = slice(g * P, (g + 1) * P)
                for n, (w, part) in enumerate(((w_hi, 0), (w_lo, 0), (w_hi, 1))):
                    for k in range(tiles):
                        yield nc.tensor.matmul(pj[:, bank], w[:, first + k, cols], xx[:, part, k],
                                               start=(n == 0 and k == 0), stop=(n == 2 and k == tiles - 1))

            def scores(s, par, t):
                u = SL * s + t
                h, kt = t // NT, t % NT
                if kt == 0:
                    e.wait_ge(act_mr, 4 * s + (h - 1 if h >= 2 else 0) + 1)
                e.wait_ge(act_ex, u + 1)
                nc.tensor.matmul(st[:, t % 2], k4[0:MR + 2, par, h, kt * P:(kt + 1) * P],
                                 q4[0:MR + 2, par, h], start=True, stop=True).then_inc(pe_st, 1)

            def product(s, par, t):
                u = SL * s + t
                h, kt = t // NT, t % NT
                e.wait_ge(dve_el, u + 3)
                if kt == 0:
                    e.wait_ge(act_ov, 4 * s + h + 1)
                    e.wait_ge(dve_ev, 4 * s + 4)
                nc.tensor.matmul(ov[0:VW, :], vc[:, par, kt, h], eh[:, t % 4], start=(kt == 0), stop=False)
                nc.tensor.matmul(ov[0:VW, :], vc[:, par, kt, h], el[:, t % 4], start=False,
                                 stop=(kt == NT - 1)).then_inc(pe_av, 1)

            def max_scores(n, par, h, qt, bank):
                e.wait_ge(dve_mx, n + 1)
                nc.tensor.matmul(mx[:, bank], q4[0:MR + 1, par, h, qt * P:(qt + 1) * P],
                                 k4[0:MR + 1, par, h], start=True, stop=True).then_inc(pe_mx, 1)

            def max_row(h, maxima, rows):
                e.wait_ge(dve_mx, maxima)
                e.wait_ge(act_mr, rows)
                for t in range(NT):
                    last = nc.tensor.matmul(mr[:, t * P:(t + 1) * P], negm[:, h % 2, t], ident_r[:, :],
                                            start=True, stop=True)
                last.then_inc(pe_mr, 1)

            def step(b, g, proj):
                s = XG * b + g
                par = g % 2
                work = None
                for t in range(SL + LAG):
                    if proj and t in (0, 3, 6):
                        if t == 0:
                            if g == 0:
                                e.wait_ge(xq_in, 32 * b + 32)
                            e.wait_ge(act_ev, 4 * s + 3)
                            work = projection(2 * CK, DK, xq, g, 1)
                        elif t == 3:
                            if g == 0:
                                e.wait_ge(xc_in, 48 * b + 48)
                            e.wait_ge(dve_ev, 4 * s + 4)
                            work = projection(0, CK, xc, g, 0)
                        else:
                            e.wait_ge(dve_ev, 4 * s + 5)
                            work = projection(CK, CK, xc, g, 1)
                    if work is not None:
                        for _ in range(4 if t < 3 else 3):
                            last = next(work)
                        if t in (2, 5, 8):
                            last.then_inc(pe_pj, 1)
                            work = None
                    if t == 5:
                        max_row(2, 16 * s + 4 + 2, 4 * s + 1)
                    if t == 9:
                        max_row(3, 16 * s + 8 + 2, 4 * s + 2)
                    if t < SL:
                        scores(s, 1 - par, t)
                    if t >= LAG:
                        product(s, 1 - par, t - LAG)
                    if t < 8:
                        max_scores(16 * s + t, 1 - par, 2 + t // NT, t % NT, t % 2)
                    if not proj:
                        continue
                    if t == 10:
                        e.wait_ge(act_ev, 4 * s + 7)
                        e.wait_ge(dve_ev, 4 * s + 6)
                        for kt in range(NT):
                            last = nc.tensor.transpose(pj[:, 0, kt * P:(kt + 1) * P],
                                                       vt[:, kt * P:(kt + 1) * P], ident[:, :])
                        last.then_inc(pe_pj, 1)
                    if t == 12:
                        e.wait_ge(k4_in[par], STEP_IN * (2 * b + g // 2 + 1) + STEP_IN)
                        e.wait_ge(q4_in[par], STEP_IN * (2 * b + g // 2 + 1) + STEP_IN)
                        if g < 2:
                            e.wait_ge(mk_in[par], 64 * b + 64)
                    for v in CROSS_MAX_AT.get(t, ()):
                        max_scores(16 * s + 8 + v, par, v // NT, v % NT, v % 2)
                    if t == 16:
                        max_row(0, 16 * s + 12 + 2, 4 * s + 3)
                if proj:
                    max_row(1, 16 * s + 16 + 2, 4 * s + 4)

            e.sem_inc(pe_pj, 4)
            e.sem_inc(pe_av, 4)
            e.wait_ge(zeroed, ZEROED)
            e.wait_ge(dve_w, 10)
            each_step(e, step)


CROSS_MAX_AT = {12: (0,), 13: (1,), 14: (2,), 15: (3,), 16: (4, 5), 17: (6, 7)}


class Scale:

    def __init__(self, sp, name, columns):
        self.partial = sp.sb(f"{name}_max", [P, columns])
        self.name = name
        self.columns = columns
        self.row = sp.sb(f"{name}_row", [P, 1])
        self.all = sp.sb(f"{name}_all", [P, 1])
        self.scale = sp.sb(f"{name}_scale", [P, 1])
        self.inverse = sp.sb(f"{name}_inv", [P, 1])


def scale_stage(nc, sc):
    with ExitStack() as ctx:
        sp = Space(nc, ctx, f"{sc.name}_sc")
        dve = sp.sem("dve")
        pool = sp.sem("pool")
        block = ctx.enter_context(nc.Block())

        @block.vector
        def _(e):
            nc.vector.tensor_reduce(sc.row[:, :], sc.partial[:, :], AX_X, ALU.max).then_inc(dve, 1)
            e.wait_ge(pool, 1)
            nc.vector.tensor_scalar(sc.scale[:, :], sc.all[:, :], 1.0 / QMAX, 1e-12, ALU.mult, ALU.max).then_inc(dve, 1)
            e.wait_ge(dve, 2)
            nc.vector.reciprocal(sc.inverse[:, :], sc.scale[:, :]).then_inc(dve, 1)

        @block.gpsimd
        def _(e):
            e.wait_ge(dve, 1)
            nc.gpsimd.partition_all_reduce(sc.all[:, :], sc.row[:, :], P, RMAX).then_inc(pool, 1)


def quantise_input_stage(nc, env):
    xh, xl, sc = env["xq_hi"], env["xq_lo"], env["x_scale"]
    with ExitStack() as ctx:
        sp = Space(nc, ctx, "qx")
        raw = sp.sb("raw", [P, 2, DK, S])
        qi = sp.sb("qi", [P, 2, DK, S], I16)
        raw_in = [sp.sem(f"raw_in{i}") for i in range(2)]
        dve_q = sp.sem("dve_q")
        act_hi = sp.sem("act_hi")
        dve_lo = sp.sem("dve_lo")
        block = ctx.enter_context(nc.Block())

        @block.sync
        def _(e):
            with e.Fori(0, B // 2) as g2:
                for u in range(2):
                    g = 2 * g2 + u
                    e.wait_ge(dve_q, g + 1)
                    e.dma_start(raw[:, u], env["xn3"][:, :, bass.ds(g * S, S)]).then_inc(raw_in[u], 16)

        @block.vector
        def _(e):
            e.sem_inc(dve_q, 2)
            with e.Fori(0, B // 2) as g2:
                for u in range(2):
                    g = 2 * g2 + u
                    at = bass.ds(g * S, S)
                    e.wait_ge(raw_in[u], 16 * g2 + 16)
                    e.wait_ge(act_hi, g + 1)
                    nc.vector.tensor_scalar(qi[:, u], raw[:, u], sc.inverse[:, 0:1], None, ALU.mult).then_inc(dve_q, 1)
                    e.wait_ge(act_hi, g + 3)
                    nc.vector.tensor_tensor(xl[:, :, at], qi[:, u], f32(xh[:, :, at]), ALU.subtract).then_inc(dve_lo, 1)

        @block.scalar
        def _(e):
            e.sem_inc(act_hi, 2)
            with e.Fori(0, B // 2) as g2:
                for u in range(2):
                    g = 2 * g2 + u
                    e.wait_ge(dve_q, g + 3)
                    nc.scalar.activation(xh[:, :, bass.ds(g * S, S)], qi[:, u], ACT.Copy).then_inc(act_hi, 1)


class Dequant:
    STEPS = 6

    def __init__(self, nc, sp, width, done):
        self.nc, self.done, self.blocks = nc, done, width // BLK
        self.s = sp.sb("blk_s", [P, 2, self.blocks])
        self.inv = sp.sb("blk_inv", [P, self.blocks])
        self.q = sp.sb("wq", [P, width], I16)
        self.clip = sp.sb("wclip", [P, width])

    def tile(self, e, w, out, par, base):
        nc, done = self.nc, self.done
        cut = lambda ap: ap.rearrange("p (b k) -> p b k", k=BLK)
        wide = lambda ap: ap.unsqueeze(2).to_broadcast([P, self.blocks, BLK])
        s = self.s[:, par]
        nc.vector.tensor_reduce(s, cut(w), AX_X, ALU.max, apply_absolute_value=True).then_inc(done, 1)
        e.wait_ge(done, base + 1)
        nc.vector.tensor_scalar(s, s, 1.0 / WQMAX, 1e-12, ALU.mult, ALU.max).then_inc(done, 1)
        e.wait_ge(done, base + 2)
        nc.vector.reciprocal(self.inv[:, :], s).then_inc(done, 1)
        e.wait_ge(done, base + 3)
        nc.vector.tensor_tensor(cut(self.q[:, :]), cut(w), wide(self.inv[:, :]), ALU.mult).then_inc(done, 1)
        e.wait_ge(done, base + 4)
        nc.vector.tensor_scalar(self.clip[:, :], self.q[:, :], -WQMAX - 1.0, WQMAX, ALU.max, ALU.min).then_inc(done, 1)
        e.wait_ge(done, base + 5)
        nc.vector.tensor_tensor(cut(out), cut(self.clip[:, :]), wide(s), ALU.mult).then_inc(done, 1)


def gate_up_stage(nc, env, name):
    xh, xl, ident = env["xq_hi"], env["xq_lo"], env["ident"]
    xsc, out_sc = env["x_scale"], env[f"{name}_scale"]
    dst = env[name]
    w = env[f"w_{name}"].rearrange("(j p) h -> j p h", p=P)
    side = name == "up"
    gsc, ssc = env["gate_scale"], env["silu_scale"]
    HALF = HB * S
    W2 = 2 * S
    PIECES = T // W2
    BANKS = 4
    with ExitStack() as ctx:
        sp = Space(nc, ctx, name)
        w_raw = sp.sb("w_raw", [P, 2, D])
        wd = sp.sb("wd", [P, 2, D])
        w_hi = sp.sb("w_hi", [P, 2, DK, P], F32R)
        w_lo = sp.sb("w_lo", [P, 2, DK, P], F32R)
        ev = sp.sb("ev", [P, 2, HALF])
        acc = sp.ps("acc", [P, BANKS, S])
        pt = sp.ps("pt", [P, 2, DK, P])
        w_in = [sp.sem(f"w_in{i}") for i in range(2)]
        passed = sp.sem("passed")
        dve_q = sp.sem("dve_q")
        pe_tr = sp.sem("pe_tr")
        act_wh = sp.sem("act_wh")
        dve_wl = sp.sem("dve_wl")
        pe_acc = sp.sem("pe_acc")
        act_ev = sp.sem("act_ev")
        dve_mx = sp.sem("dve_mx")
        out = [sp.sem(f"out{i}") for i in range(2)]
        deq = Dequant(nc, sp, D, dve_q)
        if side:
            g_buf = sp.sb("g", [P, PIECES, W2])
            gq = sp.sb("gq", [P, 2, W2], I16)
            sg = sp.sb("sg", [P, W2])
            sq = sp.sb("sq", [P, W2], U16)
            c1 = sp.sb("c1", [P, 1])
            g_in = [sp.sem(f"g_in{i}") for i in range(PIECES)]
            c_done = sp.sem("c_done")
            dve_gq = sp.sem("dve_gq")
            act_sg = sp.sem("act_sg")
            dve_sq = sp.sem("dve_sq")
            dve_gs = sp.sem("dve_gs")
            dve_sm = sp.sem("dve_sm")
            g_out = [sp.sem(f"g_out{i}") for i in range(PIECES)]
        block = ctx.enter_context(nc.Block())

        def gate_at(j, n):
            return env["gate"][j, :, n * W2:(n + 1) * W2]

        @block.sync
        def _(e):
            def load_weights(j, u):
                e.dma_start(w_raw[:, u], w[j % FT]).then_inc(w_in[u], 16)

            load_weights(0, 0)
            load_weights(1, 1)
            if side:
                for n in range(2):
                    e.dma_start(g_buf[:, n], gate_at(0, n)).then_inc(g_in[n], 16)
            with e.Fori(0, FT // 2) as j2:
                for u in range(2):
                    j = 2 * j2 + u
                    nj = (j + 2) % FT
                    e.wait_ge(dve_q, deq.STEPS * j + deq.STEPS)
                    e.dma_start(w_raw[:, u], w[nj]).then_inc(w_in[u], 16)
                    for n in range(PIECES):
                        if side:
                            ahead, jn = (n + 2) % PIECES, j + (n + 2) // PIECES
                            load_j = jn % FT
                            e.wait_ge(g_out[ahead], 16 * jn + 16)
                            e.dma_start(g_buf[:, ahead], gate_at(load_j, ahead)).then_inc(g_in[ahead], 16)
                            e.wait_ge(dve_sm, PIECES * j + n + 1)
                            e.sem_inc(passed, 1)
                            e.dma_start(gate_at(j, n), g_buf[:, n]).then_inc(g_out[n], 16)
                        if n % 2:
                            h = n // 2
                            e.wait_ge(act_ev, B * j + HB * (h + 1) + BANKS)
                            e.dma_start(dst[j, :, h * HALF:(h + 1) * HALF], ev[:, h]).then_inc(out[h], 16)
            for h in range(2):
                e.wait_ge(out[h], 16 * FT + 16)
                e.wait_ge(w_in[h], 16 * (FT // 2) + 16)
            if side:
                for n in range(PIECES):
                    e.wait_ge(g_out[n], 16 * FT + 16)
                    e.wait_ge(g_in[n], 16 * FT + (16 if n < 2 else 0))

        @block.tensor
        def _(e):
            def transposes(n, u):
                e.wait_ge(dve_q, deq.STEPS * n + deq.STEPS)
                for k in range(DK):
                    last = nc.tensor.transpose(pt[:, u, k], wd[:, u, k * P:(k + 1) * P], ident[:, :])
                last.then_inc(pe_tr, 1)

            transposes(0, 0)
            with e.Fori(0, FT // 2) as j2:
                for u in range(2):
                    j = 2 * j2 + u
                    e.wait_ge(dve_wl, j + 1)
                    e.wait_ge(act_wh, j + 1)
                    for b in range(B):
                        if b == 5:
                            transposes(j + 1, 1 - u)
                        bank = b % BANKS
                        e.wait_ge(act_ev, B * j + b + 1)
                        for n, (ww, xx) in enumerate(((w_hi, xh), (w_lo, xh), (w_hi, xl))):
                            for k in range(DK):
                                last = nc.tensor.matmul(acc[:, bank], ww[:, u, k], xx[:, k, b * S:(b + 1) * S],
                                                        start=(n == 0 and k == 0), stop=(n == 2 and k == DK - 1))
                        last.then_inc(pe_acc, 1)

        @block.scalar
        def _(e):
            def high(n, u):
                e.wait_ge(pe_tr, n + 1)
                nc.scalar.activation(w_hi[:, u], pt[:, u], ACT.Copy).then_inc(act_wh, 1)

            e.sem_inc(act_ev, BANKS)
            for h in range(2):
                e.sem_inc(out[h], 16)
            if side:
                for n in range(PIECES):
                    e.sem_inc(g_out[n], 16)
            high(0, 0)
            with e.Fori(0, FT // 2) as j2:
                for u in range(2):
                    j = 2 * j2 + u
                    for b in range(B):
                        h, c = b // HB, b % HB
                        bank = b % BANKS
                        if c == 0:
                            e.wait_ge(out[h], 16 * j + 16)
                            e.wait_ge(dve_mx, 2 * j + h + 1)
                        e.wait_ge(pe_acc, B * j + b + 1)
                        nc.scalar.activation(ev[:, h, c * S:(c + 1) * S], acc[:, bank], ACT.Copy,
                                             scale=xsc.scale[:, 0:1]).then_inc(act_ev, 1)
                        if b == 5:
                            high(j + 1, 1 - u)
                        if side and b % 2:
                            n = b // 2
                            e.wait_ge(dve_gq, PIECES * j + n + 1)
                            e.wait_ge(dve_sq, PIECES * j + n + 1)
                            nc.scalar.activation(sg[:, :], gq[:, n % 2], ACT.Sigmoid,
                                                 scale=gsc.scale[:, 0:1]).then_inc(act_sg, 1)

        @block.vector
        def _(e):
            def low(n, u):
                e.wait_ge(act_wh, n + 1)
                nc.vector.tensor_tensor(w_lo[:, u], pt[:, u], f32(w_hi[:, u]), ALU.subtract).then_inc(dve_wl, 1)

            def quantise_gate(j, n):
                e.wait_ge(g_in[n], 16 * j + 16)
                nc.vector.tensor_scalar(gq[:, n % 2], g_buf[:, n], gsc.inverse[:, 0:1], None,
                                        ALU.mult).then_inc(dve_gq, 1)

            def silu(j, n):
                m = PIECES * j + n
                e.wait_ge(act_sg, m + 1)
                nc.vector.tensor_scalar(sq[:, :], sg[:, :], 65536.0, None, ALU.mult).then_inc(dve_sq, 1)
                e.wait_ge(dve_sq, m + 2)
                nc.vector.scalar_tensor_tensor(g_buf[:, n], sq[:, :], c1[:, 0:1], gq[:, n % 2],
                                               ALU.mult, ALU.mult).then_inc(dve_gs, 1)
                e.wait_ge(dve_gs, m + 1)
                nc.vector.tensor_reduce(ssc.partial[:, bass.ds(m, 1)], g_buf[:, n], AX_X, ALU.max,
                                        apply_absolute_value=True).then_inc(dve_sm, 1)

            def maxima(j, h):
                e.wait_ge(act_ev, B * j + HB * (h + 1) + BANKS)
                nc.vector.tensor_reduce(out_sc.partial[:, bass.ds(2 * j + h, 1)], ev[:, h], AX_X, ALU.max,
                                        apply_absolute_value=True).then_inc(dve_mx, 1)

            e.sem_inc(dve_mx, 2)
            if side:
                e.sem_inc(dve_sq, 1)
                nc.vector.tensor_scalar(c1[:, :], gsc.scale[:, :], 1.0 / 65536.0, None, ALU.mult).then_inc(c_done, 1)
                e.wait_ge(c_done, 1)
            e.wait_ge(w_in[0], 16)
            deq.tile(e, w_raw[:, 0], wd[:, 0], 0, 0)
            low(0, 0)
            with e.Fori(0, FT // 2) as j2:
                for u in range(2):
                    j = 2 * j2 + u
                    e.wait_ge(w_in[1 - u], 16 * j2 + 16 + 16 * u)
                    e.wait_ge(pe_tr, j + 1)
                    deq.tile(e, w_raw[:, 1 - u], wd[:, 1 - u], 1 - u, deq.STEPS * (j + 1))
                    if side:
                        quantise_gate(j, 0)
                        quantise_gate(j, 1)
                        silu(j, 0)
                        quantise_gate(j, 2)
                        silu(j, 1)
                    maxima(j, 0)
                    low(j + 1, 1 - u)
                    if side:
                        quantise_gate(j, 3)
                        silu(j, 2)
                        silu(j, 3)
                    maxima(j, 1)


def multiply_stage(nc, env):
    ssc, usc, osc = env["silu_scale"], env["up_scale"], env["prod_scale"]
    W = 2 * S
    PIECES = T // W
    with ExitStack() as ctx:
        sp = Space(nc, ctx, "mul")
        a = sp.sb("a", [P, PIECES, W])
        b = sp.sb("b", [P, PIECES, W])
        aq = sp.sb("aq", [P, PIECES, W], I16)
        bq = sp.sb("bq", [P, PIECES, W], I16)
        c2 = sp.sb("c2", [P, 1])
        ab_in = [sp.sem(f"ab_in{i}") for i in range(PIECES)]
        passed = sp.sem("passed")
        c_done = sp.sem("c_done")
        act_q = sp.sem("act_q")
        dve_o = sp.sem("dve_o")
        dve_mx = sp.sem("dve_mx")
        out = [sp.sem(f"out{i}") for i in range(PIECES)]
        block = ctx.enter_context(nc.Block())

        @block.sync
        def _(e):
            def load(j, n):
                at = slice(n * W, (n + 1) * W)
                e.dma_start(a[:, n], env["gate"][j, :, at]).then_inc(ab_in[n], 16)
                e.dma_start(b[:, n], env["up"][j, :, at]).then_inc(ab_in[n], 16)

            load(0, 0)
            load(0, 1)
            with e.Fori(0, FT) as j:
                for n in range(PIECES):
                    ahead, jn = (n + 2) % PIECES, j + (n + 2) // PIECES
                    load_j = jn % FT
                    e.wait_ge(out[ahead], 16 * jn + 16)
                    load(load_j, ahead)
                    e.wait_ge(dve_mx, PIECES * j + n + 1)
                    e.sem_inc(passed, 1)
                    e.dma_start(env["gate"][j, :, n * W:(n + 1) * W], a[:, n]).then_inc(out[n], 16)
            for n in range(PIECES):
                e.wait_ge(out[n], 16 * FT + 16)
                e.wait_ge(ab_in[n], 32 * FT + (32 if n < 2 else 0))

        @block.scalar
        def _(e):
            for n in range(PIECES):
                e.sem_inc(out[n], 16)
            with e.Fori(0, FT) as j:
                for n in range(PIECES):
                    e.wait_ge(ab_in[n], 32 * j + 32)
                    nc.scalar.activation(aq[:, n], a[:, n], ACT.Copy, scale=ssc.inverse[:, 0:1]).then_inc(act_q, 1)
                    nc.scalar.activation(bq[:, n], b[:, n], ACT.Copy, scale=usc.inverse[:, 0:1]).then_inc(act_q, 1)

        @block.vector
        def _(e):
            nc.vector.tensor_tensor(c2[:, :], ssc.scale[:, :], usc.scale[:, :], ALU.mult).then_inc(c_done, 1)
            e.wait_ge(c_done, 1)
            with e.Fori(0, FT) as j:
                for n in range(PIECES):
                    m = PIECES * j + n
                    e.wait_ge(act_q, 2 * m + 2)
                    nc.vector.scalar_tensor_tensor(a[:, n], aq[:, n], c2[:, 0:1], bq[:, n],
                                                   ALU.mult, ALU.mult).then_inc(dve_o, 1)
                    e.wait_ge(dve_o, m + 1)
                    nc.vector.tensor_reduce(osc.partial[:, bass.ds(m, 1)], a[:, n], AX_X, ALU.max,
                                            apply_absolute_value=True).then_inc(dve_mx, 1)


def down_stage(nc, env):
    ident, osc = env["ident"], env["prod_scale"]
    HT = D // P
    RING = 4
    src = env["gate"]
    w = env["w_down"].rearrange("(j p) i -> j p i", p=P)
    x2 = env["x2"].rearrange("(g n p) d -> g p n d", n=NT, p=P)
    y = env["out"].rearrange("(g n p) d -> g p n d", n=NT, p=P)
    with ExitStack() as ctx:
        sp = Space(nc, ctx, "dn")
        w_raw = sp.sb("w_raw", [P, FF])
        wd = sp.sb("wd", [P, 2, FF])
        w_hi = sp.sb("w_hi", [P, FT, D], F32R)
        w_lo = sp.sb("w_lo", [P, FT, D], F32R)
        o = sp.sb("o", [P, RING, S])
        oq = sp.sb("oq", [P, RING, S], I16)
        oh = sp.sb("oh", [P, RING, S], F32R)
        ol = sp.sb("ol", [P, RING, S], F32R)
        xb = sp.sb("xb", [P, 2, NT, D])
        acc = sp.ps("acc", [P, 2, NT, D])
        w_in = sp.sem("w_in")
        dve_q = sp.sem("dve_q")
        pe_tr = sp.sem("pe_tr")
        act_wh = sp.sem("act_wh")
        dve_wl = sp.sem("dve_wl")
        o_in = [sp.sem(f"o_in{i}") for i in range(RING)]
        dve_oq = sp.sem("dve_oq")
        act_oh = sp.sem("act_oh")
        dve_ol = sp.sem("dve_ol")
        pe_ck = sp.sem("pe_ck")
        x_in = [sp.sem(f"x_in{i}") for i in range(2)]
        dve_y = sp.sem("dve_y")
        y_out = [sp.sem(f"y_out{i}") for i in range(2)]
        deq = Dequant(nc, sp, FF, dve_q)
        QUADS = FT // 4
        block = ctx.enter_context(nc.Block())

        @block.sync
        def _(e):
            for j in range(HT):
                if j:
                    e.wait_ge(dve_q, deq.STEPS * j)
                e.dma_start(w_raw[:, :], w[j]).then_inc(w_in, 16)
            with e.Fori(0, B // 2) as g2:
                for u in range(2):
                    g = 2 * g2 + u
                    for k in range(FT):
                        c = k % RING
                        e.wait_ge(dve_oq, FT * g + k + 1)
                        e.dma_start(o[:, c], src[k, :, bass.ds(g * S, S)]).then_inc(o_in[c], 16)
                        if k == 0:
                            e.wait_ge(y_out[u], 16 * g2 + 16)
                            e.dma_start(xb[:, u], x2[g]).then_inc(x_in[u], 16)

        @block.scalar
        def _(e):
            e.sem_inc(y_out[0], 16)
            e.sem_inc(y_out[1], 16)
            e.sem_inc(act_oh, RING)
            for j in range(HT):
                for q in range(QUADS):
                    n = QUADS * j + q
                    e.wait_ge(pe_tr, n + 1)
                    nc.scalar.activation(w_hi[:, 4 * q:4 * q + 4, j * P:(j + 1) * P],
                                         acc[:, n % 2, 0].rearrange("p (k o) -> p k o", o=P),
                                         ACT.Copy).then_inc(act_wh, 1)
            with e.Fori(0, B // 2) as g2:
                for u in range(2):
                    g = 2 * g2 + u
                    for k in range(FT):
                        c = k % RING
                        e.wait_ge(dve_oq, FT * g + k + 1 + RING)
                        e.wait_ge(pe_ck, FT * g + k + 1)
                        nc.scalar.activation(oh[:, c], oq[:, c], ACT.Copy).then_inc(act_oh, 1)
                    e.wait_ge(dve_y, g + 3)
                    e.dma_start(y[g], xb[:, u]).then_inc(y_out[u], 16)
            for u in range(2):
                e.wait_ge(y_out[u], 16 * (B // 2) + 16)

        @block.vector
        def _(e):
            for j in range(HT):
                e.wait_ge(w_in, 16 * j + 16)
                if j >= 2:
                    e.wait_ge(pe_tr, QUADS * (j - 1))
                deq.tile(e, w_raw[:, :], wd[:, j % 2], j % 2, deq.STEPS * j)
                for q in range(QUADS):
                    n = QUADS * j + q
                    e.wait_ge(act_wh, n + 1)
                    cols = (slice(None), slice(4 * q, 4 * q + 4), slice(j * P, (j + 1) * P))
                    nc.vector.tensor_tensor(w_lo[cols], acc[:, n % 2, 0].rearrange("p (k o) -> p k o", o=P),
                                            f32(w_hi[cols]), ALU.subtract).then_inc(dve_wl, 1)
            e.sem_inc(dve_oq, RING)
            e.sem_inc(dve_y, 2)
            with e.Fori(0, B // 2) as g2:
                for u in range(2):
                    g = 2 * g2 + u

                    def quantise(k):
                        c = k % RING
                        e.wait_ge(o_in[c], 16 * (FT // RING) * g + 16 * (k // RING) + 16)
                        e.wait_ge(act_oh, FT * g + k + 1)
                        nc.vector.tensor_scalar(oq[:, c], o[:, c], osc.inverse[:, 0:1], None,
                                                ALU.mult).then_inc(dve_oq, 1)

                    def low(k):
                        c = k % RING
                        e.wait_ge(act_oh, FT * g + k + 1 + RING)
                        nc.vector.tensor_tensor(ol[:, c], oq[:, c], f32(oh[:, c]), ALU.subtract).then_inc(dve_ol, 1)

                    for k in range(FT):
                        quantise(k)
                        if k:
                            low(k - 1)
                    low(FT - 1)
                    e.wait_ge(pe_ck, FT * g + FT + RING)
                    e.wait_ge(x_in[u], 16 * g2 + 16)
                    nc.vector.scalar_tensor_tensor(xb[:, u], acc[:, u], osc.scale[:, 0:1], xb[:, u],
                                                   ALU.mult, ALU.add).then_inc(dve_y, 1)

        @block.tensor
        def _(e):
            for j in range(HT):
                e.wait_ge(dve_q, deq.STEPS * j + deq.STEPS)
                for q in range(QUADS):
                    n = QUADS * j + q
                    if n >= 2:
                        e.wait_ge(dve_wl, n - 1)
                    for k in range(4):
                        i = 4 * q + k
                        last = nc.tensor.transpose(acc[:, n % 2, 0, k * P:(k + 1) * P],
                                                   wd[:, j % 2, i * P:(i + 1) * P], ident[:, :])
                    last.then_inc(pe_tr, 1)
            e.wait_ge(dve_wl, QUADS * HT)
            e.sem_inc(pe_ck, RING)
            with e.Fori(0, B // 2) as g2:
                for u in range(2):
                    g = 2 * g2 + u
                    e.wait_ge(dve_y, g + 1)
                    for k in range(FT):
                        c = k % RING
                        e.wait_ge(dve_ol, FT * g + k + 1)
                        for t in range(NT):
                            cols = slice(t * P, (t + 1) * P)
                            start, stop = k == 0, k == FT - 1
                            nc.tensor.matmul(acc[:, u, t], oh[:, c, cols], w_hi[:, k], start=start, stop=False)
                            nc.tensor.matmul(acc[:, u, t], oh[:, c, cols], w_lo[:, k], start=False, stop=False)
                            last = nc.tensor.matmul(acc[:, u, t], ol[:, c, cols], w_hi[:, k], start=False, stop=stop)
                        last.then_inc(pe_ck, 1)


def setup_stage(nc, env, ctx):
    sp = Space(nc, ctx, "top")
    env["ident"] = ident = sp.sb("ident", [P, P])
    env["ident_r"] = ident_r = sp.sb("ident_r", [P, P], F32R)
    env["minus_half"] = mhalf = sp.sb("minus_half", [P, 8])
    for name, columns in (("x", T // P), ("gate", 2 * FT), ("up", 2 * FT), ("silu", 4 * FT), ("prod", 4 * FT)):
        env[f"{name}_scale"] = Scale(sp, name, columns)
    env["xn3_max"] = env["x_scale"].partial
    made = sp.sem("made")
    with nc.Block() as block:
        @block.gpsimd
        def _(e):
            nc.gpsimd.memset(ident[:, :], 0.0).then_inc(made, 1)
            nc.gpsimd.memset(mhalf[:, :], -0.5).then_inc(made, 1)
            e.wait_ge(made, 2)
            nc.gpsimd.affine_select(out=ident[:, :], in_=ident[:, :], compare_op=ALU.not_equal, fill=1.0,
                                    base=0, pattern=[[-1, P]], channel_multiplier=1).then_inc(made, 1)

        @block.vector
        def _(e):
            e.wait_ge(made, 3)
            nc.vector.tensor_copy(ident_r[:, :], ident[:, :]).then_inc(made, 1)


def feed_forward(nc, env):
    scale_stage(nc, env["x_scale"])
    with ExitStack() as ctx:
        for part in ("hi", "lo"):
            env[f"xq_{part}"] = ctx.enter_context(nc.sbuf_tensor(f"xq_{part}", [P, DK, T], F32R))
        quantise_input_stage(nc, env)
        gate_up_stage(nc, env, "gate")
        scale_stage(nc, env["gate_scale"])
        gate_up_stage(nc, env, "up")
    scale_stage(nc, env["silu_scale"])
    scale_stage(nc, env["up_scale"])
    multiply_stage(nc, env)
    scale_stage(nc, env["prod_scale"])
    down_stage(nc, env)


_INS = ["x", "ctx_768", "mask_BxS2_bf1", "L0_attn_Wq", "L0_attn_bq", "L0_attn_Wk", "L0_attn_bk", "L0_attn_Wv",
        "L0_attn_bv", "L0_attn_Wo", "L0_attn_bo", "L0_xattn_Wq", "L0_xattn_Wk", "L0_xattn_Wv", "L0_xattn_Wo",
        "L0_ffn_w_gate", "L0_ffn_w_up", "L0_ffn_w_down"]
_ENV = ["x", "ctx", "mask", "Wq", "bq", "Wk", "bk", "Wv", "bv", "Wo", "bo", "Wq2", "Wk2", "Wv2", "Wo2",
        "w_gate", "w_up", "w_down"]


def decoder_layer(nc, args, out):
    env = dict(zip(_ENV, args))
    env["x"] = env["x"].rearrange("b s d -> (b s) d")
    env["ctx"] = env["ctx"].rearrange("b s d -> (b s) d")
    env["out"] = out.rearrange("b s d -> (b s) d")
    for name, shape in (("o_raw", [HP + 1, P, T]), ("o_sum", [HP + 1, 2, T]), ("o_rcp", [HP, 2, T]),
                        ("x1", [T, D]), ("xn2_hi", [P, DK, T]), ("xn2_lo", [P, DK, T]),
                        ("ct_hi", [P, CK, T]), ("ct_lo", [P, CK, T]), ("mask_f", [B, S]), ("mask_n", [B, S]),
                        ("c_raw", [XG, NH // XG, 2 * XD + 1, T + S]), ("c_rcp", [XG, NH // XG, T]),
                        ("x2", [T, D]), ("xn3", [P, DK, T]), ("gate", [FT, P, T]), ("up", [FT, P, T])):
        env[name] = nc.dram_tensor(name, shape, F32, kind="Internal").ap()
    with ExitStack() as ctx:
        setup_stage(nc, env, ctx)
        context_stage(nc, env)
        for half in range(2):
            with ExitStack() as inner:
                for part in ("hi", "lo"):
                    env[f"xt_{part}"] = inner.enter_context(
                        nc.sbuf_tensor(f"xt_{part}{half}", [P, DK, HTOK], F32R))
                layernorm_stage(nc, env, half)
                self_attention_stage(nc, env, half)
        reciprocal_stage(nc, env, "o")
        output_stage(nc, env, "o")
        cross_attention_stage(nc, env)
        reciprocal_stage(nc, env, "c")
        output_stage(nc, env, "c")
        feed_forward(nc, env)


def kernel(**inputs):
    import numpy as _np
    import concourse.bacc as _bacc
    from concourse import mybir as _mybir
    from concourse.bass_utils import run_bass_kernel_spmd as _run

    nc = _bacc.Bacc("TRN2", target_bir_lowering=False, num_devices=1)
    arrays, args = {}, []
    for name in _INS:
        a = _np.ascontiguousarray(inputs[name])
        if a.dtype == _np.bool_:
            a = a.view(_np.uint8)
        arrays[f"in_{name}_dram"] = a
        args.append(nc.dram_tensor(f"in_{name}_dram", a.shape, _mybir.dt.from_np(a.dtype), kind="ExternalInput").ap())
    out = nc.dram_tensor("out_0_dram", (B, S, D), _mybir.dt.from_np(_np.dtype("float32")), kind="ExternalOutput").ap()
    decoder_layer(nc, args, out)
    r = _run(nc, [arrays], core_ids=[0])
    return r.results[0]["out_0_dram"]
```

```python
from contextlib import ExitStack

import concourse.bass as bass
from concourse import mybir

F32 = mybir.dt.float32
F32R = mybir.dt.float32r
I16 = mybir.dt.int16
U16 = mybir.dt.uint16
U8 = mybir.dt.uint8
ALU = mybir.AluOpType
ACT = mybir.ActivationFunctionType
AX_X = mybir.AxisListType.X
AX_XY = mybir.AxisListType.XY
RMAX = bass.bass_isa.ReduceOp.max

P = 128
B, S, D, CD = 8, 512, 512, 384
T = B * S
DK = D // P
CK = CD // P
NT = S // P
NH = 16
HB = B // 2
HTOK = HB * S
HD = 64
HP = NH // 2
XD = D // NH
XG = D // P
FF = 1536
FT = FF // P
CTX_TILES = D // P
BLK = 32
EPS = 1e-5
QMAX = 32767.0
WQMAX = 7.0
ZEROED = 7
BIG = float(2.0 ** 100)


class Space:

    def __init__(self, nc, ctx, tag):
        self.nc, self.ctx, self.tag, self.sems = nc, ctx, tag, []
        ctx.callback(self.clear)

    def sb(self, name, shape, dt=F32):
        return self.ctx.enter_context(self.nc.sbuf_tensor(f"{self.tag}_{name}", shape, dt))

    def ps(self, name, shape, dt=F32):
        return self.ctx.enter_context(self.nc.psum_tensor(f"{self.tag}_{name}", shape, dt))

    def sem(self, name):
        self.sems.append(self.nc.alloc_semaphore(f"{self.tag}_{name}"))
        return self.sems[-1]

    def clear(self):
        self.nc.clear_and_free_semaphores(self.sems)
        self.nc.all_engine_barrier()


def f32(ap):
    return ap.bitcast(F32)


def layernorm_stage(nc, env, half):
    xh, xl, ident, mhalf = env["xt_hi"], env["xt_lo"], env["ident"], env["minus_half"]
    x = env["x"]
    with ExitStack() as ctx:
        sp = Space(nc, ctx, f"ln{half}")
        xt = sp.sb("x", [P, 2, NT, D])
        xn = sp.sb("xn", [P, NT, D])
        stats = sp.sb("stats", [P, NT, 6])
        mv = sp.sb("mv", [P, NT, 2])
        ve = sp.sb("ve", [P, NT])
        rstd = sp.sb("rstd", [P, NT])
        pt = sp.ps("pt", [P, NT, DK, P])
        x_in = [sp.sem(f"x_in{i}") for i in range(2)]
        passed = sp.sem("passed")
        dve_st = sp.sem("dve_st")
        pool_rs = sp.sem("pool_rs")
        dve_xn = sp.sem("dve_xn")
        pe_tr = sp.sem("pe_tr")
        act_hi = sp.sem("act_hi")
        dve_lo = sp.sem("dve_lo")
        xs = x.rearrange("(g n p) d -> g p n d", n=NT, p=P)
        block = ctx.enter_context(nc.Block())

        @block.sync
        def _(e):
            with e.Fori(0, HB // 2) as g2:
                for u in range(2):
                    e.wait_ge(dve_xn, 8 * g2 + 4 * u + 4)
                    e.dma_start(xt[:, u], xs[half * HB + 2 * g2 + u]).then_inc(x_in[u], 16)

        @block.vector
        def _(e):
            e.sem_inc(dve_xn, 8)
            e.sem_inc(dve_lo, 4)
            with e.Fori(0, HB // 2) as g2:
                for u in range(2):
                    g = 2 * g2 + u
                    e.wait_ge(x_in[u], 16 * g2 + 16)
                    for t in range(NT):
                        nc.vector.bn_stats(stats[:, t], xt[:, u, t]).then_inc(dve_st, 1)
                    for t in range(NT):
                        e.wait_ge(dve_st, 9 * g + t + 1)
                        e.sem_inc(passed, 1)
                        nc.vector.bn_aggr(mv[:, t], stats[:, t]).then_inc(dve_st, 1)
                    e.wait_ge(dve_st, 9 * g + 8)
                    nc.vector.tensor_scalar(ve[:, :], mv[:, :, 1], EPS, None, ALU.add).then_inc(dve_st, 1)
                    e.wait_ge(pool_rs, g + 1)
                    for t in range(NT):
                        e.wait_ge(pe_tr, 4 * g + t + 1)
                        nc.vector.tensor_scalar(xn[:, t], xt[:, u, t], mv[:, t, 0:1], rstd[:, t:t + 1],
                                                ALU.subtract, ALU.mult).then_inc(dve_xn, 1)
                    for t in range(NT):
                        e.wait_ge(act_hi, 4 * g + t + 5)
                        at = bass.ds(g * S + t * P, P)
                        nc.vector.tensor_tensor(xl[:, :, at], pt[:, t], f32(xh[:, :, at]),
                                                ALU.subtract).then_inc(dve_lo, 1)

        @block.gpsimd
        def _(e):
            with e.Fori(0, HB) as g:
                e.wait_ge(dve_st, 9 * g + 9)
                nc.gpsimd.tensor_tensor(rstd[:, :], ve[:, :], mhalf[:, 0:NT], ALU.pow).then_inc(pool_rs, 1)

        @block.tensor
        def _(e):
            e.sem_inc(pe_tr, 4)
            with e.Fori(0, HB) as g:
                for t in range(NT):
                    e.wait_ge(dve_xn, 4 * g + t + 9)
                    e.wait_ge(dve_lo, 4 * g + t + 1)
                    for k in range(DK):
                        last = nc.tensor.transpose(pt[:, t, k], xn[:, t, k * P:(k + 1) * P], ident[:, :])
                    last.then_inc(pe_tr, 1)

        @block.scalar
        def _(e):
            e.sem_inc(act_hi, 4)
            with e.Fori(0, HB) as g:
                for t in range(NT):
                    e.wait_ge(pe_tr, 4 * g + t + 5)
                    at = bass.ds(g * S + t * P, P)
                    nc.scalar.activation(xh[:, :, at], pt[:, t], ACT.Copy).then_inc(act_hi, 1)


def self_attention_stage(nc, env, half):
    xh, xl, ident, ident_r = env["xt_hi"], env["xt_lo"], env["ident"], env["ident_r"]
    o_raw, o_sum = env["o_raw"], env["o_sum"]
    weights = [env[n].rearrange("(k p) (m n) -> m p k n", p=P, n=P) for n in ("Wq", "Wk", "Wv")]
    biases = [env[n].rearrange("(m p o) -> m p o", p=P, o=1) for n in ("bq", "bk", "bv")]
    SCALE = HD ** -0.5
    LAG = 3
    own = (slice(0, HD), slice(HD, P))
    other = (slice(HD, P), slice(0, HD))
    mrow = (HD, 0)

    with ExitStack() as ctx:
        sp = Space(nc, ctx, f"sa{half}")
        w_raw = sp.sb("w_raw", [P, 3, DK, P])
        b_raw = sp.sb("b_raw", [P, 4])
        w_hi = sp.sb("w_hi", [P, 2, 3, DK, P], F32R)
        w_lo = sp.sb("w_lo", [P, 2, 3, DK, P], F32R)
        bias = sp.sb("bias", [P, 2, 4])
        qa = sp.sb("qa", [P, 2, 2, S], F32R)
        qb = sp.sb("qb", [P, 2, 2, S], F32R)
        ka = sp.sb("ka", [P, 2, 2, S], F32R)
        kb = sp.sb("kb", [P, 2, 2, S], F32R)
        vt = sp.sb("vt", [P, S])
        va = sp.sb("va", [P, 2, NT, 3, HD], F32R)
        vb = sp.sb("vb", [P, 2, NT, 3, HD], F32R)
        ex = sp.sb("ex", [P, 2, S])
        eh = sp.sb("eh", [P, 4, S], F32R)
        el = sp.sb("el", [P, 4, S], F32R)
        negm = sp.sb("negm", [P, 2, NT, P], F32R)
        osb = sp.sb("osb", [P, 2, S])
        pj = sp.ps("pj", [P, 2, S])
        st = sp.ps("st", [P, 2, S])
        mx = sp.ps("mx", [P, 2, S])
        ov = sp.ps("ov", [P, S])
        mr = sp.ps("mr", [P, S])

        w_in = sp.sem("w_in")
        w_split = sp.sem("w_split")
        act_w = sp.sem("act_w")
        pe_pj = sp.sem("pe_pj")
        act_ev = sp.sem("act_ev")
        dve_ev = sp.sem("dve_ev")
        pool_ev = sp.sem("pool_ev")
        passed = sp.sem("passed")
        zeroed = sp.sem("zeroed")
        pe_mx = sp.sem("pe_mx")
        dve_mx = sp.sem("dve_mx")
        pe_mr = sp.sem("pe_mr")
        act_mr = sp.sem("act_mr")
        pe_st = sp.sem("pe_st")
        act_ex = sp.sem("act_ex")
        act_eh = sp.sem("act_eh")
        dve_el = sp.sem("dve_el")
        pe_av = sp.sem("pe_av")
        act_ov = sp.sem("act_ov")
        o_out = [sp.sem(f"o_out{i}") for i in range(2)]

        block = ctx.enter_context(nc.Block())

        def each_pair(e, step, extra):
            with e.Fori(0, HP // 2) as hp2:
                for wp in range(2):
                    for b in range(HB):
                        step(2 * hp2 + wp, wp, b, True)
            step(HP, 0, 0, False)
            extra()

        @block.sync
        def _(e):
            def load_weights(hp):
                for m in range(3):
                    e.dma_start(w_raw[:, m], weights[m][hp]).then_inc(w_in, 16)
                    e.dma_start(b_raw[:, m:m + 1], biases[m][hp]).then_inc(w_in, 16)

            def step(hp, wp, b, proj):
                s = HB * hp + b
                bp = (b - 1) % HB
                slot = hp + (1 if b else 0)
                if proj and b == HB - 1:
                    after = (hp + 2) % HP
                    e.wait_ge(act_w, 4 * hp + 8)
                    e.wait_ge(w_split, 3 * hp + 6)
                    load_weights(after)
                for h in range(2):
                    e.wait_ge(act_ov, 2 * s + h + 2)
                    rows = own[h]
                    sums = HD if h == 0 else 0
                    e.dma_start(o_raw[slot, rows, half * HTOK + bp * S:half * HTOK + (bp + 1) * S],
                                osb[rows, h]).then_inc(o_out[h], 16)
                    e.dma_start(o_sum[slot, h:h + 1, half * HTOK + bp * S:half * HTOK + (bp + 1) * S],
                                osb[sums:sums + 1, h]).then_inc(o_out[h], 16)

            def end():
                for h in range(2):
                    e.wait_ge(o_out[h], 32 * (HB * HP + 2))
                e.wait_ge(w_in, 96 * (HP + 2))

            load_weights(0)
            e.wait_ge(act_w, 4)
            e.wait_ge(w_split, 3)
            load_weights(1)
            each_pair(e, step, end)

        @block.scalar
        def _(e):
            def split_weights(n, wp, m):
                e.wait_ge(w_in, 96 * n + 96)
                nc.scalar.activation(w_hi[:, wp, m], w_raw[:, m], ACT.Copy).then_inc(act_w, 1)
                if m == 2:
                    nc.scalar.activation(bias[:, wp, 0:3], b_raw[:, 0:3], ACT.Copy).then_inc(act_w, 1)

            def exp_tile(s, t):
                u = 8 * s + t
                e.wait_ge(pe_st, u + 1)
                e.wait_ge(dve_el, u + 1)
                nc.scalar.activation(ex[:, t % 2], st[:, t % 2], ACT.Exp, scale=SCALE).then_inc(act_ex, 1)

            def high_tile(s, t):
                u = 8 * s + t
                e.wait_ge(act_ex, u + 3)
                e.wait_ge(pe_av, u + 1)
                nc.scalar.activation(eh[:, t % 4], ex[:, t % 2], ACT.Copy).then_inc(act_eh, 1)

            def high_part(dst, s, wp, b, m, h):
                e.wait_ge(pe_pj, 4 * s + m + 1)
                nc.scalar.activation(dst[own[h], b % 2, h], pj[own[h], m], ACT.Identity,
                                     bias=bias[own[h], wp, m:m + 1]).then_inc(act_ev, 1)

            def max_row(s, par, h, n):
                e.wait_ge(pe_mr, n)
                r = mrow[h]
                nc.scalar.activation(qb[r:r + 1, par, h], mr[r:r + 1, :], ACT.Copy).then_inc(act_mr, 1)

            def out_tile(s, h):
                e.wait_ge(pe_av, 8 * s + 4 * h + 8)
                e.wait_ge(o_out[h], 32 * s + 32)
                nc.scalar.activation(osb[:, h], ov[:, :], ACT.Copy).then_inc(act_ov, 1)

            def step(hp, wp, b, proj):
                s = HB * hp + b
                for t in range(8 + LAG):
                    if 1 <= t < 9:
                        high_tile(s, t - 1)
                    if t < 8:
                        exp_tile(s, t)
                    if proj and t == 2:
                        high_part(qa, s, wp, b, 0, 0)
                        high_part(qa, s, wp, b, 0, 1)
                    if t == 3:
                        max_row(s, (b - 1) % 2, 1, 2 * s + 1)
                    if proj and t == 5:
                        high_part(ka, s, wp, b, 1, 0)
                        high_part(ka, s, wp, b, 1, 1)
                    if t == 6:
                        out_tile(s, 0)
                    if proj and t == 8:
                        e.wait_ge(pe_pj, 4 * s + 3)
                        nc.scalar.activation(vt[:, :], pj[:, 0], ACT.Identity,
                                             bias=bias[:, wp, 2:3]).then_inc(act_ev, 1)
                    if proj and t == 10:
                        max_row(s, b % 2, 0, 2 * s + 2)
                        e.wait_ge(pe_pj, 4 * s + 4)
                        nc.scalar.activation(va[:, b % 2, :, 0:3:2, :],
                                             pj[:, 1].rearrange("p (k h d) -> p k h d", h=2, d=HD),
                                             ACT.Copy).then_inc(act_ev, 1)
                    if proj and t == 9 and b < 3:
                        split_weights(hp + 1, 1 - wp, b)
                out_tile(s, 1)

            e.sem_inc(act_ev, 6)
            e.sem_inc(act_mr, 1)
            e.sem_inc(act_ex, 2)
            e.sem_inc(act_ov, 1)
            e.sem_inc(o_out[0], 32)
            e.sem_inc(o_out[1], 32)
            for m in range(3):
                split_weights(0, 0, m)
            e.wait_ge(act_w, 4)
            e.wait_ge(zeroed, 12)
            each_pair(e, step, lambda: None)

        @block.vector
        def _(e):
            def split_weights(n, wp, m):
                e.wait_ge(act_w, 4 * n + m + 1)
                nc.vector.tensor_tensor(w_lo[:, wp, m], w_raw[:, m], f32(w_hi[:, wp, m]),
                                        ALU.subtract).then_inc(w_split, 1)

            def low_tile(s, t):
                u = 8 * s + t
                e.wait_ge(act_eh, u + 1)
                nc.vector.tensor_tensor(el[:, t % 4], ex[:, t % 2], f32(eh[:, t % 4]),
                                        ALU.subtract).then_inc(dve_el, 1)

            def low_part(dst, rows, hi, s, wp, b, m, h):
                e.wait_ge(act_ev, 6 * s + 2 * m + h + 7)
                nc.vector.scalar_tensor_tensor(dst[rows, b % 2, h], pj[own[h], m],
                                               bias[own[h], wp, m:m + 1], f32(hi[own[h], b % 2, h]),
                                               ALU.add, ALU.subtract).then_inc(dve_ev, 1)

            def max_tile(n, h, qt):
                e.wait_ge(pe_mx, n + 1)
                nc.vector.tensor_reduce(negm[:, h, qt, mrow[h]:mrow[h] + 1], mx[:, qt % 2], AX_X,
                                        ALU.max, negate=True).then_inc(dve_mx, 1)

            def step(hp, wp, b, proj):
                s = HB * hp + b
                for t in range(8 + LAG):
                    for qt in MAX1_AT.get(t, ())[:1]:
                        max_tile(8 * s + qt, 1, qt)
                    for qt in MAX0_AT.get(t, ())[:1] if proj else ():
                        max_tile(8 * s + NT + qt, 0, qt)
                    if 1 <= t < 9:
                        low_tile(s, t - 1)
                    for qt in MAX1_AT.get(t, ())[1:]:
                        max_tile(8 * s + qt, 1, qt)
                    if not proj:
                        continue
                    if t == 3:
                        low_part(qa, other[0], qa, s, wp, b, 0, 0)
                        low_part(qa, other[1], qa, s, wp, b, 0, 1)
                    if t == 6:
                        low_part(kb, own[0], ka, s, wp, b, 1, 0)
                        low_part(kb, own[1], ka, s, wp, b, 1, 1)
                    for qt in MAX0_AT.get(t, ())[1:]:
                        max_tile(8 * s + NT + qt, 0, qt)
                    if t == 10:
                        e.wait_ge(act_ev, 6 * s + 12)
                        nc.vector.tensor_tensor(vb[:, b % 2, :, 0:3:2, :],
                                                pj[:, 1].rearrange("p (k h d) -> p k h d", h=2, d=HD),
                                                f32(va[:, b % 2, :, 0:3:2, :]),
                                                ALU.subtract).then_inc(dve_ev, 1)
                    if t == 10 and b < 3:
                        split_weights(hp + 1, 1 - wp, b)

            for tile, value in ((qa, 0.0), (qb, 0.0), (ka, 0.0), (kb, 0.0), (va, 0.0), (vb, 0.0),
                                (negm, 0.0)):
                nc.vector.memset(f32(tile[:]), value).then_inc(zeroed, 1)
            e.wait_ge(zeroed, 7)
            nc.vector.memset(f32(va[:, :, :, 1, :]), 1.0).then_inc(zeroed, 1)
            for h in range(2):
                for par in range(2):
                    nc.vector.memset(f32(kb[mrow[h]:mrow[h] + 1, par, h]), 1.0).then_inc(zeroed, 1)
            e.wait_ge(zeroed, 12)
            e.sem_inc(dve_ev, 5)
            e.sem_inc(dve_mx, 2)
            e.sem_inc(dve_el, 2)
            for m in range(3):
                split_weights(0, 0, m)
            each_pair(e, step, lambda: None)

        @block.gpsimd
        def _(e):
            e.wait_ge(zeroed, 12)

            def step(hp, wp, b, proj):
                if not proj:
                    return
                s = HB * hp + b
                for h in range(2):
                    e.wait_ge(act_ev, 6 * s + h + 7)
                    e.sem_inc(passed, 1)
                    nc.gpsimd.tensor_scalar(qb[own[h], b % 2, h], f32(qa[own[h], b % 2, h]), 1.0, 1.0,
                                            ALU.mult, ALU.mult).then_inc(pool_ev, 1)
                    e.wait_ge(pool_ev, 4 * s + h + 1)
                for h in range(2):
                    e.wait_ge(act_ev, 6 * s + h + 9)
                    e.sem_inc(passed, 1)
                    nc.gpsimd.tensor_scalar(ka[other[h], b % 2, h], f32(ka[own[h], b % 2, h]), 1.0, 1.0,
                                            ALU.mult, ALU.mult).then_inc(pool_ev, 1)
                    e.wait_ge(pool_ev, 4 * s + h + 3)

            each_pair(e, step, lambda: None)

        @block.tensor
        def _(e):
            def projection(wp, b, m):
                passes = [(w_hi, xh), (w_lo, xh), (w_hi, xl)]
                for n, (w, xx) in enumerate(passes):
                    for k in range(DK):
                        yield nc.tensor.matmul(pj[:, m % 2], w[:, wp, m, k], xx[:, k, b * S:(b + 1) * S],
                                               start=(n == 0 and k == 0), stop=(n == 2 and k == DK - 1))

            def scores(s, par, t):
                u = 8 * s + t
                h, kt = t // NT, t % NT
                cols = slice(kt * P, (kt + 1) * P)
                if kt == 0:
                    e.wait_ge(act_mr, 2 * s + h + 1)
                    e.wait_ge(dve_ev, 5 * s + 5)
                e.wait_ge(act_ex, u + 1)
                nc.tensor.matmul(st[:, t % 2], ka[:, par, h, cols], qa[:, par, h], start=True, stop=False)
                nc.tensor.matmul(st[:, t % 2], kb[:, par, h, cols], qb[:, par, h], start=False,
                                 stop=True).then_inc(pe_st, 1)

            def product(s, par, t):
                u = 8 * s + t
                h, kt = t // NT, t % NT
                e.wait_ge(dve_el, u + 3)
                if kt == 0:
                    e.wait_ge(act_ov, 2 * s + h + 1)
                a = va[:, par, kt].rearrange("p c d -> p (c d)")[:, HD * h:HD * h + P]
                c = vb[:, par, kt].rearrange("p c d -> p (c d)")[:, HD * h:HD * h + P]
                nc.tensor.matmul(ov[:, :], a, eh[:, t % 4], start=(kt == 0), stop=False)
                nc.tensor.matmul(ov[:, :], c, eh[:, t % 4], start=False, stop=False)
                nc.tensor.matmul(ov[:, :], a, el[:, t % 4], start=False, stop=(kt == NT - 1)).then_inc(pe_av, 1)

            def max_scores(s, par, n, h, qt):
                if h == 0 and qt == 0:
                    e.wait_ge(act_ev, 6 * s + 10)
                    e.wait_ge(dve_ev, 5 * s + 7)
                    e.wait_ge(pool_ev, 4 * s + 4)
                e.wait_ge(dve_mx, n + 1)
                nc.tensor.matmul(mx[:, qt % 2], qa[:, par, h, qt * P:(qt + 1) * P], ka[:, par, h],
                                 start=True, stop=True).then_inc(pe_mx, 1)

            def max_row(s, h, maxima, rows):
                e.wait_ge(dve_mx, maxima)
                e.wait_ge(act_mr, rows)
                for t in range(NT):
                    last = nc.tensor.matmul(mr[:, t * P:(t + 1) * P], negm[:, h, t], ident_r[:, :],
                                            start=True, stop=True)
                last.then_inc(pe_mr, 1)

            def start_projection(hp, wp, b, s, m):
                if b == 0 and m == 0:
                    e.wait_ge(act_w, 4 * hp + 4)
                    e.wait_ge(w_split, 3 * hp + 3)
                if m == 0:
                    e.wait_ge(act_ev, 6 * s + 5)
                elif m == 1:
                    e.wait_ge(act_ev, 6 * s + 6)
                    e.wait_ge(dve_ev, 5 * s + 5)
                else:
                    e.wait_ge(act_ev, 6 * s + 8)
                    e.wait_ge(dve_ev, 5 * s + 7)
                return projection(wp, b, m)

            def step(hp, wp, b, proj):
                s = HB * hp + b
                par = (b - 1) % 2
                work = None
                for t in range(8 + LAG):
                    if 0 < t < 8:
                        scores(s, par, t)
                    if proj and t < 8:
                        m, count, first, last_part = PROJECTION_AT[t]
                        if first:
                            work = start_projection(hp, wp, b, s, m)
                        for _ in range(count):
                            last = next(work)
                        if last_part:
                            last.then_inc(pe_pj, 1)
                    if t == 0:
                        scores(s, par, t)
                    if t == 3:
                        max_row(s, 1, 8 * s + 4 + 2, 2 * s + 1)
                    for qt in MAX1_AT.get(t, ()):
                        max_scores(s, par, 8 * s + qt, 1, qt)
                    for qt in MAX0_AT.get(t, ())[:1] if proj else ():
                        max_scores(s, b % 2, 8 * s + NT + qt, 0, qt)
                    if t >= LAG:
                        product(s, par, t - LAG)
                    if not proj:
                        continue
                    if t == 9:
                        e.wait_ge(act_ev, 6 * s + 11)
                        e.wait_ge(dve_ev, 5 * s + 9)
                        for kt in range(NT):
                            last = nc.tensor.transpose(pj[:, 1, kt * P:(kt + 1) * P],
                                                       vt[:, kt * P:(kt + 1) * P], ident[:, :])
                        last.then_inc(pe_pj, 1)
                    for qt in MAX0_AT.get(t, ())[1:]:
                        max_scores(s, b % 2, 8 * s + NT + qt, 0, qt)
                    if t == 10:
                        max_row(s, 0, 8 * s + 8 + 2, 2 * s + 2)

            e.sem_inc(pe_av, 4)
            e.wait_ge(zeroed, 12)
            each_pair(e, step, lambda: None)


MAX1_AT = {0: (0, 1), 1: (2,), 2: (3,)}
MAX0_AT = {7: (0,), 8: (1,), 9: (2, 3)}
PROJECTION_AT = ((0, 6, True, False), (0, 6, False, True), (1, 6, True, False), (1, 3, False, False),
                 (1, 3, False, True), (2, 4, True, False), (2, 4, False, False), (2, 4, False, True))


def reciprocal_stage(nc, env, name):
    dst = env[f"{name}_rcp"]
    src = env["o_sum"][1:] if name == "o" else env["c_raw"][:, :, 2 * XD, S:]
    slots, heads = dst.shape[0], dst.shape[1]
    cut = P // (slots * heads)
    width = T // cut
    with ExitStack() as ctx:
        sp = Space(nc, ctx, f"{name}rc")
        sums = sp.sb("sums", [P, width])
        rcp = sp.sb("rcp", [P, width])
        landed = sp.sem("landed")
        done = sp.sem("done")
        stored = sp.sem("stored")
        block = ctx.enter_context(nc.Block())

        @block.sync
        def _(e):
            for n in range(slots):
                for h in range(heads):
                    row = (n * heads + h) * cut
                    e.dma_start(sums[row:row + cut, :], src[n, h].rearrange("(c w) -> c w", w=width)).then_inc(landed, 16)
            e.wait_ge(done, 1)
            for n in range(slots):
                for h in range(heads):
                    row = (n * heads + h) * cut
                    e.dma_start(dst[n, h].rearrange("(c w) -> c w", w=width), rcp[row:row + cut, :]).then_inc(stored, 16)
            e.wait_ge(stored, 16 * slots * heads)

        @block.vector
        def _(e):
            e.wait_ge(landed, 16 * slots * heads)
            nc.vector.reciprocal(rcp[:, :], sums[:, :]).then_inc(done, 1)


def output_stage(nc, env, name):
    ident, mhalf = env["ident"], env["minus_half"]
    final = name == "c"
    KT = CTX_TILES if final else HP
    heads = 4 if final else 2
    width = P // heads
    rcp = env[f"{name}_rcp"]
    x_in = env["x1"] if final else env["x"]
    x_out = env["x2"] if final else env["x1"]
    wo = env["Wo2" if final else "Wo"].rearrange("(k p) n -> p k n", p=P)
    RING = 4
    LW = 2
    parts = 2 if final else 1
    per_chunk = 16 * (8 + heads if final else 1 + heads)
    xt_out = [env["xn3"]] if final else [env["xn2_hi"], env["xn2_lo"]]
    LATE = KT - 1 if final else KT - 2
    OUTS = 16 * len(xt_out)

    with ExitStack() as ctx:
        sp = Space(nc, ctx, f"{name}p")
        w_raw = sp.sb("w_raw", [P, 2, LW, D])
        w_hi = sp.sb("w_hi", [P, KT, D], F32R)
        w_lo = sp.sb("w_lo", [P, KT, D], F32R)
        o = sp.sb("o", [P, RING, parts, S])
        r = sp.sb("r", [P, RING, S])
        oh = sp.sb("oh", [P, RING, S], F32R)
        ol = sp.sb("ol", [P, RING, S], F32R)
        xin = sp.sb("xin", [P, 2, NT, D])
        x1 = sp.sb("x1", [P, 2, NT, D])
        xn = sp.sb("xn", [P, NT, D])
        stats = sp.sb("stats", [P, NT, 6])
        mv = sp.sb("mv", [P, NT, 2])
        ve = sp.sb("ve", [P, NT])
        rstd = sp.sb("rstd", [P, NT])
        xo = sp.sb("xo", [P, 2, DK, S], F32 if final else F32R)
        if not final:
            xol = sp.sb("xol", [P, 2, DK, S], F32R)
            bo = sp.sb("bo", [1, D])
            bo_hi = sp.sb("bo_hi", [1, D], F32R)
            bo_lo = sp.sb("bo_lo", [1, D], F32R)
            ones = sp.sb("ones", [1, P], F32R)
        acc = sp.ps("acc", [P, NT, D])
        pt = sp.ps("pt", [P, NT, DK, P])
        w_in = [sp.sem(f"w_in{i}") for i in range(2)]
        act_w = sp.sem("act_w")
        dve_w = sp.sem("dve_w")
        chunk_in = [sp.sem(f"chunk_in{i}") for i in range(RING)]
        dve_o = sp.sem("dve_o")
        act_oh = sp.sem("act_oh")
        dve_ol = sp.sem("dve_ol")
        pe_ck = sp.sem("pe_ck")
        pe_acc = sp.sem("pe_acc")
        xin_in = [sp.sem(f"xin_in{i}") for i in range(2)]
        dve_x1 = sp.sem("dve_x1")
        x1_out = [sp.sem(f"x1_out{i}") for i in range(2)]
        passed = sp.sem("passed")
        dve_st = sp.sem("dve_st")
        pool_rs = sp.sem("pool_rs")
        dve_xn = sp.sem("dve_xn")
        pe_tr = sp.sem("pe_tr")
        act_hi = sp.sem("act_hi")
        dve_lo = sp.sem("dve_lo")
        xo_out = [sp.sem(f"xo_out{i}") for i in range(2)]
        bo_in = sp.sem("bo_in")
        ones_in = sp.sem("ones_in")

        xs_in = x_in.rearrange("(g n p) d -> g p n d", n=NT, p=P)
        xs_out = x_out.rearrange("(g n p) d -> g p n d", n=NT, p=P)
        block = ctx.enter_context(nc.Block())

        def each_batch(e, step):
            step(0, 0, 0, True, False)
            with e.Fori(0, B // 2 - 1) as g2:
                step(2 * g2 + 1, 1, g2, True, True)
                step(2 * g2 + 2, 0, g2 + 1, True, True)
            step(B - 1, 1, B // 2 - 1, True, True)
            step(B, 0, B // 2, False, True)

        @block.sync
        def _(e):
            for n in range(KT // LW):
                if n >= 2:
                    e.wait_ge(act_w, n - 1)
                    e.wait_ge(dve_w, n - 1)
                e.dma_start(w_raw[:, n % 2], wo[:, n * LW:(n + 1) * LW]).then_inc(w_in[n % 2], 16)
            if not final:
                e.dma_start(bo[:, :], env["bo"].rearrange("(a n) -> a n", a=1)).then_inc(bo_in, 16)
            with e.Fori(0, B // 2) as g2:
                for u in range(2):
                    g = 2 * g2 + u
                    at = bass.ds(g * S, S)
                    e.wait_ge(dve_x1, 8 * g2 + 4 * u + 4)
                    e.dma_start(xin[:, u], xs_in[g]).then_inc(xin_in[u], 16)
                    for k in range(KT):
                        c = k % RING
                        e.wait_ge(dve_ol, KT * g + k + 1)
                        e.wait_ge(act_oh, KT * g + k + 1)
                        if final:
                            for n in range(parts):
                                for h in range(heads):
                                    e.dma_start(o[h * width:(h + 1) * width, c, n],
                                                env["c_raw"][k, h, n * width:(n + 1) * width,
                                                             bass.ds(g * S + S, S)]).then_inc(chunk_in[c], 16)
                        else:
                            e.dma_start(o[:, c, 0], env["o_raw"][k + 1, :, at]).then_inc(chunk_in[c], 16)
                        for h in range(heads):
                            e.dma_start(r[h * width:(h + 1) * width, c],
                                        rcp[k, h:h + 1, at].partition_broadcast(width)
                                        ).then_inc(chunk_in[c], 16)

        @block.gpsimd
        def _(e):
            with e.Fori(0, B // 2) as g2:
                for u in range(2):
                    g = 2 * g2 + u
                    e.wait_ge(dve_st, 9 * g + 9)
                    nc.gpsimd.tensor_tensor(rstd[:, :], ve[:, :], mhalf[:, 0:NT], ALU.pow).then_inc(pool_rs, 1)

        @block.scalar
        def _(e):
            for n in range(KT // LW):
                e.wait_ge(w_in[n % 2], 16 * (n // 2) + 16)
                nc.scalar.activation(w_hi[:, n * LW:(n + 1) * LW], w_raw[:, n % 2], ACT.Copy).then_inc(act_w, 1)
            if not final:
                e.wait_ge(bo_in, 16)
                nc.scalar.activation(bo_hi[:, :], bo[:, :], ACT.Copy).then_inc(ones_in, 1)
            e.sem_inc(act_oh, RING)
            e.sem_inc(act_hi, 4)
            for u in range(2):
                e.sem_inc(x1_out[u], 16)
                e.sem_inc(xo_out[u], OUTS)
            def step(g, par, gh, products, norm):
                last, prev = g - 1, 1 - par
                prev_h = gh if par else gh - 1
                for k in range(KT if products else 0):
                    c = k % RING
                    e.wait_ge(dve_o, parts * (KT * g + k + 1))
                    e.wait_ge(pe_ck, KT * g + k + 1)
                    nc.scalar.activation(oh[:, c], o[:, c, 0], ACT.Copy).then_inc(act_oh, 1)
                    if norm and k == 0:
                        store(last, prev)
                    if norm and k == LATE:
                        transposed(last, prev, prev_h)
                if not products:
                    store(last, prev)
                    transposed(last, prev, prev_h)

            def store(g, par):
                e.wait_ge(dve_x1, 4 * g + 12)
                e.dma_start(xs_out[g], x1[:, par]).then_inc(x1_out[par], 16)

            def transposed(g, par, gh):
                e.wait_ge(xo_out[par], OUTS * gh + OUTS)
                for t in range(NT):
                    e.wait_ge(pe_tr, 4 * g + t + 5)
                    nc.scalar.activation(xo[:, par, :, t * P:(t + 1) * P], pt[:, t], ACT.Copy).then_inc(act_hi, 1)
                e.wait_ge(act_hi, 4 * g + 8)
                e.wait_ge(dve_lo, 4 * g + 8)
                e.dma_start(xt_out[0][:, :, bass.ds(g * S, S)], xo[:, par].bitcast(F32)).then_inc(xo_out[par], 16)
                if not final:
                    e.dma_start(xt_out[1][:, :, bass.ds(g * S, S)], f32(xol[:, par])).then_inc(xo_out[par], 16)

            each_batch(e, step)
            for u in range(2):
                e.wait_ge(x1_out[u], 16 * (B // 2) + 16)
                e.wait_ge(xo_out[u], OUTS * (B // 2) + OUTS)

        @block.vector
        def _(e):
            if not final:
                nc.vector.memset(f32(ones[:, :]), 1.0).then_inc(ones_in, 1)
            for n in range(KT // LW):
                e.wait_ge(act_w, n + 1)
                nc.vector.tensor_tensor(w_lo[:, n * LW:(n + 1) * LW], w_raw[:, n % 2],
                                        f32(w_hi[:, n * LW:(n + 1) * LW]), ALU.subtract).then_inc(dve_w, 1)
            if not final:
                e.wait_ge(ones_in, 2)
                nc.vector.tensor_tensor(bo_lo[:, :], bo[:, :], f32(bo_hi[:, :]), ALU.subtract).then_inc(ones_in, 1)
            e.sem_inc(dve_ol, RING)
            e.sem_inc(dve_x1, 8)
            e.sem_inc(dve_lo, 4)
            def step(g, par, gh, products, norm):
                last, prev = g - 1, 1 - par

                def normalise(g, k):
                    c = k % RING
                    e.wait_ge(chunk_in[c], per_chunk * ((KT // RING) * g + k // RING + 1))
                    if final:
                        nc.vector.tensor_tensor(o[:, c, 0], o[:, c, 0], o[:, c, 1], ALU.add).then_inc(dve_o, 1)
                        e.wait_ge(dve_o, 2 * (KT * g + k) + 1)
                    nc.vector.tensor_tensor(o[:, c, 0], o[:, c, 0], r[:, c], ALU.mult).then_inc(dve_o, 1)

                def low(g, k):
                    c = k % RING
                    e.wait_ge(act_oh, KT * g + k + 1 + RING)
                    nc.vector.tensor_tensor(ol[:, c], o[:, c, 0], f32(oh[:, c]), ALU.subtract).then_inc(dve_ol, 1)

                if products and not norm:
                    normalise(g, 0)
                    low(g, 0)
                for k in range(1, KT if products else 0):
                    normalise(g, k)
                    if k > 1:
                        low(g, k - 1)
                    if norm and k < 4:
                        (statistics, aggregates, normalised)[k - 1](last, prev)
                    if norm and k == LATE:
                        low_or_maximum(last, prev)
                if not products:
                    statistics(last, prev)
                    aggregates(last, prev)
                    normalised(last, prev)
                    low_or_maximum(last, prev)
                    return
                has_next = not isinstance(g, int) or g < B - 1
                if has_next:
                    normalise(g + 1, 0)
                low(g, KT - 1)
                if has_next:
                    low(g + 1, 0)
                if final:
                    e.wait_ge(pe_ck, KT * g + KT + RING)
                else:
                    e.wait_ge(pe_acc, g + 1)
                e.wait_ge(xin_in[par], 16 * gh + 16)
                e.wait_ge(x1_out[par], 16 * gh + 16)
                for t in range(NT):
                    nc.vector.tensor_tensor(x1[:, par, t], acc[:, t], xin[:, par, t], ALU.add).then_inc(dve_x1, 1)

            def statistics(g, par):
                for t in range(NT):
                    e.wait_ge(dve_x1, 4 * g + t + 9)
                    nc.vector.bn_stats(stats[:, t], x1[:, par, t]).then_inc(dve_st, 1)

            def aggregates(g, par):
                for t in range(NT):
                    e.wait_ge(dve_st, 9 * g + t + 1)
                    e.sem_inc(passed, 1)
                    nc.vector.bn_aggr(mv[:, t], stats[:, t]).then_inc(dve_st, 1)
                e.wait_ge(dve_st, 9 * g + 8)
                nc.vector.tensor_scalar(ve[:, :], mv[:, :, 1], EPS, None, ALU.add).then_inc(dve_st, 1)

            def normalised(g, par):
                e.wait_ge(pool_rs, g + 1)
                for t in range(NT):
                    e.wait_ge(pe_tr, 4 * g + t + 1)
                    nc.vector.tensor_scalar(xn[:, t], x1[:, par, t], mv[:, t, 0:1], rstd[:, t:t + 1],
                                            ALU.subtract, ALU.mult).then_inc(dve_xn, 1)

            def low_or_maximum(g, par):
                for t in range(NT):
                    cols = slice(t * P, (t + 1) * P)
                    e.wait_ge(act_hi, 4 * g + t + 5)
                    if final:
                        nc.vector.tensor_reduce(env["xn3_max"][:, bass.ds(4 * g + t, 1)], xo[:, par, :, cols],
                                                AX_XY, ALU.max, apply_absolute_value=True).then_inc(dve_lo, 1)
                    else:
                        nc.vector.tensor_tensor(xol[:, par, :, cols], pt[:, t], f32(xo[:, par, :, cols]),
                                                ALU.subtract).then_inc(dve_lo, 1)

            each_batch(e, step)

        @block.tensor
        def _(e):
            e.wait_ge(act_w, KT // LW)
            e.wait_ge(dve_w, KT // LW)
            if not final:
                e.wait_ge(ones_in, 3)
            e.sem_inc(pe_ck, RING)
            e.sem_inc(pe_tr, 4)
            def transposes(g):
                for t in range(NT):
                    e.wait_ge(dve_xn, 4 * g + t + 1)
                    e.wait_ge(dve_lo, 4 * g + t + 1)
                    e.wait_ge(act_hi, 4 * g + t + 1)
                    for k in range(DK):
                        last = nc.tensor.transpose(pt[:, t, k], xn[:, t, k * P:(k + 1) * P], ident[:, :])
                    last.then_inc(pe_tr, 1)

            def step(g, par, gh, products, norm):
                if not products:
                    transposes(g - 1)
                    return
                e.wait_ge(dve_x1, 4 * g + 8)
                for k in range(KT):
                    c = k % RING
                    e.wait_ge(dve_ol, KT * g + k + 1 + RING)
                    for t in range(NT):
                        cols = slice(t * P, (t + 1) * P)
                        start = k == 0
                        stop = final and k == KT - 1
                        nc.tensor.matmul(acc[:, t], oh[:, c, cols], w_hi[:, k], start=start, stop=False)
                        nc.tensor.matmul(acc[:, t], oh[:, c, cols], w_lo[:, k], start=False, stop=False)
                        last = nc.tensor.matmul(acc[:, t], ol[:, c, cols], w_hi[:, k], start=False, stop=stop)
                    last.then_inc(pe_ck, 1)
                    if norm and k == LATE - (1 if final else 2):
                        transposes(g - 1)
                if not final:
                    for t in range(NT):
                        nc.tensor.matmul(acc[:, t], ones[:, :], bo_hi[:, :], start=False, stop=False)
                        last = nc.tensor.matmul(acc[:, t], ones[:, :], bo_lo[:, :], start=False, stop=True)
                    last.then_inc(pe_acc, 1)

            each_batch(e, step)


def context_stage(nc, env):
    ident = env["ident"]
    with ExitStack() as ctx:
        sp = Space(nc, ctx, "cx")
        xt = sp.sb("x", [P, 2, NT, CD])
        ch = sp.sb("ch", [P, 2, CK, S], F32R)
        cl = sp.sb("cl", [P, 2, CK, S], F32R)
        mask_u8 = sp.sb("mask_u8", [B, S], U8)
        mask_f = sp.sb("mask_f", [B, S])
        mask_n = sp.sb("mask_n", [B, S])
        pt = sp.ps("pt", [P, NT, 4, P])
        x_in = [sp.sem(f"x_in{i}") for i in range(2)]
        pe_tr = sp.sem("pe_tr")
        act_hi = sp.sem("act_hi")
        dve_lo = sp.sem("dve_lo")
        c_out = [sp.sem(f"c_out{i}") for i in range(2)]
        mask_in = sp.sem("mask_in")
        mask_done = sp.sem("mask_done")
        mask_out = sp.sem("mask_out")
        xs = env["ctx"].rearrange("(g n p) d -> g p n d", n=NT, p=P)
        block = ctx.enter_context(nc.Block())

        @block.sync
        def _(e):
            e.dma_start(mask_u8[:, :], env["mask"]).then_inc(mask_in, 16)
            with e.Fori(0, B // 2) as g2:
                for u in range(2):
                    e.wait_ge(pe_tr, 8 * g2 + 4 * u + 4)
                    e.dma_start(xt[:, u], xs[2 * g2 + u]).then_inc(x_in[u], 16)
            e.wait_ge(mask_done, 2)
            e.dma_start(env["mask_f"], mask_f[:, :]).then_inc(mask_out, 16)
            e.dma_start(env["mask_n"], mask_n[:, :]).then_inc(mask_out, 16)
            e.wait_ge(mask_out, 32)

        @block.tensor
        def _(e):
            e.sem_inc(pe_tr, 8)
            with e.Fori(0, B // 2) as g2:
                for u in range(2):
                    g = 2 * g2 + u
                    e.wait_ge(x_in[u], 16 * g2 + 16)
                    for t in range(NT):
                        e.wait_ge(dve_lo, 4 * g + t + 1)
                        for k in range(CK):
                            last = nc.tensor.transpose(pt[:, t, k], xt[:, u, t, k * P:(k + 1) * P], ident[:, :])
                        last.then_inc(pe_tr, 1)

        @block.scalar
        def _(e):
            e.sem_inc(act_hi, 4)
            e.sem_inc(c_out[0], 32)
            e.sem_inc(c_out[1], 32)
            with e.Fori(0, B // 2) as g2:
                for u in range(2):
                    g = 2 * g2 + u
                    e.wait_ge(c_out[u], 32 * g2 + 32)
                    for t in range(NT):
                        e.wait_ge(pe_tr, 4 * g + t + 9)
                        nc.scalar.activation(ch[:, u, :, t * P:(t + 1) * P], pt[:, t, 0:CK], ACT.Copy).then_inc(act_hi, 1)
                    e.wait_ge(act_hi, 4 * g + 8)
                    e.dma_start(env["ct_hi"][:, :, bass.ds(g * S, S)], f32(ch[:, u])).then_inc(c_out[u], 16)
                    e.wait_ge(dve_lo, 4 * g + 8)
                    e.dma_start(env["ct_lo"][:, :, bass.ds(g * S, S)], f32(cl[:, u])).then_inc(c_out[u], 16)
            for u in range(2):
                e.wait_ge(c_out[u], 32 * (B // 2) + 32)

        @block.vector
        def _(e):
            e.sem_inc(dve_lo, 4)
            e.wait_ge(mask_in, 16)
            nc.vector.tensor_copy(mask_f[:, :], mask_u8[:, :]).then_inc(mask_done, 1)
            e.wait_ge(mask_done, 1)
            nc.vector.tensor_scalar(mask_n[:, :], mask_f[:, :], 1.0, BIG, ALU.subtract, ALU.mult).then_inc(mask_done, 1)
            with e.Fori(0, B // 2) as g2:
                for u in range(2):
                    g = 2 * g2 + u
                    for t in range(NT):
                        cols = slice(t * P, (t + 1) * P)
                        e.wait_ge(act_hi, 4 * g + t + 5)
                        nc.vector.tensor_tensor(cl[:, u, :, cols], pt[:, t, 0:CK], f32(ch[:, u, :, cols]),
                                                ALU.subtract).then_inc(dve_lo, 1)


def cross_attention_stage(nc, env):
    ident, ident_r = env["ident"], env["ident_r"]
    SCALE = XD ** -0.5
    HS = 4
    SL = HS * NT
    LAG = 3
    VW = 3 * XD
    RING = 8
    MR = 3 * XD
    ROWS = 2 * XD + 1

    with ExitStack() as ctx:
        sp = Space(nc, ctx, "ca")
        w_raw = sp.sb("w_raw", [P, 2, D])
        w_hi = sp.sb("w_hi", [P, 10, D], F32R)
        w_lo = sp.sb("w_lo", [P, 10, D], F32R)
        xq = sp.sb("xq", [P, 2, DK, S], F32R)
        xc = sp.sb("xc", [P, 2, CK, S], F32R)
        maskb = sp.sb("maskb", [P, S])
        qh = sp.sb("qh", [P, S], F32R)
        ql = sp.sb("ql", [P, S], F32R)
        km = sp.sb("km", [P, S])
        kh = sp.sb("kh", [P, S], F32R)
        kl = sp.sb("kl", [P, S], F32R)
        q4 = sp.sb("q4", [P, 2, HS, S], F32R)
        k4 = sp.sb("k4", [P, 2, HS, S], F32R)
        vt = sp.sb("vt", [P, S])
        vc = sp.sb("vc", [P, 2, NT, HS, VW], F32R)
        ex = sp.sb("ex", [P, RING, S])
        eh = sp.sb("eh", [P, 4, S], F32R)
        el = sp.sb("el", [P, 4, S], F32R)
        negm = sp.sb("negm", [P, 2, NT, P], F32R)
        osb = sp.sb("osb", [VW, 2, S])
        pj = sp.ps("pj", [P, 2, S])
        st = sp.ps("st", [P, 2, S])
        mx = sp.ps("mx", [P, 2, S])
        ov = sp.ps("ov", [P, S])
        mr = sp.ps("mr", [P, S])

        w_in = [sp.sem(f"w_in{i}") for i in range(2)]
        act_w = sp.sem("act_w")
        dve_w = sp.sem("dve_w")
        zeroed = sp.sem("zeroed")
        xc_in = sp.sem("xc_in")
        xq_in = sp.sem("xq_in")
        mk_in = [sp.sem(f"mk_in{i}") for i in range(2)]
        pe_pj = sp.sem("pe_pj")
        act_ev = sp.sem("act_ev")
        dve_ev = sp.sem("dve_ev")
        pool_k = sp.sem("pool_k")
        pool_q = sp.sem("pool_q")
        k4_in = [sp.sem(f"k4_in{i}") for i in range(2)]
        passed = sp.sem("passed")
        q4_in = [sp.sem(f"q4_in{i}") for i in range(2)]
        pe_mx = sp.sem("pe_mx")
        dve_mx = sp.sem("dve_mx")
        pe_mr = sp.sem("pe_mr")
        act_mr = sp.sem("act_mr")
        pe_st = sp.sem("pe_st")
        act_ex = sp.sem("act_ex")
        act_eh = sp.sem("act_eh")
        dve_el = sp.sem("dve_el")
        pe_av = sp.sem("pe_av")
        act_ov = sp.sem("act_ov")
        o_out = [sp.sem(f"o_out{i}") for i in range(2)]
        STACKS = 2 * HS
        STEP_IN = 16 * HS

        block = ctx.enter_context(nc.Block())

        def each_step(e, step):
            with e.Fori(0, B) as b:
                for g in range(XG):
                    step(b, g, True)
            step(B, 0, False)

        @block.sync
        def _(e):
            def stack(dst, par, block_rows, src, landed):
                for j in range(HS):
                    e.dma_start(f32(dst[block_rows * XD:(block_rows + 1) * XD, par, j]),
                                f32(src[j * XD:(j + 1) * XD, :])).then_inc(landed, 16)

            def outputs(b, g, j):
                s = XG * b + g
                e.wait_ge(act_ov, 4 * s + j + 2)
                gp = (g - 1) % XG
                at = bass.ds((b + (1 if g else 0)) * S, S)
                e.dma_start(env["c_raw"][gp, j, 0:ROWS, at], osb[0:ROWS, j % 2]).then_inc(o_out[j % 2], 16)

            def step(b, g, proj):
                s = XG * b + g
                par = g % 2
                if proj:
                    e.wait_ge(dve_ev, 4 * s + 5)
                    stack(q4, par, 1, ql, q4_in[par])
                    if g == XG - 1:
                        load_batch_q((b + 1) % B, s)
                    e.wait_ge(act_ev, 4 * s + 6)
                    stack(k4, par, 1, kh, k4_in[par])
                    if g < 2:
                        for j in range(HS):
                            e.dma_start(f32(k4[MR:MR + 1, par, j]), env["mask_n"][bass.ds(b, 1), :]
                                        ).then_inc(mk_in[par], 16)
                outputs(b, g, 0)
                if proj and g == XG - 1:
                    load_batch_c((b + 1) % B, s)
                for j in range(1, HS):
                    outputs(b, g, j)

            def load_batch_c(nb, s):
                if s is not None:
                    e.wait_ge(pe_pj, 4 * s + 7)
                    e.wait_ge(dve_ev, 4 * s + 6)
                    e.sem_inc(passed, 1)
                e.dma_start(f32(xc[:, 0]), env["ct_hi"][:, :, bass.ds(nb * S, S)]).then_inc(xc_in, 16)
                e.dma_start(f32(xc[:, 1]), env["ct_lo"][:, :, bass.ds(nb * S, S)]).then_inc(xc_in, 16)
                e.dma_start(maskb[:, :], env["mask_f"][bass.ds(nb, 1), :].partition_broadcast(P)
                            ).then_inc(xc_in, 16)

            def load_batch_q(nb, s):
                if s is not None:
                    e.wait_ge(pe_pj, 4 * s + 5)
                e.dma_start(f32(xq[:, 0]), env["xn2_hi"][:, :, bass.ds(nb * S, S)]).then_inc(xq_in, 16)
                e.dma_start(f32(xq[:, 1]), env["xn2_lo"][:, :, bass.ds(nb * S, S)]).then_inc(xq_in, 16)

            tiles = [(env[n].rearrange("(k p) n -> k p n", p=P), k)
                     for n, kk in (("Wk2", CK), ("Wv2", CK), ("Wq2", DK)) for k in range(kk)]
            for n, (w, k) in enumerate(tiles):
                if n >= 2:
                    e.wait_ge(dve_w, n - 1)
                e.dma_start(w_raw[:, n % 2], w[k]).then_inc(w_in[n % 2], 16)
            load_batch_q(0, None)
            load_batch_c(0, None)
            e.wait_ge(zeroed, ZEROED)
            each_step(e, step)
            for i in range(2):
                e.wait_ge(o_out[i], 16 * (2 * XG * B + 2) + 16)
            e.wait_ge(xc_in, 48 * (B + 1))
            e.wait_ge(xq_in, 32 * (B + 1))

        @block.scalar
        def _(e):
            def exp_tile(s, t):
                u = SL * s + t
                e.wait_ge(pe_st, u + 1)
                e.wait_ge(pe_av, u + 1)
                nc.scalar.activation(ex[:, t % RING], st[:, t % 2], ACT.Exp, scale=SCALE).then_inc(act_ex, 1)

            def high_tile(s, t):
                if t not in SPLIT:
                    return
                u = SL * s + t
                e.wait_ge(act_ex, u + 3)
                e.wait_ge(pe_av, u + 5)
                nc.scalar.activation(eh[:, t % 4], ex[:, t % RING], ACT.Copy).then_inc(act_eh, 1)

            def max_row(par, h, n):
                e.wait_ge(pe_mr, n)
                nc.scalar.activation(q4[MR:MR + 2, par, h], mr[MR:MR + 2, :], ACT.Copy).then_inc(act_mr, 1)

            def out_tile(s, h):
                e.wait_ge(pe_av, SL * s + NT * h + NT + 8)
                e.wait_ge(o_out[h % 2], 16 * (2 * s + h // 2) + 16)
                nc.scalar.activation(osb[:, h % 2], ov[0:VW, :], ACT.Copy).then_inc(act_ov, 1)

            def step(b, g, proj):
                s = XG * b + g
                par = g % 2
                for t in range(SL + LAG):
                    if 1 <= t <= SL:
                        high_tile(s, t - 1)
                    if t < SL:
                        exp_tile(s, t)
                    if t in (6, 10, 14):
                        out_tile(s, (t - 6) // NT)
                    if t == 6:
                        max_row(1 - par, 2, 4 * s + 1)
                    if t == 10:
                        max_row(1 - par, 3, 4 * s + 2)
                    if proj and t == 17:
                        max_row(par, 0, 4 * s + 3)
                    if proj and t == 3:
                        e.wait_ge(pe_pj, 4 * s + 5)
                        e.wait_ge(pool_q, STACKS * s + STACKS)
                        nc.scalar.activation(qh[:, :], pj[:, 1], ACT.Copy).then_inc(act_ev, 1)
                    if proj and t == 7:
                        e.wait_ge(dve_ev, 4 * s + 6)
                        e.wait_ge(pool_k, STACKS * s + STACKS)
                        e.wait_ge(k4_in[1 - par], stacked(b, g - 1))
                        nc.scalar.activation(kh[:, :], km[:, :], ACT.Copy).then_inc(act_ev, 1)
                    if proj and t == 9:
                        e.wait_ge(pe_pj, 4 * s + 7)
                        nc.scalar.activation(vt[:, :], pj[:, 1], ACT.Copy).then_inc(act_ev, 1)
                    if proj and t == 11:
                        e.wait_ge(pe_pj, 4 * s + 8)
                        nc.scalar.activation(vc[:, par, :, :, 0:XD],
                                             pj[:, 0].rearrange("p (k h d) -> p k h d", h=HS, d=XD),
                                             ACT.Copy).then_inc(act_ev, 1)
                if proj:
                    max_row(par, 1, 4 * s + 4)
                out_tile(s, 3)

            def stacked(b, g):
                if g < 0:
                    return STEP_IN * 2 * b + STEP_IN
                return STEP_IN * (2 * b + g // 2 + 1) + STEP_IN

            for n in range(10):
                e.wait_ge(w_in[n % 2], 16 * (n // 2) + 16)
                nc.scalar.activation(w_hi[:, n], w_raw[:, n % 2], ACT.Copy).then_inc(act_w, 1)
            e.sem_inc(act_ev, 4)
            e.sem_inc(act_mr, 1)
            e.sem_inc(act_ex, 2)
            e.sem_inc(act_ov, 1)
            for i in range(2):
                e.sem_inc(o_out[i], 16)
                e.sem_inc(q4_in[i], STEP_IN)
                e.sem_inc(k4_in[i], STEP_IN)
            e.wait_ge(zeroed, ZEROED)
            each_step(e, step)

        @block.vector
        def _(e):
            def low_tile(s, t):
                if t not in SPLIT:
                    return
                e.wait_ge(act_eh, len(SPLIT) * s + SPLIT.index(t) + 1)
                nc.vector.tensor_tensor(el[:, t % 4], ex[:, t % RING], f32(eh[:, t % 4]),
                                        ALU.subtract).then_inc(dve_el, 1)

            def max_tile(n, h, qt, bank):
                e.wait_ge(pe_mx, n + 1)
                nc.vector.tensor_reduce(negm[:, h % 2, qt, MR + 1:MR + 2], mx[:, bank], AX_X,
                                        ALU.max, negate=True).then_inc(dve_mx, 1)

            def stacked(b, g):
                if g < 0:
                    return STEP_IN * 2 * b + STEP_IN
                return STEP_IN * (2 * b + g // 2 + 1) + STEP_IN

            def step(b, g, proj):
                s = XG * b + g
                par = g % 2
                for t in range(SL + LAG):
                    if t < 8:
                        max_tile(16 * s + t, 2 + t // NT, t % NT, t % 2)
                    at = CROSS_MAX_AT.get(t, ()) if proj else ()
                    for v in at[:1]:
                        max_tile(16 * s + 8 + v, v // NT, v % NT, v % 2)
                    if 1 <= t <= SL:
                        low_tile(s, t - 1)
                    for v in at[1:]:
                        max_tile(16 * s + 8 + v, v // NT, v % NT, v % 2)
                    if proj and t == 6:
                        e.wait_ge(pe_pj, 4 * s + 6)
                        if g == 0:
                            e.wait_ge(xc_in, 48 * b + 48)
                        e.wait_ge(act_ev, 4 * s + 2)
                        nc.vector.tensor_tensor(km[:, :], pj[:, 0], maskb[:, :], ALU.mult).then_inc(dve_ev, 1)
                    if proj and t == 4:
                        e.wait_ge(act_ev, 4 * s + 5)
                        e.wait_ge(q4_in[1 - par], stacked(b, g - 1))
                        nc.vector.tensor_tensor(ql[:, :], pj[:, 1], f32(qh[:, :]), ALU.subtract).then_inc(dve_ev, 1)
                    if proj and t == 8:
                        e.wait_ge(act_ev, 4 * s + 6)
                        e.wait_ge(pool_k, STACKS * s + STACKS)
                        nc.vector.tensor_tensor(kl[:, :], km[:, :], f32(kh[:, :]), ALU.subtract).then_inc(dve_ev, 1)
                    if proj and t == 12:
                        e.wait_ge(act_ev, 4 * s + 8)
                        nc.vector.tensor_tensor(vc[:, par, :, :, XD:2 * XD],
                                                pj[:, 0].rearrange("p (k h d) -> p k h d", h=HS, d=XD),
                                                f32(vc[:, par, :, :, 0:XD]), ALU.subtract).then_inc(dve_ev, 1)

            nc.vector.memset(f32(q4[:]), 0.0).then_inc(zeroed, 1)
            nc.vector.memset(f32(k4[:]), 0.0).then_inc(zeroed, 1)
            nc.vector.memset(f32(negm[:]), 0.0).then_inc(zeroed, 1)
            nc.vector.memset(f32(vc[:]), 1.0).then_inc(zeroed, 1)
            e.wait_ge(zeroed, 4)
            nc.vector.memset(f32(negm[:, :, :, MR:MR + 1]), 1.0).then_inc(zeroed, 1)
            nc.vector.memset(f32(q4[MR:MR + 1]), 1.0).then_inc(zeroed, 1)
            nc.vector.memset(f32(k4[MR:MR + 2]), 1.0).then_inc(zeroed, 1)
            for n in range(10):
                e.wait_ge(act_w, n + 1)
                nc.vector.tensor_tensor(w_lo[:, n], w_raw[:, n % 2], f32(w_hi[:, n]), ALU.subtract).then_inc(dve_w, 1)
            e.sem_inc(dve_ev, 4)
            e.sem_inc(dve_mx, 2)
            e.wait_ge(zeroed, ZEROED)
            each_step(e, step)

        @block.gpsimd
        def _(e):
            def stack(dst, par, part, src, done, count):
                for j in range(HS):
                    nc.gpsimd.tensor_scalar(dst[part * XD:(part + 1) * XD, par, j],
                                            f32(src[j * XD:(j + 1) * XD, :]), 1.0, 1.0,
                                            ALU.mult, ALU.mult).then_inc(done, 1)
                e.wait_ge(done, count)
                e.sem_inc(passed, 1)

            def step(b, g, proj):
                s = XG * b + g
                for t in range(SL + LAG):
                    if not proj:
                        continue
                    if t == 3:
                        e.wait_ge(act_ev, 4 * s + 5)
                        e.sem_inc(passed, 1)
                        stack(q4, g % 2, 0, qh, pool_q, STACKS * s + STACKS + HS)
                    if t == 5:
                        e.sem_inc(passed, 1)
                        stack(q4, g % 2, 2, qh, pool_q, STACKS * s + 2 * STACKS)
                    if t == 7:
                        e.wait_ge(act_ev, 4 * s + 6)
                        e.sem_inc(passed, 1)
                        stack(k4, g % 2, 0, kh, pool_k, STACKS * s + STACKS + HS)
                    if t == 8:
                        e.wait_ge(dve_ev, 4 * s + 7)
                        e.sem_inc(passed, 1)
                        stack(k4, g % 2, 2, kl, pool_k, STACKS * s + 2 * STACKS)

            e.sem_inc(pool_k, STACKS)
            e.sem_inc(pool_q, STACKS)
            e.wait_ge(zeroed, ZEROED)
            each_step(e, step)

        @block.tensor
        def _(e):
            def projection(first, tiles, xx, g, bank):
                cols = slice(g * P, (g + 1) * P)
                for n, (w, part) in enumerate(((w_hi, 0), (w_lo, 0), (w_hi, 1))):
                    for k in range(tiles):
                        yield nc.tensor.matmul(pj[:, bank], w[:, first + k, cols], xx[:, part, k],
                                               start=(n == 0 and k == 0), stop=(n == 2 and k == tiles - 1))

            def scores(s, par, t):
                u = SL * s + t
                h, kt = t // NT, t % NT
                if kt == 0:
                    e.wait_ge(act_mr, 4 * s + (h - 1 if h >= 2 else 0) + 1)
                e.wait_ge(act_ex, u + 1)
                nc.tensor.matmul(st[:, t % 2], k4[0:MR + 2, par, h, kt * P:(kt + 1) * P],
                                 q4[0:MR + 2, par, h], start=True, stop=True).then_inc(pe_st, 1)

            def product(s, par, t):
                u = SL * s + t
                h, kt = t // NT, t % NT
                if t in SPLIT:
                    e.wait_ge(dve_el, len(SPLIT) * s + SPLIT.index(t) + 1)
                else:
                    e.wait_ge(act_ex, u + 3)
                if kt == 0:
                    e.wait_ge(act_ov, 4 * s + h + 1)
                    e.wait_ge(dve_ev, 4 * s + 4)
                if t not in SPLIT:
                    nc.tensor.matmul(ov[0:VW, :], f32(vc[:, par, kt, h]), ex[:, t % RING], start=(kt == 0),
                                     stop=(kt == NT - 1)).then_inc(pe_av, 1)
                    return
                nc.tensor.matmul(ov[0:VW, :], vc[:, par, kt, h], eh[:, t % 4], start=(kt == 0), stop=False)
                nc.tensor.matmul(ov[0:VW, :], vc[:, par, kt, h], el[:, t % 4], start=False,
                                 stop=(kt == NT - 1)).then_inc(pe_av, 1)

            def max_scores(n, par, h, qt, bank):
                e.wait_ge(dve_mx, n + 1)
                nc.tensor.matmul(mx[:, bank], q4[0:MR + 1, par, h, qt * P:(qt + 1) * P],
                                 k4[0:MR + 1, par, h], start=True, stop=True).then_inc(pe_mx, 1)

            def max_row(h, maxima, rows):
                e.wait_ge(dve_mx, maxima)
                e.wait_ge(act_mr, rows)
                for t in range(NT):
                    last = nc.tensor.matmul(mr[:, t * P:(t + 1) * P], negm[:, h % 2, t], ident_r[:, :],
                                            start=True, stop=True)
                last.then_inc(pe_mr, 1)

            def step(b, g, proj):
                s = XG * b + g
                par = g % 2
                work = None
                for t in range(SL + LAG):
                    if 0 < t < SL:
                        scores(s, 1 - par, t)
                    if proj and t in (0, 3, 6):
                        if t == 0:
                            if g == 0:
                                e.wait_ge(xq_in, 32 * b + 32)
                            e.wait_ge(act_ev, 4 * s + 3)
                            work = projection(2 * CK, DK, xq, g, 1)
                        elif t == 3:
                            if g == 0:
                                e.wait_ge(xc_in, 48 * b + 48)
                            e.wait_ge(dve_ev, 4 * s + 4)
                            work = projection(0, CK, xc, g, 0)
                        else:
                            e.wait_ge(dve_ev, 4 * s + 5)
                            work = projection(CK, CK, xc, g, 1)
                    if work is not None:
                        for _ in range(4 if t < 3 else 3):
                            last = next(work)
                        if t in (2, 5, 8):
                            last.then_inc(pe_pj, 1)
                            work = None
                    if t == 0:
                        scores(s, 1 - par, t)
                    if t == 5:
                        max_row(2, 16 * s + 4 + 2, 4 * s + 1)
                    if t == 9:
                        max_row(3, 16 * s + 8 + 2, 4 * s + 2)
                    if t < 8:
                        max_scores(16 * s + t, 1 - par, 2 + t // NT, t % NT, t % 2)
                    if t >= LAG:
                        product(s, 1 - par, t - LAG)
                    if not proj:
                        continue
                    if t == 10:
                        e.wait_ge(act_ev, 4 * s + 7)
                        e.wait_ge(dve_ev, 4 * s + 6)
                        for kt in range(NT):
                            last = nc.tensor.transpose(pj[:, 0, kt * P:(kt + 1) * P],
                                                       vt[:, kt * P:(kt + 1) * P], ident[:, :])
                        last.then_inc(pe_pj, 1)
                    if t == 12:
                        e.wait_ge(pool_k, STACKS * s + 2 * STACKS)
                        e.wait_ge(pool_q, STACKS * s + 2 * STACKS)
                        e.wait_ge(k4_in[par], STEP_IN * (2 * b + g // 2 + 1) + STEP_IN)
                        e.wait_ge(q4_in[par], STEP_IN * (2 * b + g // 2 + 1) + STEP_IN)
                        if g < 2:
                            e.wait_ge(mk_in[par], 64 * b + 64)
                    for v in CROSS_MAX_AT.get(t, ()):
                        max_scores(16 * s + 8 + v, par, v // NT, v % NT, v % 2)
                    if t == 16:
                        max_row(0, 16 * s + 12 + 2, 4 * s + 3)
                if proj:
                    max_row(1, 16 * s + 16 + 2, 4 * s + 4)

            e.sem_inc(pe_pj, 4)
            e.sem_inc(pe_av, 8)
            e.wait_ge(zeroed, ZEROED)
            e.wait_ge(dve_w, 10)
            each_step(e, step)


SPLIT = (0, 2, 4, 6, 8, 10, 12, 14)
CROSS_MAX_AT = {12: (0,), 13: (1, 2), 14: (3,), 15: (4, 5), 16: (6,), 17: (7,)}


class Scale:

    def __init__(self, sp, name, columns):
        self.partial = sp.sb(f"{name}_max", [P, columns])
        self.name = name
        self.columns = columns
        self.row = sp.sb(f"{name}_row", [P, 1])
        self.all = sp.sb(f"{name}_all", [P, 1])
        self.scale = sp.sb(f"{name}_scale", [P, 1])
        self.inverse = sp.sb(f"{name}_inv", [P, 1])


def scale_stage(nc, sc):
    with ExitStack() as ctx:
        sp = Space(nc, ctx, f"{sc.name}_sc")
        dve = sp.sem("dve")
        pool = sp.sem("pool")
        block = ctx.enter_context(nc.Block())

        @block.vector
        def _(e):
            nc.vector.tensor_reduce(sc.row[:, :], sc.partial[:, :], AX_X, ALU.max).then_inc(dve, 1)
            e.wait_ge(pool, 1)
            nc.vector.tensor_scalar(sc.scale[:, :], sc.all[:, :], 1.0 / QMAX, 1e-12, ALU.mult, ALU.max).then_inc(dve, 1)
            e.wait_ge(dve, 2)
            nc.vector.reciprocal(sc.inverse[:, :], sc.scale[:, :]).then_inc(dve, 1)

        @block.gpsimd
        def _(e):
            e.wait_ge(dve, 1)
            nc.gpsimd.partition_all_reduce(sc.all[:, :], sc.row[:, :], P, RMAX).then_inc(pool, 1)


def quantise_input_stage(nc, env):
    xh, xl, sc = env["xq_hi"], env["xq_lo"], env["x_scale"]
    with ExitStack() as ctx:
        sp = Space(nc, ctx, "qx")
        raw = sp.sb("raw", [P, 2, DK, S])
        qi = sp.sb("qi", [P, 2, DK, S], I16)
        raw_in = [sp.sem(f"raw_in{i}") for i in range(2)]
        dve_q = sp.sem("dve_q")
        act_hi = sp.sem("act_hi")
        dve_lo = sp.sem("dve_lo")
        block = ctx.enter_context(nc.Block())

        @block.sync
        def _(e):
            with e.Fori(0, B // 2) as g2:
                for u in range(2):
                    g = 2 * g2 + u
                    e.wait_ge(dve_q, g + 1)
                    e.dma_start(raw[:, u], env["xn3"][:, :, bass.ds(g * S, S)]).then_inc(raw_in[u], 16)

        @block.vector
        def _(e):
            e.sem_inc(dve_q, 2)
            with e.Fori(0, B // 2) as g2:
                for u in range(2):
                    g = 2 * g2 + u
                    at = bass.ds(g * S, S)
                    e.wait_ge(raw_in[u], 16 * g2 + 16)
                    e.wait_ge(act_hi, g + 1)
                    nc.vector.tensor_scalar(qi[:, u], raw[:, u], sc.inverse[:, 0:1], None, ALU.mult).then_inc(dve_q, 1)
                    e.wait_ge(act_hi, g + 3)
                    nc.vector.tensor_tensor(xl[:, :, at], qi[:, u], f32(xh[:, :, at]), ALU.subtract).then_inc(dve_lo, 1)

        @block.scalar
        def _(e):
            e.sem_inc(act_hi, 2)
            with e.Fori(0, B // 2) as g2:
                for u in range(2):
                    g = 2 * g2 + u
                    e.wait_ge(dve_q, g + 3)
                    nc.scalar.activation(xh[:, :, bass.ds(g * S, S)], qi[:, u], ACT.Copy).then_inc(act_hi, 1)


class Dequant:
    STEPS = 6

    def __init__(self, nc, sp, width, done):
        self.nc, self.done, self.blocks = nc, done, width // BLK
        self.s = sp.sb("blk_s", [P, 2, self.blocks])
        self.inv = sp.sb("blk_inv", [P, self.blocks])
        self.q = sp.sb("wq", [P, width], I16)
        self.clip = sp.sb("wclip", [P, width])

    def tile(self, e, w, out, par, base):
        nc, done = self.nc, self.done
        cut = lambda ap: ap.rearrange("p (b k) -> p b k", k=BLK)
        wide = lambda ap: ap.unsqueeze(2).to_broadcast([P, self.blocks, BLK])
        s = self.s[:, par]
        nc.vector.tensor_reduce(s, cut(w), AX_X, ALU.max, apply_absolute_value=True).then_inc(done, 1)
        e.wait_ge(done, base + 1)
        nc.vector.tensor_scalar(s, s, 1.0 / WQMAX, 1e-12, ALU.mult, ALU.max).then_inc(done, 1)
        e.wait_ge(done, base + 2)
        nc.vector.reciprocal(self.inv[:, :], s).then_inc(done, 1)
        e.wait_ge(done, base + 3)
        nc.vector.tensor_tensor(cut(self.q[:, :]), cut(w), wide(self.inv[:, :]), ALU.mult).then_inc(done, 1)
        e.wait_ge(done, base + 4)
        nc.vector.tensor_scalar(self.clip[:, :], self.q[:, :], -WQMAX - 1.0, WQMAX, ALU.max, ALU.min).then_inc(done, 1)
        e.wait_ge(done, base + 5)
        nc.vector.tensor_tensor(cut(out), cut(self.clip[:, :]), wide(s), ALU.mult).then_inc(done, 1)


def gate_up_stage(nc, env, name):
    xh, xl, ident = env["xq_hi"], env["xq_lo"], env["ident"]
    xsc, out_sc = env["x_scale"], env[f"{name}_scale"]
    dst = env[name]
    w = env[f"w_{name}"].rearrange("(j p) h -> j p h", p=P)
    side = name == "up"
    gsc, ssc = env["gate_scale"], env["silu_scale"]
    HALF = HB * S
    W2 = 2 * S
    PIECES = T // W2
    BANKS = 4
    with ExitStack() as ctx:
        sp = Space(nc, ctx, name)
        w_raw = sp.sb("w_raw", [P, 2, D])
        wd = sp.sb("wd", [P, 2, D])
        w_hi = sp.sb("w_hi", [P, 2, DK, P], F32R)
        w_lo = sp.sb("w_lo", [P, 2, DK, P], F32R)
        ev = sp.sb("ev", [P, 2, HALF])
        acc = sp.ps("acc", [P, BANKS, S])
        pt = sp.ps("pt", [P, 2, DK, P])
        w_in = [sp.sem(f"w_in{i}") for i in range(2)]
        passed = sp.sem("passed")
        dve_q = sp.sem("dve_q")
        pe_tr = sp.sem("pe_tr")
        act_wh = sp.sem("act_wh")
        dve_wl = sp.sem("dve_wl")
        pe_acc = sp.sem("pe_acc")
        act_ev = sp.sem("act_ev")
        dve_mx = sp.sem("dve_mx")
        out = [sp.sem(f"out{i}") for i in range(2)]
        deq = Dequant(nc, sp, D, dve_q)
        if side:
            g_buf = sp.sb("g", [P, PIECES, W2])
            gq = sp.sb("gq", [P, 2, W2], I16)
            sg = sp.sb("sg", [P, W2])
            sq = sp.sb("sq", [P, W2], U16)
            c1 = sp.sb("c1", [P, 1])
            g_in = [sp.sem(f"g_in{i}") for i in range(PIECES)]
            c_done = sp.sem("c_done")
            dve_gq = sp.sem("dve_gq")
            act_sg = sp.sem("act_sg")
            dve_sq = sp.sem("dve_sq")
            dve_gs = sp.sem("dve_gs")
            dve_sm = sp.sem("dve_sm")
            g_out = [sp.sem(f"g_out{i}") for i in range(PIECES)]
        block = ctx.enter_context(nc.Block())

        def gate_at(j, n):
            return env["gate"][j, :, n * W2:(n + 1) * W2]

        @block.sync
        def _(e):
            def load_weights(j, u):
                e.dma_start(w_raw[:, u], w[j % FT]).then_inc(w_in[u], 16)

            load_weights(0, 0)
            load_weights(1, 1)
            if side:
                for n in range(2):
                    e.dma_start(g_buf[:, n], gate_at(0, n)).then_inc(g_in[n], 16)
            with e.Fori(0, FT // 2) as j2:
                for u in range(2):
                    j = 2 * j2 + u
                    nj = (j + 2) % FT
                    e.wait_ge(dve_q, deq.STEPS * j + deq.STEPS)
                    e.dma_start(w_raw[:, u], w[nj]).then_inc(w_in[u], 16)
                    for n in range(PIECES):
                        if side:
                            ahead, jn = (n + 2) % PIECES, j + (n + 2) // PIECES
                            load_j = jn % FT
                            e.wait_ge(g_out[ahead], 16 * jn + 16)
                            e.dma_start(g_buf[:, ahead], gate_at(load_j, ahead)).then_inc(g_in[ahead], 16)
                            e.wait_ge(dve_sm, PIECES * j + n + 1)
                            e.sem_inc(passed, 1)
                            e.dma_start(gate_at(j, n), g_buf[:, n]).then_inc(g_out[n], 16)
                        if n % 2:
                            h = n // 2
                            e.wait_ge(act_ev, B * j + HB * (h + 1) + BANKS)
                            e.dma_start(dst[j, :, h * HALF:(h + 1) * HALF], ev[:, h]).then_inc(out[h], 16)
            for h in range(2):
                e.wait_ge(out[h], 16 * FT + 16)
                e.wait_ge(w_in[h], 16 * (FT // 2) + 16)
            if side:
                for n in range(PIECES):
                    e.wait_ge(g_out[n], 16 * FT + 16)
                    e.wait_ge(g_in[n], 16 * FT + (16 if n < 2 else 0))

        @block.tensor
        def _(e):
            def transposes(n, u):
                e.wait_ge(dve_q, deq.STEPS * n + deq.STEPS)
                for k in range(DK):
                    last = nc.tensor.transpose(pt[:, u, k], wd[:, u, k * P:(k + 1) * P], ident[:, :])
                last.then_inc(pe_tr, 1)

            transposes(0, 0)
            with e.Fori(0, FT // 2) as j2:
                for u in range(2):
                    j = 2 * j2 + u
                    e.wait_ge(dve_wl, j + 1)
                    e.wait_ge(act_wh, j + 1)
                    for b in range(B):
                        if b == 5:
                            transposes(j + 1, 1 - u)
                        bank = b % BANKS
                        e.wait_ge(act_ev, B * j + b + 1)
                        for n, (ww, xx) in enumerate(((w_hi, xh), (w_lo, xh), (w_hi, xl))):
                            for k in range(DK):
                                last = nc.tensor.matmul(acc[:, bank], ww[:, u, k], xx[:, k, b * S:(b + 1) * S],
                                                        start=(n == 0 and k == 0), stop=(n == 2 and k == DK - 1))
                        last.then_inc(pe_acc, 1)

        @block.scalar
        def _(e):
            def high(n, u):
                e.wait_ge(pe_tr, n + 1)
                nc.scalar.activation(w_hi[:, u], pt[:, u], ACT.Copy).then_inc(act_wh, 1)

            e.sem_inc(act_ev, BANKS)
            for h in range(2):
                e.sem_inc(out[h], 16)
            if side:
                for n in range(PIECES):
                    e.sem_inc(g_out[n], 16)
            high(0, 0)
            with e.Fori(0, FT // 2) as j2:
                for u in range(2):
                    j = 2 * j2 + u
                    for b in range(B):
                        h, c = b // HB, b % HB
                        bank = b % BANKS
                        if c == 0:
                            e.wait_ge(out[h], 16 * j + 16)
                            e.wait_ge(dve_mx, 2 * j + h + 1)
                        e.wait_ge(pe_acc, B * j + b + 1)
                        nc.scalar.activation(ev[:, h, c * S:(c + 1) * S], acc[:, bank], ACT.Copy,
                                             scale=xsc.scale[:, 0:1]).then_inc(act_ev, 1)
                        if b == 5:
                            high(j + 1, 1 - u)
                        if side and b % 2:
                            n = b // 2
                            e.wait_ge(dve_gq, PIECES * j + n + 1)
                            e.wait_ge(dve_sq, PIECES * j + n + 1)
                            nc.scalar.activation(sg[:, :], gq[:, n % 2], ACT.Sigmoid,
                                                 scale=gsc.scale[:, 0:1]).then_inc(act_sg, 1)

        @block.vector
        def _(e):
            def low(n, u):
                e.wait_ge(act_wh, n + 1)
                nc.vector.tensor_tensor(w_lo[:, u], pt[:, u], f32(w_hi[:, u]), ALU.subtract).then_inc(dve_wl, 1)

            def quantise_gate(j, n):
                e.wait_ge(g_in[n], 16 * j + 16)
                nc.vector.tensor_scalar(gq[:, n % 2], g_buf[:, n], gsc.inverse[:, 0:1], None,
                                        ALU.mult).then_inc(dve_gq, 1)

            def silu(j, n):
                m = PIECES * j + n
                e.wait_ge(act_sg, m + 1)
                nc.vector.tensor_scalar(sq[:, :], sg[:, :], 65536.0, None, ALU.mult).then_inc(dve_sq, 1)
                e.wait_ge(dve_sq, m + 2)
                nc.vector.scalar_tensor_tensor(g_buf[:, n], sq[:, :], c1[:, 0:1], gq[:, n % 2],
                                               ALU.mult, ALU.mult).then_inc(dve_gs, 1)
                e.wait_ge(dve_gs, m + 1)
                nc.vector.tensor_reduce(ssc.partial[:, bass.ds(m, 1)], g_buf[:, n], AX_X, ALU.max,
                                        apply_absolute_value=True).then_inc(dve_sm, 1)

            def maxima(j, h):
                e.wait_ge(act_ev, B * j + HB * (h + 1) + BANKS)
                nc.vector.tensor_reduce(out_sc.partial[:, bass.ds(2 * j + h, 1)], ev[:, h], AX_X, ALU.max,
                                        apply_absolute_value=True).then_inc(dve_mx, 1)

            e.sem_inc(dve_mx, 2)
            if side:
                e.sem_inc(dve_sq, 1)
                nc.vector.tensor_scalar(c1[:, :], gsc.scale[:, :], 1.0 / 65536.0, None, ALU.mult).then_inc(c_done, 1)
                e.wait_ge(c_done, 1)
            e.wait_ge(w_in[0], 16)
            deq.tile(e, w_raw[:, 0], wd[:, 0], 0, 0)
            low(0, 0)
            with e.Fori(0, FT // 2) as j2:
                for u in range(2):
                    j = 2 * j2 + u
                    e.wait_ge(w_in[1 - u], 16 * j2 + 16 + 16 * u)
                    e.wait_ge(pe_tr, j + 1)
                    deq.tile(e, w_raw[:, 1 - u], wd[:, 1 - u], 1 - u, deq.STEPS * (j + 1))
                    if side:
                        quantise_gate(j, 0)
                        quantise_gate(j, 1)
                        silu(j, 0)
                        quantise_gate(j, 2)
                        silu(j, 1)
                    maxima(j, 0)
                    low(j + 1, 1 - u)
                    if side:
                        quantise_gate(j, 3)
                        silu(j, 2)
                        silu(j, 3)
                    maxima(j, 1)


def multiply_stage(nc, env):
    ssc, usc, osc = env["silu_scale"], env["up_scale"], env["prod_scale"]
    W = 2 * S
    PIECES = T // W
    ident, w_hi, w_lo = env["ident"], env["wd_hi"], env["wd_lo"]
    HT = D // P
    QUADS = FT // 4
    w = env["w_down"].rearrange("(j p) i -> j p i", p=P)
    with ExitStack() as ctx:
        sp = Space(nc, ctx, "mul")
        a = sp.sb("a", [P, PIECES, W])
        b = sp.sb("b", [P, PIECES, W])
        aq = sp.sb("aq", [P, PIECES, W], I16)
        bq = sp.sb("bq", [P, PIECES, W], I16)
        c2 = sp.sb("c2", [P, 1])
        ab_in = [sp.sem(f"ab_in{i}") for i in range(PIECES)]
        c_done = sp.sem("c_done")
        act_q = sp.sem("act_q")
        dve_o = sp.sem("dve_o")
        dve_mx = sp.sem("dve_mx")
        w_raw = sp.sb("w_raw", [P, FF])
        wd = sp.sb("wd", [P, 2, FF])
        acc = sp.ps("acc", [P, 2, DK * P])
        w_in = sp.sem("w_in")
        dve_q = sp.sem("dve_q")
        pe_tr = sp.sem("pe_tr")
        act_wh = sp.sem("act_wh")
        dve_wl = sp.sem("dve_wl")
        deq = Dequant(nc, sp, FF, dve_q)
        block = ctx.enter_context(nc.Block())

        @block.sync
        def _(e):
            def load(j, n):
                at = slice(n * W, (n + 1) * W)
                e.dma_start(a[:, n], env["gate"][j, :, at]).then_inc(ab_in[n], 16)
                e.dma_start(b[:, n], env["up"][j, :, at]).then_inc(ab_in[n], 16)

            e.dma_start(w_raw[:, :], w[0]).then_inc(w_in, 16)
            load(0, 0)
            load(0, 1)
            for j in range(1, HT):
                e.wait_ge(dve_q, deq.STEPS * j)
                e.dma_start(w_raw[:, :], w[j]).then_inc(w_in, 16)
            with e.Fori(0, FT) as j:
                for n in range(PIECES):
                    ahead, jn = (n + 2) % PIECES, j + (n + 2) // PIECES
                    load_j = jn % FT
                    e.wait_ge(dve_mx, PIECES * j + n + 2 + 1)
                    load(load_j, ahead)
            for n in range(PIECES):
                e.wait_ge(ab_in[n], 32 * FT + (32 if n < 2 else 0))

        @block.scalar
        def _(e):
            for j in range(HT):
                for q in range(QUADS):
                    n = QUADS * j + q
                    e.wait_ge(pe_tr, n + 1)
                    nc.scalar.activation(w_hi[:, 4 * q:4 * q + 4, j * P:(j + 1) * P],
                                         acc[:, n % 2].rearrange("p (k o) -> p k o", o=P),
                                         ACT.Copy).then_inc(act_wh, 1)
            with e.Fori(0, FT) as j:
                for n in range(PIECES):
                    e.wait_ge(ab_in[n], 32 * j + 32)
                    e.wait_ge(dve_mx, PIECES * j + n + 1)
                    nc.scalar.activation(aq[:, n], a[:, n], ACT.Copy, scale=ssc.inverse[:, 0:1]).then_inc(act_q, 1)
                    nc.scalar.activation(bq[:, n], b[:, n], ACT.Copy, scale=usc.inverse[:, 0:1]).then_inc(act_q, 1)

        @block.vector
        def _(e):
            nc.vector.tensor_tensor(c2[:, :], ssc.scale[:, :], usc.scale[:, :], ALU.mult).then_inc(c_done, 1)
            e.wait_ge(c_done, 1)
            e.sem_inc(dve_mx, PIECES)
            for j in range(HT):
                e.wait_ge(w_in, 16 * j + 16)
                if j >= 2:
                    e.wait_ge(pe_tr, QUADS * (j - 1))
                deq.tile(e, w_raw[:, :], wd[:, j % 2], j % 2, deq.STEPS * j)
                for q in range(QUADS):
                    n = QUADS * j + q
                    e.wait_ge(act_wh, n + 1)
                    cols = (slice(None), slice(4 * q, 4 * q + 4), slice(j * P, (j + 1) * P))
                    nc.vector.tensor_tensor(w_lo[cols], acc[:, n % 2].rearrange("p (k o) -> p k o", o=P),
                                            f32(w_hi[cols]), ALU.subtract).then_inc(dve_wl, 1)
            with e.Fori(0, FT) as j:
                for n in range(PIECES):
                    m = PIECES * j + n
                    e.wait_ge(act_q, 2 * m + 2)
                    nc.vector.scalar_tensor_tensor(a[:, n], aq[:, n], c2[:, 0:1], bq[:, n],
                                                   ALU.mult, ALU.mult).then_inc(dve_o, 1)
                    e.wait_ge(dve_o, m + 1)
                    nc.vector.tensor_reduce(osc.partial[:, bass.ds(m, 1)], a[:, n], AX_X, ALU.max,
                                            apply_absolute_value=True).then_inc(dve_mx, 1)

        @block.tensor
        def _(e):
            for j in range(HT):
                e.wait_ge(dve_q, deq.STEPS * j + deq.STEPS)
                for q in range(QUADS):
                    n = QUADS * j + q
                    if n >= 2:
                        e.wait_ge(dve_wl, n - 1)
                    for k in range(4):
                        i = 4 * q + k
                        last = nc.tensor.transpose(acc[:, n % 2, k * P:(k + 1) * P],
                                                   wd[:, j % 2, i * P:(i + 1) * P], ident[:, :])
                    last.then_inc(pe_tr, 1)


def down_stage(nc, env):
    ssc, usc, osc = env["silu_scale"], env["up_scale"], env["prod_scale"]
    w_hi, w_lo = env["wd_hi"], env["wd_lo"]
    RING = 4
    x2 = env["x2"].rearrange("(g n p) d -> g p n d", n=NT, p=P)
    y = env["out"].rearrange("(g n p) d -> g p n d", n=NT, p=P)
    with ExitStack() as ctx:
        sp = Space(nc, ctx, "dn")
        a = sp.sb("a", [P, RING, S])
        b = sp.sb("b", [P, RING, S])
        aq = sp.sb("aq", [P, RING, S], I16)
        bq = sp.sb("bq", [P, RING, S], I16)
        c2 = sp.sb("c2", [P, 1])
        c3 = sp.sb("c3", [P, 1])
        oq = sp.sb("oq", [P, RING, S], I16)
        oh = sp.sb("oh", [P, RING, S], F32R)
        ol = sp.sb("ol", [P, RING, S], F32R)
        xb = sp.sb("xb", [P, 2, NT, D])
        acc = sp.ps("acc", [P, 2, NT, D])
        ab_in = [sp.sem(f"ab_in{i}") for i in range(RING)]
        c_done = sp.sem("c_done")
        act_q = sp.sem("act_q")
        dve_oq = sp.sem("dve_oq")
        act_oh = sp.sem("act_oh")
        dve_ol = sp.sem("dve_ol")
        pe_ck = sp.sem("pe_ck")
        x_in = [sp.sem(f"x_in{i}") for i in range(2)]
        dve_y = sp.sem("dve_y")
        y_out = [sp.sem(f"y_out{i}") for i in range(2)]
        block = ctx.enter_context(nc.Block())

        def each_batch(e, step):
            step(0, 0, 0, True, False)
            with e.Fori(0, B // 2 - 1) as g2:
                step(2 * g2 + 1, 1, g2, True, True)
                step(2 * g2 + 2, 0, g2 + 1, True, True)
            step(B - 1, 1, B // 2 - 1, True, True)
            step(B, 0, B // 2, False, True)

        @block.sync
        def _(e):
            with e.Fori(0, B // 2) as g2:
                for u in range(2):
                    g = 2 * g2 + u
                    for k in range(FT):
                        c = k % RING
                        at = bass.ds(g * S, S)
                        e.wait_ge(act_q, 2 * (FT * g + k) + 2)
                        e.dma_start(a[:, c], env["gate"][k, :, at]).then_inc(ab_in[c], 16)
                        e.dma_start(b[:, c], env["up"][k, :, at]).then_inc(ab_in[c], 16)
                        if k == 0:
                            e.wait_ge(y_out[u], 16 * g2 + 16)
                            e.dma_start(xb[:, u], x2[g]).then_inc(x_in[u], 16)

        @block.scalar
        def _(e):
            e.sem_inc(y_out[0], 16)
            e.sem_inc(y_out[1], 16)
            e.sem_inc(act_oh, RING)
            e.sem_inc(act_q, 2 * RING)
            def high(g, k):
                c = k % RING
                e.wait_ge(dve_oq, FT * g + k + 1 + RING)
                e.wait_ge(pe_ck, FT * g + k + 1)
                nc.scalar.activation(oh[:, c], oq[:, c], ACT.Copy).then_inc(act_oh, 1)

            def store(g, par):
                e.wait_ge(dve_y, g + 3)
                e.dma_start(y[g], xb[:, par]).then_inc(y_out[par], 16)

            def step(g, par, gh, products, previous):
                for k in range(FT if products else 0):
                    c = k % RING
                    e.wait_ge(ab_in[c], 32 * (FT // RING) * g + 32 * (k // RING) + 32)
                    e.wait_ge(dve_oq, FT * g + k + 1)
                    nc.scalar.activation(aq[:, c], a[:, c], ACT.Copy, scale=ssc.inverse[:, 0:1]).then_inc(act_q, 1)
                    nc.scalar.activation(bq[:, c], b[:, c], ACT.Copy, scale=usc.inverse[:, 0:1]).then_inc(act_q, 1)
                    if k:
                        high(g, k - 1)
                    if previous and k == 6:
                        store(g - 1, 1 - par)
                if products:
                    high(g, FT - 1)
                else:
                    store(g - 1, 1 - par)

            each_batch(e, step)
            for u in range(2):
                e.wait_ge(y_out[u], 16 * (B // 2) + 16)

        @block.vector
        def _(e):
            nc.vector.tensor_tensor(c2[:, :], ssc.scale[:, :], usc.scale[:, :], ALU.mult).then_inc(c_done, 1)
            e.wait_ge(c_done, 1)
            nc.vector.tensor_tensor(c3[:, :], c2[:, :], osc.inverse[:, :], ALU.mult).then_inc(c_done, 1)
            e.wait_ge(c_done, 2)
            e.sem_inc(dve_oq, RING)
            e.sem_inc(dve_y, 2)
            def quantise(g, k):
                c = k % RING
                e.wait_ge(act_q, 2 * (FT * g + k) + 2 + 2 * RING)
                e.wait_ge(act_oh, FT * g + k + 1)
                nc.vector.scalar_tensor_tensor(oq[:, c], aq[:, c], c3[:, 0:1], bq[:, c],
                                               ALU.mult, ALU.mult).then_inc(dve_oq, 1)

            def low(g, k):
                c = k % RING
                e.wait_ge(act_oh, FT * g + k + 1 + RING)
                nc.vector.tensor_tensor(ol[:, c], oq[:, c], f32(oh[:, c]), ALU.subtract).then_inc(dve_ol, 1)

            def output(g, par, gh):
                e.wait_ge(pe_ck, FT * g + FT + RING)
                e.wait_ge(x_in[par], 16 * gh + 16)
                nc.vector.scalar_tensor_tensor(xb[:, par], acc[:, par], osc.scale[:, 0:1], xb[:, par],
                                               ALU.mult, ALU.add).then_inc(dve_y, 1)

            def step(g, par, gh, products, previous):
                before = (g - 1, 1 - par, gh if par else gh - 1)
                for k in range(FT if products else 0):
                    quantise(g, k)
                    if k:
                        low(g, k - 1)
                    if previous and k == 3:
                        output(*before)
                if products:
                    low(g, FT - 1)
                else:
                    output(*before)

            each_batch(e, step)

        @block.tensor
        def _(e):
            e.sem_inc(pe_ck, RING)
            with e.Fori(0, B // 2) as g2:
                for u in range(2):
                    g = 2 * g2 + u
                    e.wait_ge(dve_y, g + 1)
                    for k in range(FT):
                        c = k % RING
                        e.wait_ge(dve_ol, FT * g + k + 1)
                        for t in range(NT):
                            cols = slice(t * P, (t + 1) * P)
                            start, stop = k == 0, k == FT - 1
                            nc.tensor.matmul(acc[:, u, t], oh[:, c, cols], w_hi[:, k], start=start, stop=False)
                            nc.tensor.matmul(acc[:, u, t], oh[:, c, cols], w_lo[:, k], start=False, stop=False)
                            last = nc.tensor.matmul(acc[:, u, t], ol[:, c, cols], w_hi[:, k], start=False, stop=stop)
                        last.then_inc(pe_ck, 1)


def setup_stage(nc, env, ctx):
    sp = Space(nc, ctx, "top")
    env["ident"] = ident = sp.sb("ident", [P, P])
    env["ident_r"] = ident_r = sp.sb("ident_r", [P, P], F32R)
    env["minus_half"] = mhalf = sp.sb("minus_half", [P, 8])
    for name, columns in (("x", T // P), ("gate", 2 * FT), ("up", 2 * FT), ("silu", 4 * FT), ("prod", 4 * FT)):
        env[f"{name}_scale"] = Scale(sp, name, columns)
    env["xn3_max"] = env["x_scale"].partial
    made = sp.sem("made")
    with nc.Block() as block:
        @block.gpsimd
        def _(e):
            nc.gpsimd.memset(ident[:, :], 0.0).then_inc(made, 1)
            nc.gpsimd.memset(mhalf[:, :], -0.5).then_inc(made, 1)
            e.wait_ge(made, 2)
            nc.gpsimd.affine_select(out=ident[:, :], in_=ident[:, :], compare_op=ALU.not_equal, fill=1.0,
                                    base=0, pattern=[[-1, P]], channel_multiplier=1).then_inc(made, 1)

        @block.vector
        def _(e):
            e.wait_ge(made, 3)
            nc.vector.tensor_copy(ident_r[:, :], ident[:, :]).then_inc(made, 1)


def feed_forward(nc, env):
    scale_stage(nc, env["x_scale"])
    with ExitStack() as ctx:
        for part in ("hi", "lo"):
            env[f"xq_{part}"] = ctx.enter_context(nc.sbuf_tensor(f"xq_{part}", [P, DK, T], F32R))
        quantise_input_stage(nc, env)
        gate_up_stage(nc, env, "gate")
        scale_stage(nc, env["gate_scale"])
        gate_up_stage(nc, env, "up")
    scale_stage(nc, env["silu_scale"])
    scale_stage(nc, env["up_scale"])
    with ExitStack() as ctx:
        for part in ("hi", "lo"):
            env[f"wd_{part}"] = ctx.enter_context(nc.sbuf_tensor(f"wd_{part}", [P, FT, D], F32R))
        multiply_stage(nc, env)
        scale_stage(nc, env["prod_scale"])
        down_stage(nc, env)


_INS = ["x", "ctx_768", "mask_BxS2_bf1", "L0_attn_Wq", "L0_attn_bq", "L0_attn_Wk", "L0_attn_bk", "L0_attn_Wv",
        "L0_attn_bv", "L0_attn_Wo", "L0_attn_bo", "L0_xattn_Wq", "L0_xattn_Wk", "L0_xattn_Wv", "L0_xattn_Wo",
        "L0_ffn_w_gate", "L0_ffn_w_up", "L0_ffn_w_down"]
_ENV = ["x", "ctx", "mask", "Wq", "bq", "Wk", "bk", "Wv", "bv", "Wo", "bo", "Wq2", "Wk2", "Wv2", "Wo2",
        "w_gate", "w_up", "w_down"]


def decoder_layer(nc, args, out):
    env = dict(zip(_ENV, args))
    env["x"] = env["x"].rearrange("b s d -> (b s) d")
    env["ctx"] = env["ctx"].rearrange("b s d -> (b s) d")
    env["out"] = out.rearrange("b s d -> (b s) d")
    for name, shape in (("o_raw", [HP + 1, P, T]), ("o_sum", [HP + 1, 2, T]), ("o_rcp", [HP, 2, T]),
                        ("x1", [T, D]), ("xn2_hi", [P, DK, T]), ("xn2_lo", [P, DK, T]),
                        ("ct_hi", [P, CK, T]), ("ct_lo", [P, CK, T]), ("mask_f", [B, S]), ("mask_n", [B, S]),
                        ("c_raw", [XG, NH // XG, 2 * XD + 1, T + S]), ("c_rcp", [XG, NH // XG, T]),
                        ("x2", [T, D]), ("xn3", [P, DK, T]), ("gate", [FT, P, T]), ("up", [FT, P, T])):
        env[name] = nc.dram_tensor(name, shape, F32, kind="Internal").ap()
    with ExitStack() as ctx:
        setup_stage(nc, env, ctx)
        context_stage(nc, env)
        for half in range(2):
            with ExitStack() as inner:
                for part in ("hi", "lo"):
                    env[f"xt_{part}"] = inner.enter_context(
                        nc.sbuf_tensor(f"xt_{part}{half}", [P, DK, HTOK], F32R))
                layernorm_stage(nc, env, half)
                self_attention_stage(nc, env, half)
        reciprocal_stage(nc, env, "o")
        output_stage(nc, env, "o")
        cross_attention_stage(nc, env)
        reciprocal_stage(nc, env, "c")
        output_stage(nc, env, "c")
        feed_forward(nc, env)


def kernel(**inputs):
    import numpy as _np
    import concourse.bacc as _bacc
    from concourse import mybir as _mybir
    from concourse.bass_utils import run_bass_kernel_spmd as _run

    nc = _bacc.Bacc("TRN2", target_bir_lowering=False, num_devices=1)
    arrays, args = {}, []
    for name in _INS:
        a = _np.ascontiguousarray(inputs[name])
        if a.dtype == _np.bool_:
            a = a.view(_np.uint8)
        arrays[f"in_{name}_dram"] = a
        args.append(nc.dram_tensor(f"in_{name}_dram", a.shape, _mybir.dt.from_np(a.dtype), kind="ExternalInput").ap())
    out = nc.dram_tensor("out_0_dram", (B, S, D), _mybir.dt.from_np(_np.dtype("float32")), kind="ExternalOutput").ap()
    decoder_layer(nc, args, out)
    r = _run(nc, [arrays], core_ids=[0])
    return r.results[0]["out_0_dram"]
```
